# Optimizing a Trainium2 kernel written in Bass

```python
import numpy as np
import jax
import jax.numpy as jnp

def _softmax(x, axis=-1):
    return jax.nn.softmax(x, axis=axis)

def _gelu(x):
    return jax.nn.gelu(x, approximate=True)

def _silu(x):
    return jax.nn.silu(x)

def _sigmoid(x):
    return jax.nn.sigmoid(x)

def _layernorm(x, axis=-1, eps=1e-05):
    m = jnp.mean(x, axis=axis, keepdims=True)
    v = jnp.var(x, axis=axis, keepdims=True)
    return (x - m) / jnp.sqrt(v + eps)

def _scatter_add(tgt, idx, src, axis=0):
    return tgt.at[idx].add(src)

def _segment_sum(src, seg, n):
    return jax.ops.segment_sum(src, seg, n)
kernel_name = 'mk_pixart_resid_d4_seqx_r8_c10e00'

def setup_inputs(seed: int=0):
    np.random.seed(seed)
    _w = jnp.asarray

    def _rec_inputs():
        import jax
        import jax.numpy as jnp
        _rk = jax.random.key(seed)
        x = 7.22e-05 + 1 * jax.random.normal(jax.random.fold_in(_rk, 1), (64, 64, 128), jnp.float32)
        _lenS = 64 - jax.random.randint(jax.random.fold_in(_rk, 7), (64,), 0, max(1, 64 // 4) + 1, jnp.int32)
        _lenS2 = 64 - jax.random.randint(jax.random.fold_in(_rk, 8), (64,), 0, max(1, 64 // 4) + 1, jnp.int32)
        _ctx_1024P = jax.random.normal(jax.random.fold_in(_rk, 11), (64, 16, 128), jnp.float32)
        _ctx_1024c = jax.random.dirichlet(jax.random.fold_in(_rk, 511), 0.3 * jnp.ones((16,), jnp.float32), (64, 64))
        _ctx_1024t = jnp.einsum('bsk,bkd->bsd', _ctx_1024c, _ctx_1024P)
        _ctx_1024t = _ctx_1024t * jax.lax.rsqrt(jnp.mean(jnp.square(_ctx_1024t)) + 1e-12) * 0.953939
        ctx_1024 = 4.13588e-05 + 0.999923 * (_ctx_1024t + 0.3 * jax.random.normal(jax.random.fold_in(_rk, 611), (64, 64, 128), jnp.float32))
        condB_tau = jax.random.uniform(jax.random.fold_in(_rk, 12), (64,), jnp.float32, 0.0, 1.45372)
        fside_BxS2_0 = 0.0088954 + 1.00633 * jax.random.normal(jax.random.fold_in(_rk, 13), (64, 64), jnp.float32)
        condB_pt = jax.random.uniform(jax.random.fold_in(_rk, 15), (64,), jnp.float32, 0.0, 226.919)
        return (x, ctx_1024, condB_tau, fside_BxS2_0, condB_pt, _lenS2)
    x, ctx_1024, condB_tau, fside_BxS2_0, condB_pt, _lenS2 = _rec_inputs()

    def _L0_xcond_setup():
        import jax, jax.numpy as jnp
        import numpy as np
        D_MODEL = 128
        N_HEADS = 16
        key = jax.random.key(seed)
        ks = jax.random.split(key, 16)
        B, L, S, D = (4, 256, 256, D_MODEL)
        inp = {'q': jax.random.normal(ks[0], (B, L, D), jnp.float32), 'k': jax.random.normal(ks[1], (B, S, D), jnp.float32), 'v': jax.random.normal(ks[2], (B, S, D), jnp.float32), 'tau': jax.random.uniform(ks[3], (B, 1), jnp.float32, 0.5, 1.5), 'delta': jax.random.normal(ks[4], (B, S), jnp.float32)}
        s = 1.0 / np.sqrt(D)
        inp['Wq'] = jax.random.normal(ks[5], (D, D), jnp.float32) * s
        inp['bq'] = jnp.zeros((D,), jnp.float32)
        inp['Wk'] = jax.random.normal(ks[6], (D, D), jnp.float32) * s
        inp['bk'] = jnp.zeros((D,), jnp.float32)
        inp['Wv'] = jax.random.normal(ks[7], (D, D), jnp.float32) * s
        inp['bv'] = jnp.zeros((D,), jnp.float32)
        inp['Wo'] = jax.random.normal(ks[8], (D, D), jnp.float32) * s
        inp['bo'] = jnp.zeros((D,), jnp.float32)
        return inp
    _L0_xcond_all = _L0_xcond_setup()
    _L0_xcond_in = {k: v for k, v in _L0_xcond_all.items() if k in ('Wq', 'bq', 'Wk', 'bk', 'Wv', 'bv', 'Wo', 'bo')}
    del _L0_xcond_all

    def _L0_ffn_setup():
        import jax, jax.numpy as jnp
        import numpy as np
        B, N, C, H, REG = (1, 2309, 128, 16, 5)
        D = C // H
        key = jax.random.key(seed)
        k0, k1, k2, k3 = jax.random.split(key, 4)
        x = jax.random.normal(k0, (B, N, C), dtype=jnp.float32)
        g_info = jax.random.normal(k1, (12, 2, C), dtype=jnp.float32)
        W_qkv = jax.random.normal(k2, (C, 3 * C), dtype=jnp.float32) * 0.02
        W_proj = jax.random.normal(k3, (C, C), dtype=jnp.float32) * 0.02
        b_proj = jnp.zeros((C,), dtype=jnp.float32)
        return {'x': x, 'g_info': g_info, 'W_qkv': W_qkv, 'W_proj': W_proj, 'b_proj': b_proj}
    _L0_ffn_all = _L0_ffn_setup()
    _L0_ffn_in = {k: v for k, v in _L0_ffn_all.items() if k in ('g_info', 'W_qkv', 'W_proj', 'b_proj')}
    del _L0_ffn_all

    def _L1_xcond_setup():
        import jax, jax.numpy as jnp
        import numpy as np
        B, S, D, H = (2, 256, 128, 16)
        DK = D // H

        def _split_heads(x):
            b, s, _ = x.shape
            return x.reshape(b, s, H, DK).transpose(0, 2, 1, 3)
        key = jax.random.key(seed)
        ks = jax.random.split(key, 14)
        inp = {'query': jax.random.normal(ks[0], (B, S, D), jnp.float32), 'key': jax.random.normal(ks[1], (B, S, D), jnp.float32), 'value': jax.random.normal(ks[2], (B, S, D), jnp.float32), 'tau': jax.random.uniform(ks[3], (B, 1), jnp.float32, 0.5, 1.5), 'delta': jax.random.normal(ks[4], (B, S), jnp.float32)}
        sc = 1.0 / np.sqrt(D)
        for i, name in enumerate(['q', 'k', 'v', 'o']):
            inp[f'W{name}'] = jax.random.normal(ks[5 + 2 * i], (D, D), jnp.float32) * sc
            inp[f'b{name}'] = jax.random.normal(ks[6 + 2 * i], (D,), jnp.float32) * 0.01
        return inp
    _L1_xcond_all = _L1_xcond_setup()
    _L1_xcond_in = {k: v for k, v in _L1_xcond_all.items() if k in ('Wq', 'bq', 'Wk', 'bk', 'Wv', 'bv', 'Wo', 'bo')}
    del _L1_xcond_all

    def _L1_ffn_setup():
        import jax, jax.numpy as jnp
        import numpy as np
        B, S, D = (4, 256, 128)
        E = 8
        CF = 1
        key = jax.random.key(seed)
        k_x, k_g, k_w, k_b = jax.random.split(key, 4)
        x = jax.random.normal(k_x, (B, S, D), dtype=jnp.float32)
        Wg = jax.random.normal(k_g, (D, E), dtype=jnp.float32) * (1.0 / np.sqrt(D))
        We = jax.random.normal(k_w, (D, D), dtype=jnp.float32) * (1.0 / np.sqrt(D))
        be = jax.random.normal(k_b, (D,), dtype=jnp.float32) * 0.01
        return {'x': x, 'Wg': Wg, 'We': We, 'be': be}
    _L1_ffn_all = _L1_ffn_setup()
    _L1_ffn_in = {k: v for k, v in _L1_ffn_all.items() if k in ('Wg', 'We', 'be')}
    del _L1_ffn_all

    def _L2_xcond_setup():
        import jax, jax.numpy as jnp
        import numpy as np
        N, L, H, Q = (64, 258, 128, 32)
        WINDOW = 16.0
        DEV_POW = 128.0
        key = jax.random.key(seed)
        k1, k2, k3, k4, k5, k6 = jax.random.split(key, 6)
        encoder_outputs = jax.random.normal(k1, (N, L, H), dtype=jnp.float32)
        decoder_h_t = jax.random.normal(k2, (N, Q, H), dtype=jnp.float32)
        src_len = jax.random.randint(k3, (N,), 32, L + 1).astype(jnp.int32)
        p_t = jax.random.uniform(k4, (N,), dtype=jnp.float32) * (src_len.astype(jnp.float32) - 1.0)
        W_a = jax.random.normal(k5, (H, H), dtype=jnp.float32) * (1.0 / np.sqrt(H))
        W_c = jax.random.normal(k6, (H, 2 * H), dtype=jnp.float32) * (1.0 / np.sqrt(2 * H))
        return {'encoder_outputs': encoder_outputs, 'decoder_h_t': decoder_h_t, 'src_len': src_len, 'p_t': p_t, 'W_a': W_a, 'W_c': W_c}
    _L2_xcond_all = _L2_xcond_setup()
    _L2_xcond_in = {k: v for k, v in _L2_xcond_all.items() if k in ('W_a', 'W_c')}
    del _L2_xcond_all

    def _L2_ffn_setup():
        import jax, jax.numpy as jnp
        import numpy as np
        H = 128
        I = 256
        E = 8
        B, S = (2, 128)

        def _swiglu(x, wg, wu, wd):
            return jax.nn.silu(x @ wg) * (x @ wu) @ wd
        key = jax.random.key(seed)
        ks = jax.random.split(key, 8)
        sc_h = 1.0 / np.sqrt(H)
        sc_i = 1.0 / np.sqrt(I)
        return {'hidden_states': jax.random.normal(ks[0], (B, S, H), jnp.float32), 'gate_w': jax.random.normal(ks[1], (H, E), jnp.float32) * sc_h, 'sh_gate': jax.random.normal(ks[2], (H, I), jnp.float32) * sc_h, 'sh_up': jax.random.normal(ks[3], (H, I), jnp.float32) * sc_h, 'sh_down': jax.random.normal(ks[4], (I, H), jnp.float32) * sc_i, 'rt_gate': jax.random.normal(ks[5], (E, H, I), jnp.float32) * sc_h, 'rt_up': jax.random.normal(ks[6], (E, H, I), jnp.float32) * sc_h, 'rt_down': jax.random.normal(ks[7], (E, I, H), jnp.float32) * sc_i}
    _L2_ffn_all = _L2_ffn_setup()
    _L2_ffn_in = {k: v for k, v in _L2_ffn_all.items() if k in ('gate_w', 'sh_gate', 'sh_up', 'sh_down', 'rt_gate', 'rt_up', 'rt_down')}
    del _L2_ffn_all

    def _L3_xcond_setup():
        import jax, jax.numpy as jnp
        import numpy as np
        B, S, D, H = (2, 256, 128, 16)
        DK = D // H

        def _split_heads(x):
            b, s, _ = x.shape
            return x.reshape(b, s, H, DK).transpose(0, 2, 1, 3)
        key = jax.random.key(seed)
        ks = jax.random.split(key, 14)
        inp = {'query': jax.random.normal(ks[0], (B, S, D), jnp.float32), 'key': jax.random.normal(ks[1], (B, S, D), jnp.float32), 'value': jax.random.normal(ks[2], (B, S, D), jnp.float32), 'tau': jax.random.uniform(ks[3], (B, 1), jnp.float32, 0.5, 1.5), 'delta': jax.random.normal(ks[4], (B, S), jnp.float32)}
        sc = 1.0 / np.sqrt(D)
        for i, name in enumerate(['q', 'k', 'v', 'o']):
            inp[f'W{name}'] = jax.random.normal(ks[5 + 2 * i], (D, D), jnp.float32) * sc
            inp[f'b{name}'] = jax.random.normal(ks[6 + 2 * i], (D,), jnp.float32) * 0.01
        return inp
    _L3_xcond_all = _L3_xcond_setup()
    _L3_xcond_in = {k: v for k, v in _L3_xcond_all.items() if k in ('Wq', 'bq', 'Wk', 'bk', 'Wv', 'bv', 'Wo', 'bo')}
    del _L3_xcond_all

    def _L3_ffn_setup():
        import jax, jax.numpy as jnp
        import numpy as np
        D_MODEL, D_FF, N_EXP = (128, 512, 8)
        key = jax.random.key(seed)
        ks = jax.random.split(key, 8)
        s = lambda fan_in: 1.0 / np.sqrt(fan_in)
        x = jax.random.normal(ks[0], (4, 256, D_MODEL), dtype=jnp.float32)
        Wr = jax.random.uniform(ks[1], (N_EXP, D_MODEL), jnp.float32, -s(D_MODEL), s(D_MODEL))
        br = jax.random.uniform(ks[2], (N_EXP,), jnp.float32, -s(D_MODEL), s(D_MODEL))
        W1 = jax.random.uniform(ks[3], (N_EXP, D_FF, D_MODEL), jnp.float32, -s(D_MODEL), s(D_MODEL))
        b1 = jax.random.uniform(ks[4], (N_EXP, D_FF), jnp.float32, -s(D_MODEL), s(D_MODEL))
        W2 = jax.random.uniform(ks[5], (N_EXP, D_MODEL, D_FF), jnp.float32, -s(D_FF), s(D_FF))
        b2 = jax.random.uniform(ks[6], (N_EXP, D_MODEL), jnp.float32, -s(D_FF), s(D_FF))
        return {'x': x, 'Wr': Wr, 'br': br, 'W1': W1, 'b1': b1, 'W2': W2, 'b2': b2}
    _L3_ffn_all = _L3_ffn_setup()
    _L3_ffn_in = {k: v for k, v in _L3_ffn_all.items() if k in ('Wr', 'br', 'W1', 'b1', 'W2', 'b2')}
    del _L3_ffn_all
    return {'x': x, 'ctx_1024': ctx_1024, 'condB_tau': condB_tau, 'fside_BxS2_0': fside_BxS2_0, 'condB_pt': condB_pt, '_lenS2': _lenS2, 'L0_xcond_Wq': _L0_xcond_in['Wq'], 'L0_xcond_bq': _L0_xcond_in['bq'], 'L0_xcond_Wk': _L0_xcond_in['Wk'], 'L0_xcond_bk': _L0_xcond_in['bk'], 'L0_xcond_Wv': _L0_xcond_in['Wv'], 'L0_xcond_bv': _L0_xcond_in['bv'], 'L0_xcond_Wo': _L0_xcond_in['Wo'], 'L0_xcond_bo': _L0_xcond_in['bo'], 'L0_ffn_g_info': _L0_ffn_in['g_info'], 'L0_ffn_W_qkv': _L0_ffn_in['W_qkv'], 'L0_ffn_W_proj': _L0_ffn_in['W_proj'], 'L0_ffn_b_proj': _L0_ffn_in['b_proj'], 'L1_xcond_Wq': _L1_xcond_in['Wq'], 'L1_xcond_bq': _L1_xcond_in['bq'], 'L1_xcond_Wk': _L1_xcond_in['Wk'], 'L1_xcond_bk': _L1_xcond_in['bk'], 'L1_xcond_Wv': _L1_xcond_in['Wv'], 'L1_xcond_bv': _L1_xcond_in['bv'], 'L1_xcond_Wo': _L1_xcond_in['Wo'], 'L1_xcond_bo': _L1_xcond_in['bo'], 'L1_ffn_Wg': _L1_ffn_in['Wg'], 'L1_ffn_We': _L1_ffn_in['We'], 'L1_ffn_be': _L1_ffn_in['be'], 'L2_xcond_W_a': _L2_xcond_in['W_a'], 'L2_xcond_W_c': _L2_xcond_in['W_c'], 'L2_ffn_gate_w': _L2_ffn_in['gate_w'], 'L2_ffn_sh_gate': _L2_ffn_in['sh_gate'], 'L2_ffn_sh_up': _L2_ffn_in['sh_up'], 'L2_ffn_sh_down': _L2_ffn_in['sh_down'], 'L2_ffn_rt_gate': _L2_ffn_in['rt_gate'], 'L2_ffn_rt_up': _L2_ffn_in['rt_up'], 'L2_ffn_rt_down': _L2_ffn_in['rt_down'], 'L3_xcond_Wq': _L3_xcond_in['Wq'], 'L3_xcond_bq': _L3_xcond_in['bq'], 'L3_xcond_Wk': _L3_xcond_in['Wk'], 'L3_xcond_bk': _L3_xcond_in['bk'], 'L3_xcond_Wv': _L3_xcond_in['Wv'], 'L3_xcond_bv': _L3_xcond_in['bv'], 'L3_xcond_Wo': _L3_xcond_in['Wo'], 'L3_xcond_bo': _L3_xcond_in['bo'], 'L3_ffn_Wr': _L3_ffn_in['Wr'], 'L3_ffn_br': _L3_ffn_in['br'], 'L3_ffn_W1': _L3_ffn_in['W1'], 'L3_ffn_b1': _L3_ffn_in['b1'], 'L3_ffn_W2': _L3_ffn_in['W2'], 'L3_ffn_b2': _L3_ffn_in['b2']}

def reference(x, ctx_1024, condB_tau, fside_BxS2_0, condB_pt, _lenS2, L0_xcond_Wq, L0_xcond_bq, L0_xcond_Wk, L0_xcond_bk, L0_xcond_Wv, L0_xcond_bv, L0_xcond_Wo, L0_xcond_bo, L0_ffn_g_info, L0_ffn_W_qkv, L0_ffn_W_proj, L0_ffn_b_proj, L1_xcond_Wq, L1_xcond_bq, L1_xcond_Wk, L1_xcond_bk, L1_xcond_Wv, L1_xcond_bv, L1_xcond_Wo, L1_xcond_bo, L1_ffn_Wg, L1_ffn_We, L1_ffn_be, L2_xcond_W_a, L2_xcond_W_c, L2_ffn_gate_w, L2_ffn_sh_gate, L2_ffn_sh_up, L2_ffn_sh_down, L2_ffn_rt_gate, L2_ffn_rt_up, L2_ffn_rt_down, L3_xcond_Wq, L3_xcond_bq, L3_xcond_Wk, L3_xcond_bk, L3_xcond_Wv, L3_xcond_bv, L3_xcond_Wo, L3_xcond_bo, L3_ffn_Wr, L3_ffn_br, L3_ffn_W1, L3_ffn_b1, L3_ffn_W2, L3_ffn_b2):
    import jax
    import jax.numpy as jnp

    def _L0_xcond_ref(q, k, v, tau, delta, Wq, bq, Wk, bk, Wv, bv, Wo, bo):
        import jax, jax.numpy as jnp
        import numpy as np
        D_MODEL = 128
        N_HEADS = 16
        B, L, D = q.shape
        S = k.shape[1]
        H = N_HEADS
        E = D // H
        qh = (q @ Wq.T + bq).reshape(B, L, H, E)
        kh = (k @ Wk.T + bk).reshape(B, S, H, E)
        vh = (v @ Wv.T + bv).reshape(B, S, H, E)
        scale = 1.0 / np.sqrt(E).astype(np.float32)
        scores = jnp.einsum('blhe,bshe->bhls', qh, kh)
        scores = scores * tau[:, None, None, :] + delta[:, None, None, :]
        a = jax.nn.softmax(scale * scores, axis=-1)
        out = jnp.einsum('bhls,bshd->blhd', a, vh).reshape(B, L, D)
        return out @ Wo.T + bo

    def _L0_ffn_ref(x, g_info, W_qkv, W_proj, b_proj):
        import jax, jax.numpy as jnp
        import numpy as np
        B, N, C, H, REG = (1, 2309, 128, 16, 5)
        D = C // H
        Bx, Nx, Cx = x.shape
        scale = D ** (-0.5)
        qkv = (x @ W_qkv).reshape(Bx, Nx, 3, H, D)
        q, k, v = (qkv[:, :, 0], qkv[:, :, 1], qkv[:, :, 2])
        g_layer = g_info[0].reshape(-1, H, D)
        q_g = g_layer[0]
        q_pure = q[:, REG:]
        q_n = q_pure / jnp.linalg.norm(q_pure, axis=-1, keepdims=True)
        qg_n = q_g / jnp.linalg.norm(q_g, axis=-1, keepdims=True)
        sim = (qg_n[None, None] * q_n).sum(-1).mean(-1)
        sim = (sim - sim.min()) / (sim.max() - sim.min())
        pos = sim > 0.9
        logits = jnp.einsum('bqhd,bkhd->bhqk', q * scale, k)

        def masked_attn(tok_mask):
            key_mask = jnp.concatenate([jnp.ones((Bx, REG), bool), tok_mask], axis=1)
            l = jnp.where(key_mask[:, None, None, :], logits, -jnp.inf)
            a = jax.nn.softmax(l, axis=-1)
            return jnp.einsum('bhqk,bkhd->bqhd', a, v)
        x_pos = masked_attn(pos)
        x_neg = masked_attn(~pos)
        reg_out = (x_pos[:, :REG] + x_neg[:, :REG]) * 0.5
        tok_out = jnp.where(pos[:, :, None, None], x_pos[:, REG:], x_neg[:, REG:])
        out = jnp.concatenate([reg_out, tok_out], axis=1).reshape(Bx, Nx, Cx)
        return out @ W_proj + b_proj

    def _L1_xcond_ref(query, key, value, tau, delta, Wq, bq, Wk, bk, Wv, bv, Wo, bo):
        import jax, jax.numpy as jnp
        import numpy as np
        B, S, D, H = (2, 256, 128, 16)
        DK = D // H

        def _split_heads(x):
            b, s, _ = x.shape
            return x.reshape(b, s, H, DK).transpose(0, 2, 1, 3)
        q = _split_heads(query @ Wq.T + bq)
        k = _split_heads(key @ Wk.T + bk)
        v = _split_heads(value @ Wv.T + bv)
        scores = jnp.einsum('bhqd,bhkd->bhqk', q, k)
        scores = scores * tau[:, :, None, None] + delta[:, None, None, :]
        scores = scores / jnp.sqrt(jnp.asarray(DK, scores.dtype))
        p_attn = jax.nn.softmax(scores, axis=-1)
        x = jnp.einsum('bhqk,bhkd->bhqd', p_attn, v)
        x = x.transpose(0, 2, 1, 3).reshape(query.shape[0], -1, H * DK)
        return x @ Wo.T + bo

    def _L1_ffn_ref(x, Wg, We, be):
        import jax, jax.numpy as jnp
        import numpy as np
        B, S, D = (4, 256, 128)
        E = 8
        CF = 1
        b, s, d = x.shape
        n = b * s
        cap = n // E * CF
        h = x.reshape(n, d)
        router_logits = h @ Wg
        probs = jax.nn.softmax(router_logits, axis=1)
        best = jnp.argmax(probs, axis=1)
        mask = jax.nn.one_hot(best, E, dtype=probs.dtype)
        gate = jnp.sum(probs * mask, axis=1)
        locations = jnp.cumsum(mask, axis=0) - 1.0
        mask = mask * (locations < cap).astype(mask.dtype)
        loc_idx = jnp.sum(locations * mask, axis=1).astype(jnp.int32)
        new_gate = gate[:, None] * mask
        loc_oh = jax.nn.one_hot(loc_idx, cap, dtype=new_gate.dtype)
        combine = new_gate[:, :, None] * loc_oh[:, None, :]
        dispatch = (combine != 0).astype(h.dtype)
        dispatched = jnp.einsum('nec,nd->ecd', dispatch, h).reshape(E * cap, d)
        expert_out = dispatched @ We + be
        out = combine.reshape(n, E * cap) @ expert_out
        return out.reshape(b, s, d)

    def _L2_xcond_ref(encoder_outputs, decoder_h_t, src_len, p_t, W_a, W_c):
        import jax, jax.numpy as jnp
        import numpy as np
        N, L, H, Q = (64, 258, 128, 32)
        WINDOW = 16.0
        DEV_POW = 128.0
        n, l, h = encoder_outputs.shape
        idx = jnp.arange(l, dtype=jnp.float32)
        src_end = src_len.astype(jnp.float32)
        attn_start = jnp.maximum(p_t - WINDOW, 0.0)
        attn_end = jnp.minimum(p_t + WINDOW, src_end)
        mask = (idx[None, :] < attn_start[:, None]) | (idx[None, :] > attn_end[:, None])
        score = jnp.einsum('nqh,hk,nlk->nql', decoder_h_t, W_a, encoder_outputs)
        score = jnp.where(mask[:, None, :], -1000000000.0, score)
        align = jax.nn.softmax(score, axis=2)
        gauss = jnp.exp(-(idx[None, :] - p_t[:, None]) ** 2 / DEV_POW)
        align = align * gauss[:, None, :]
        context = jnp.einsum('nql,nlh->nqh', align, encoder_outputs)
        cat = jnp.concatenate([context, decoder_h_t], axis=2)
        return jnp.tanh(cat @ W_c.T)

    def _L2_ffn_ref(hidden_states, gate_w, sh_gate, sh_up, sh_down, rt_gate, rt_up, rt_down):
        import jax, jax.numpy as jnp
        import numpy as np
        H = 128
        I = 256
        E = 8
        B, S = (2, 128)

        def _swiglu(x, wg, wu, wd):
            return jax.nn.silu(x @ wg) * (x @ wu) @ wd
        b, s, h = hidden_states.shape
        x = hidden_states.reshape(-1, h)
        logits = x @ gate_w
        top_val = jnp.max(logits, axis=-1, keepdims=True)
        top_id = jnp.argmax(logits, axis=-1)
        score = jax.nn.sigmoid(top_val)
        xs = x * score
        g = jnp.einsum('th,ehi->eti', xs, rt_gate)
        u = jnp.einsum('th,ehi->eti', xs, rt_up)
        act = jax.nn.silu(g) * u
        y = jnp.einsum('eti,eih->eth', act, rt_down)
        onehot = jax.nn.one_hot(top_id, E, dtype=x.dtype)
        routed = jnp.einsum('eth,te->th', y, onehot)
        shared = _swiglu(x, sh_gate, sh_up, sh_down)
        return (shared + routed).reshape(b, s, h)

    def _L3_xcond_ref(query, key, value, tau, delta, Wq, bq, Wk, bk, Wv, bv, Wo, bo):
        import jax, jax.numpy as jnp
        import numpy as np
        B, S, D, H = (2, 256, 128, 16)
        DK = D // H

        def _split_heads(x):
            b, s, _ = x.shape
            return x.reshape(b, s, H, DK).transpose(0, 2, 1, 3)
        q = _split_heads(query @ Wq.T + bq)
        k = _split_heads(key @ Wk.T + bk)
        v = _split_heads(value @ Wv.T + bv)
        scores = jnp.einsum('bhqd,bhkd->bhqk', q, k)
        scores = scores * tau[:, :, None, None] + delta[:, None, None, :]
        scores = scores / jnp.sqrt(jnp.asarray(DK, scores.dtype))
        p_attn = jax.nn.softmax(scores, axis=-1)
        x = jnp.einsum('bhqk,bhkd->bhqd', p_attn, v)
        x = x.transpose(0, 2, 1, 3).reshape(query.shape[0], -1, H * DK)
        return x @ Wo.T + bo

    def _L3_ffn_ref(x, Wr, br, W1, b1, W2, b2):
        import jax, jax.numpy as jnp
        import numpy as np
        D_MODEL, D_FF, N_EXP = (128, 512, 8)
        B, S, D = x.shape
        xf = x.reshape(-1, D)
        logits = xf @ Wr.T + br
        expert_idx = jnp.argmax(logits, axis=-1)
        h = jax.nn.relu(jnp.einsum('td,efd->etf', xf, W1) + b1[:, None, :])
        y = jnp.einsum('etf,edf->etd', h, W2) + b2[:, None, :]
        out = y[expert_idx, jnp.arange(xf.shape[0])]
        return out.reshape(B, S, D)
    x = x + _L0_xcond_ref(_layernorm(x, axis=-1), ctx_1024, ctx_1024, condB_tau[:, None], fside_BxS2_0, L0_xcond_Wq, L0_xcond_bq, L0_xcond_Wk, L0_xcond_bk, L0_xcond_Wv, L0_xcond_bv, L0_xcond_Wo, L0_xcond_bo)
    x = x + _L0_ffn_ref(_layernorm(x, axis=-1), L0_ffn_g_info, L0_ffn_W_qkv, L0_ffn_W_proj, L0_ffn_b_proj)
    x = x + _L1_xcond_ref(_layernorm(x, axis=-1), ctx_1024, ctx_1024, condB_tau[:, None], fside_BxS2_0, L1_xcond_Wq, L1_xcond_bq, L1_xcond_Wk, L1_xcond_bk, L1_xcond_Wv, L1_xcond_bv, L1_xcond_Wo, L1_xcond_bo)
    x = x + _L1_ffn_ref(_layernorm(x, axis=-1), L1_ffn_Wg, L1_ffn_We, L1_ffn_be)
    x = x + _L2_xcond_ref(ctx_1024, _layernorm(x, axis=-1), _lenS2, condB_pt, L2_xcond_W_a, L2_xcond_W_c)
    x = x + _L2_ffn_ref(_layernorm(x, axis=-1), L2_ffn_gate_w, L2_ffn_sh_gate, L2_ffn_sh_up, L2_ffn_sh_down, L2_ffn_rt_gate, L2_ffn_rt_up, L2_ffn_rt_down)
    x = x + _L3_xcond_ref(_layernorm(x, axis=-1), ctx_1024, ctx_1024, condB_tau[:, None], fside_BxS2_0, L3_xcond_Wq, L3_xcond_bq, L3_xcond_Wk, L3_xcond_bk, L3_xcond_Wv, L3_xcond_bv, L3_xcond_Wo, L3_xcond_bo)
    x = x + _L3_ffn_ref(_layernorm(x, axis=-1), L3_ffn_Wr, L3_ffn_br, L3_ffn_W1, L3_ffn_b1, L3_ffn_W2, L3_ffn_b2)
    return x

_drawn_inputs = setup_inputs


def setup_inputs(seed=0):
    import zlib

    import numpy as np

    out = dict(_drawn_inputs(seed))
    spreads = {'L0_xcond_bq': (0.0, 0.1),
     'L0_xcond_bk': (0.0, 2.0),
     'L0_xcond_bv': (0.0, 0.1),
     'L0_xcond_bo': (0.0, 0.1),
     'L0_ffn_b_proj': (0.0, 0.1)}
    factors = {'L0_ffn_g_info': 56.497,
     'L1_xcond_bq': 5.975,
     'L1_xcond_bk': 64.0,
     'L1_ffn_be': 3.896,
     'L3_xcond_bq': 24.813,
     'L3_xcond_bk': 64.0,
     'L3_xcond_bv': 4.542,
     'L3_xcond_bo': 4.633,
     'L3_ffn_b1': 5.179,
     'L3_ffn_b2': 4.058}
    for name, (base, spread) in spreads.items():
        noise = np.random.default_rng([zlib.crc32(name.encode()), seed]).standard_normal(out[name].shape)
        drawn = base * np.exp(spread * noise) if base else spread * noise
        out[name] = jnp.asarray(drawn.astype(out[name].dtype))
    for name, factor in factors.items():
        out[name] = (out[name] * factor).astype(out[name].dtype)
    return out
```

```python
from contextlib import ExitStack

import numpy as np

import concourse.bass as bass
from concourse import mybir
from concourse.alu_op_type import AluOpType as ALU

ACT = mybir.ActivationFunctionType
AX = mybir.AxisListType
F32 = mybir.dt.float32
BF16 = mybir.dt.bfloat16
I32 = mybir.dt.int32
U32 = mybir.dt.uint32

B, S, D = 64, 64, 128
H, E = 16, 8
G = H // 2
TOK = B * S
TILES = TOK // 128
CHUNK = 512
CHUNKS = TOK // CHUNK
TPC = CHUNK // 128
BPC = CHUNK // S
REG = 5
EPS = 1e-5
VW = E * 2 + 1
NE = 8
CAP = TOK // NE
WINDOW, DEV_POW = 16.0, 128.0
BIG = float(2 ** 60)


SLOTS = -(-(TOK // 128 + 8 - 1) // 4) * 4
CST_COLS = 332 + 128 + G + 240 + 128 + 8 + 256 + 256 + 128 + 128 + 128 + SLOTS


def constants():
    p = np.arange(128)
    head, pair = p // E, p // (2 * E)
    fold = (p[:, None] % S == np.arange(S)[None, :]).astype(np.float32)
    is_reg = (np.arange(S) < REG)[None, :]
    cst = np.concatenate([
        np.eye(128), fold, fold * np.where(is_reg, 0.5, 1.0), fold * np.where(is_reg, 0.5, 0.0),
        head[:, None] % 2 == np.arange(2)[None, :], pair[:, None] % 2 == np.arange(2)[None, :],
        pair[:, None] == np.arange(G)[None, :],
        p[:, None] // S == pair[None, :] % 2, p[:, None] // S == np.arange(G)[None, :] % 2,
        np.zeros((128, 112)), head[:, None] == np.arange(H)[None, :], np.zeros((128, 112)),
        head[:, None] == p[None, :] % H, (p[:, None] // H == np.arange(CHUNKS)[None, :]) / H,
        np.repeat(NE - np.arange(NE), TILES)[None, :] + 0 * p[:, None],
        np.tile(np.arange(TILES) > 0, NE)[None, :] + 0 * p[:, None],
        p[:, None] <= p[None, :],
        np.where(p[:, None] // S == p[None, :] // S, p[None, :] % S, 10 ** 6),
        np.where(p[:, None] // S == p[None, :] // S, -1e9, -1e30),
        np.arange(SLOTS)[None, :] + 0 * p[:, None],
    ], axis=1).astype(np.float32)
    return cst


def wait_reuse(eng, semaphore, value):
    if not isinstance(value, int) or value > 0:
        eng.wait_ge(semaphore, value)


def pipeline(eng, count, period, lag, step):
    first = -(-max(lag + 1, period) // period)
    for k in range(first * period):
        step(k, k // period, k % period, lambda l, k=k: k - l >= 0)
    with eng.Fori(first, count // period) as turn:
        for u in range(period):
            step(turn * period + u, turn, u, lambda l: True)
    for k in range(count, count + lag):
        step(k, k // period, k % period, lambda l, k=k: k - l < count)


def build(nc, a, out):
    ctx = ExitStack()
    with ctx:
        def sb(name, shape, dt=F32):
            return ctx.enter_context(nc.sbuf_tensor(name, shape, dt))

        def pb(name):
            return ctx.enter_context(nc.psum_tensor(name, [128, 512], F32))

        def sem(name):
            return ctx.enter_context(nc.semaphore(name))

        X = sb("X", [128, TILES, D])
        ctxT = sb("ctxT", [128, TOK])
        QT = sb("QT", [128, TOK])
        KT = sb("KT", [128, TOK])
        VB = sb("VB", [128, B, G * VW])
        xd = [sb(f"xd{i}", [128, BPC, 2, S]) for i in range(2)]
        cst = sb("cst", [128, CST_COLS])
        ident = cst[:, 0:128]
        fold2 = cst[:, 128:192]
        foldp = [cst[:, 192:256], cst[:, 256:320]]
        hp_mask = cst[:, 320:322]
        g2_mask = cst[:, 322:324]
        g_mask = cst[:, 324:332]
        v_mask = cst[:, 332:460]
        v_ones = cst[:, 460:468]
        heads_pad = cst[:, 468:708]
        heads_rep = cst[:, 708:836]
        mean_h = cst[:, 836:844]
        first_w = cst[:, 844:1100]
        not_first = cst[:, 1100:1356]
        upto = cst[:, 1356:1484]
        own_idx = cst[:, 1484:1612]
        far = cst[:, 1612:1740]
        slot_no = cst[:, 1740:1740 + SLOTS]
        gcol = sb("gcol", [128, 2])
        guide_pad = sb("guide_pad", [128, 240])
        n2g = sb("n2g", [128, 1])
        ext = sb("ext", [CHUNKS, 6])
        clsb = sb("clsb", [CHUNKS, 4, CHUNK], BF16)
        onesr = sb("onesr", [3, 128], BF16)
        ones_row = sb("ones_row", [1, 128])
        stats = sb("stats", [128, TILES, 6])
        lnw = sb("lnw", [128, 6, TILES])
        rstd = sb("rstd", [128, TILES])
        nmr = sb("nmr", [128, TILES])
        xn = sb("xn", [128, TPC, D])
        xts = [sb(f"xts{i}", [128, CHUNK]) for i in range(2)]
        tau_b = sb("tau_b", [128, B])
        tau_s = sb("tau_s", [128, B])
        dl = sb("dl", [64, 3, 64])
        dlb = sb("dlb", [64, 3, 64], BF16)
        rows_sb = sb("rows_sb", [65, TOK], BF16)
        addR = rows_sb[0:3, :]
        clsrow = [rows_sb[32:33, :], rows_sb[64:65, :]]
        maskR = sb("maskR", [3, TOK], BF16)
        W = {}
        for n in ("0", "1", "2", "3"):
            W[n] = sb(f"W{n}", [128, 4, 128])
        bqkv = sb("bqkv", [128, 4, 4])
        bo = sb("bo", [128, 4, D])
        qbd = [sb(f"qbd{i}", [128, 128]) for i in range(2)]
        kbd = [sb(f"kbd{i}", [128, 512]) for i in range(2)]
        addL = [sb(f"addL{i}", [2, 128], BF16) for i in range(2)]
        mx = [sb(f"mx{i}", [128, G]) for i in range(2)]
        Pr = [sb(f"Pr{i}", [128, 512]) for i in range(2)]
        Pt = [sb(f"Pt{i}", [128, 512]) for i in range(2)]
        rden = sb("rden", [128, 2 * G])
        on = [sb(f"on{i}", [128, 2, H * E]) for i in range(2)]
        ots = [sb(f"ots{i}", [128, 128]) for i in range(2)]

        th = [sb(f"th{i}", [128, CHUNK]) for i in range(2)]
        n2 = [kbd[0], kbd[1], Pt[0], Pt[1], Pr[0]]
        sq = [Pr[1], th[1]]
        simr = th[0][0:CHUNKS, :]
        logit = sb("logit", [128, NE, TILES])
        oh = sb("oh", [128, NE, TILES])
        rt = sb("rt", [128, 4, NE, TILES])
        gate = sb("gate", [128, 4, TILES])
        ones128 = sb("ones128", [128, 128])
        w1f = sb("w1f", [128, NE + D])
        be = sb("be", [128, D])
        Yt = QT
        wa = sb("wa", [128, 3, 128])
        win = sb("win", [128, 8, TILES])
        leni = sb("leni", [128, TILES], I32)
        keep = VB[:, :, :].rearrange("p b c -> p (b c)")[:, 0:TOK]
        gauss = VB[:, :, :].rearrange("p b c -> p (b c)")[:, TOK:2 * TOK]
        sc2 = [sb(f"sc2{i}", [128, CHUNK]) for i in range(2)]
        nmx = [sb(f"nmx{i}", [128, TPC]) for i in range(2)]
        den = [sb(f"den{i}", [128, 2, TPC]) for i in range(2)]
        at2 = [kbd[i] for i in range(2)]
        cx = [Pr[i] for i in range(2)]
        cxT = [Pt[i] for i in range(2)]
        rw = sb("rw", [128, 2, NE])
        rb = sb("rb", [128, NE])
        dest = sb("dest", [128, TILES], U32)
        ei = sb("ei", [128, 2, NE], I32)
        ef = sb("ef", [128, 3, NE])
        slots = sb("slots", [128, SLOTS, NE])
        slotf = sb("slotf", [128, SLOTS])
        slot_e = sb("slot_e", [128, SLOTS + TILES], I32)
        wv = VB[:, :, :].rearrange("p b c -> p (b c)")
        xl = [th[0][:, 128 * i:128 * i + 128] for i in range(4)]
        ys = [th[1][:, 128 * i:128 * i + 128] for i in range(4)]
        xT = [Pr[i][:, 0:128] for i in range(2)]
        hb, hT, act2 = kbd, Pt, sc2
        b1r = maskR[0:3, :]
        b2r = sb("b2r", [3, NE * D], BF16)
        b2l = sb("b2l", [64, 3, 16])
        b2b = sb("b2b", [64, 3, 16], BF16)
        xs_dram = nc.dram_tensor("xs_dram", [(SLOTS + TILES) * 128, D], F32).ap()
        ys_dram = nc.dram_tensor("ys_dram", [(SLOTS + TILES) * 128, D], F32).ap()

        psS = [pb("psS0"), pb("psS1")]
        psP = [pb("psP0"), pb("psP1")]
        psO = [pb("psO0"), pb("psO1")]
        psT = pb("psT")
        psY = pb("psY")

        x_loaded = sem("x_loaded")
        ctx_loaded = sem("ctx_loaded")
        w_loaded = sem("w_loaded")
        side_loaded = sem("side_loaded")
        rows_moved = sem("rows_moved")
        consts_ready = sem("consts_ready")
        cst_loaded = sem("cst_loaded")
        CST_DMAS, CONSTS, W_DMAS = 1, 8, 12
        ROUTE_STEPS = 9
        setup_step = sem("setup_step")
        delta_split = sem("delta_split")
        stats_ready = sem("stats_ready")
        ln_step = sem("ln_step")
        rsqrt_ready = sem("rsqrt_ready")
        norm_ready = sem("norm_ready")
        xn_ready = sem("xn_ready")
        xt_in_psum = sem("xt_in_psum")
        xt_ready = sem("xt_ready")
        proj_ready = sem("proj_ready")
        q_ready = sem("q_ready")
        k_ready = sem("k_ready")
        v_ready = sem("v_ready")
        doubled = sem("doubled")
        class_staged = sem("class_staged")
        staged = sem("staged")
        bo_added = sem("bo_added")
        bias_through = sem("bias_through")
        bo_ready = sem("bo_ready")
        v_turned = sem("v_turned")
        scores_ready = sem("scores_ready")
        max_ready = sem("max_ready")
        shifted = sem("shifted")
        exp_ready = sem("exp_ready")
        p_turned = sem("p_turned")
        p_evac = sem("p_evac")
        v_evac = sem("v_evac")
        pv_ready = sem("pv_ready")
        rden_ready = sem("rden_ready")
        on_ready = sem("on_ready")
        ot_ready = sem("ot_ready")
        ot_evac = sem("ot_evac")
        y_ready = sem("y_ready")
        x_updated = sem("x_updated")
        slot_free = sem("slot_free")
        stored = sem("stored")
        w1f_loaded = sem("w1f_loaded")
        route_pe = sem("route_pe")
        logit_ready = sem("logit_ready")
        y_kept = sem("y_kept")
        route_step = sem("route_step")
        route_act = sem("route_act")
        rank_ready = sem("rank_ready")
        l2_loaded = sem("l2_loaded")
        win_step = sem("win_step")
        keep_ready = sem("keep_ready")
        ctx2_loaded = sem("ctx2_loaded")
        a_in_psum = sem("a_in_psum")
        a_ready = sem("a_ready")
        s2_ready = sem("s2_ready")
        capped = sem("capped")
        nmx_ready = sem("nmx_ready")
        e2_ready = sem("e2_ready")
        g2_ready = sem("g2_ready")
        rd2_ready = sem("rd2_ready")
        at_turned = sem("at_turned")
        at_ready = sem("at_ready")
        cx_in_psum = sem("cx_in_psum")
        cx_ready = sem("cx_ready")
        cx_turned = sem("cx_turned")
        cxT_ready = sem("cxT_ready")
        c_in_psum = sem("c_in_psum")
        th_ready = sem("th_ready")
        mw_loaded = sem("mw_loaded")
        zero_ready = sem("zero_ready")
        zeroed = sem("zeroed")
        xn_kept = sem("xn_kept")
        shared_rows = sem("shared_rows")
        place_step = sem("place_step")
        score_act = sem("score_act")
        scattered = sem("scattered")
        experts_loaded = sem("experts_loaded")
        tile_loaded = [sem(f"tile_loaded{i}") for i in range(4)]
        tile_stored = [sem(f"tile_stored{i}") for i in range(4)]
        e_turned = sem("e_turned")
        e_xT = sem("e_xT")
        e_hidden = sem("e_hidden")
        e_act = sem("e_act")
        e_h = sem("e_h")
        e_hturned = sem("e_hturned")
        e_hT = sem("e_hT")
        e_out = sem("e_out")
        e_y = sem("e_y")
        gathered = sem("gathered")
        shared_back = sem("shared_back")
        b_split = sem("b_split")
        b_rows = sem("b_rows")
        b_loaded = sem("b_loaded")
        ones_again = sem("ones_again")
        routed_added = sem("routed_added")
        PLACE_STEPS = [0, 16, 28]
        gauss_ready = sem("gauss_ready")
        g_loaded = sem("g_loaded")
        sim_step = sem("sim_step")
        sim_pe = sem("sim_pe")
        sim_act = sem("sim_act")
        sim_pool = sem("sim_pool")
        squared = sem("squared")
        sq_summed = sem("sq_summed")
        sim_newton = sem("sim_newton")
        cls_rows = sem("cls_rows")

        PASSES = [1, 2, 1, 1]
        LN_OF = [0, 1, 2, 6]
        UPD_OF = [0, 1, 2, 6]
        units_before = [B * sum(PASSES[:l]) for l in range(5)]

        def unit(turn, u, passes):
            return turn * 4 + u if passes == 1 else turn * 2 + (u // 4) * 2 + u % 2

        MOE = [(5, 256, SLOTS + TILES, 0), (7, 512, SLOTS, SLOTS + TILES)]

        def rows_of(dram, tile, n=1):
            return dram[bass.ds(tile * 128, 128 * n), :]

        def by_batch(row):
            return row.rearrange("c (b s) -> c b s", s=S)

        block = ctx.enter_context(nc.Block())

        @block.sync
        def _(sp):
            sp.dma_start(cst[:, :], a["cst"]).then_inc(cst_loaded, 16)
            xv = a["x"].rearrange("b s d -> (b s) d").rearrange("(t p) d -> p t d", p=128)
            for q in range(4):
                sp.dma_start(X[:, 8 * q:8 * q + 8, :], xv[:, 8 * q:8 * q + 8, :]).then_inc(x_loaded, 16)
            for q in range(4):
                sp.dma_start(ctxT[:, 1024 * q:1024 * q + 1024],
                             a["ctxT"][:, 1024 * q:1024 * q + 1024]).then_inc(ctx_loaded, 16)
            sp.dma_start(w1f[:, 0:NE], a["L1_ffn_Wg"]).then_inc(w1f_loaded, 16)
            sp.dma_start(w1f[:, NE:NE + D], a["L1_ffn_We"]).then_inc(w1f_loaded, 16)
            sp.dma_start(be[:, :], a["L1_ffn_be"].broadcast_to([128, D])).then_inc(w1f_loaded, 16)
            sp.dma_start(wa[:, :, :], a["L2_W"].rearrange("j d e -> d j e")).then_inc(l2_loaded, 16)
            for h in range(2):
                sp.dma_start(win[64 * h:64 * h + 64, 0, :], a["pt2"][h:h + 1, :].broadcast_to([64, TILES])).then_inc(l2_loaded, 16)
                sp.dma_start(leni[64 * h:64 * h + 64, :], a["len2"][h:h + 1, :].broadcast_to([64, TILES])).then_inc(l2_loaded, 16)
            sp.dma_start(rw[:, 0, :], a["L2_ffn_gate_w"]).then_inc(mw_loaded, 16)
            sp.dma_start(rw[:, 1, :], a["L3_ffn_WrT"]).then_inc(mw_loaded, 16)
            sp.dma_start(rb[:, :], a["L3_ffn_br"].broadcast_to([128, NE])).then_inc(mw_loaded, 16)
            sp.wait_ge(zero_ready, 1)
            sp.dma_start(xs_dram[0:SLOTS * 128, :].rearrange("(t p) d -> p t d", p=128),
                         th[0][:, 0:128].unsqueeze(1).broadcast_to([128, SLOTS, 128])).then_inc(zeroed, 16)
            sp.wait_ge(delta_split, 5)
            for j in range(3):
                sp.dma_start(addR[j:j + 1, :].rearrange("o (b k) -> o b k", b=B), dlb[:, j, :]).then_inc(rows_moved, 16)
            sp.wait_ge(rows_moved, 48)
            sp.dma_start(dl[:, 1, :], a["L3_ffn_b1"]).then_inc(b_loaded, 16)
            sp.dma_start(b2l[:, 1, :], a["L3_ffn_b2"]).then_inc(b_loaded, 16)
            sp.wait_ge(sim_step, 11)
            sp.wait_ge(sim_pool, 4)
            for dst, j in ((maskR[0:1, :], 0), (maskR[1:2, :], 1), (clsrow[0], 2), (clsrow[1], 3)):
                sp.dma_start(dst.rearrange("o (c k) -> o c k", c=CHUNKS), clsb[:, j, :]).then_inc(cls_rows, 16)
            sp.wait_ge(x_updated, TILES * 4)
            sp.dma_start(QT[:, :].rearrange("p (t d) -> p t d", d=D),
                         a["ctx_1024"].rearrange("b s d -> (b s) d").rearrange("(t p) d -> p t d", p=128)).then_inc(ctx2_loaded, 16)
            def mixture(m):
                ln, F, tiles, before = MOE[m]
                if m == 0:
                    sp.wait_ge(g2_ready, CHUNKS)
                    w_in = wv[:, 0:(NE + 1) * 512]
                    w_out = wv[:, (NE + 1) * 512:(NE + 1) * 768]
                    for j, n in enumerate(("rt_gate", "rt_up")):
                        sp.dma_start(w_in[:, 0:NE * 512].rearrange("p (e j f) -> p e j f", e=NE, j=2)[:, :, j, :],
                                     a["L2_ffn_" + n].rearrange("e p f -> p e f")).then_inc(experts_loaded, 16)
                    for j, n in enumerate(("sh_gate", "sh_up")):
                        sp.dma_start(w_in[:, NE * 512 + 256 * j:NE * 512 + 256 * j + 256], a["L2_ffn_" + n]).then_inc(experts_loaded, 16)
                    sp.dma_start(w_out[:, 0:NE * 256].rearrange("p (e j d) -> p e j d", e=NE, j=2),
                                 a["L2_ffn_rt_down"].rearrange("e (j p) d -> p e j d", p=128)).then_inc(experts_loaded, 16)
                    sp.dma_start(w_out[:, NE * 256:(NE + 1) * 256].rearrange("p (j d) -> p j d", j=2),
                                 a["L2_ffn_sh_down"].rearrange("(j p) d -> p j d", p=128)).then_inc(experts_loaded, 16)
                    sp.wait_ge(xn_kept, CHUNKS)
                    sp.dma_start(xs_dram[SLOTS * 128:, :].rearrange("(t p) d -> p t d", p=128),
                                 QT[:, :].rearrange("p (t d) -> p t d", d=D)).then_inc(shared_rows, 16)
                else:
                    sp.wait_ge(b_split, 10)
                    for j in range(3):
                        sp.dma_start(b1r[j:j + 1, :].rearrange("o (b k) -> o b k", b=64), dlb[:, j, :]).then_inc(b_rows, 16)
                        sp.dma_start(b2r[j:j + 1, :].rearrange("o (b k) -> o b k", b=64), b2b[:, j, :]).then_inc(b_rows, 16)
                    sp.wait_ge(pv_ready, units_before[4])
                    for h in range(2):
                        e = slice(4 * h, 4 * h + 4)
                        sp.dma_start(wv[:, 2048 * h:2048 * h + 2048].rearrange("p (e f) -> p e f", e=4),
                                     a["L3_ffn_W1T"][e].rearrange("e p f -> p e f")).then_inc(experts_loaded, 16)
                        sp.dma_start(wv[:, 4096 + 2048 * h:6144 + 2048 * h].rearrange("p (e j d) -> p e j d", e=4, j=4),
                                     a["L3_ffn_W2T"][e].rearrange("e (j p) d -> p e j d", p=128)).then_inc(experts_loaded, 16)
                sp.wait_ge(shared_rows, 16)
                sp.wait_ge(scattered, 16 * TILES * (m + 1))

                def step(k, turn, u, live):
                    if live(0):
                        wait_reuse(sp, e_turned, before + k - 3)
                        sp.dma_start(xl[u], rows_of(xs_dram, k)).then_inc(tile_loaded[u], 16)
                    if live(4):
                        sp.wait_ge(e_y, before + k - 3)
                        sp.dma_start(rows_of(ys_dram, k - 4), ys[u]).then_inc(tile_stored[u], 16)

                pipeline(sp, tiles, 4, 4, step)
                for i in range(4):
                    sp.wait_ge(tile_stored[i], 4 * (before + tiles))
                if m == 0:
                    sp.dma_start(KT[:, :].rearrange("p (t d) -> p t d", d=D),
                                 ys_dram[SLOTS * 128:, :].rearrange("(t p) d -> p t d", p=128)).then_inc(shared_back, 16)

            mixture(0)
            mixture(1)
            ov = out.rearrange("b s d -> (b s) d").rearrange("(t p) d -> p t d", p=128)
            for q in range(4):
                sp.wait_ge(x_updated, TILES * 7 + 8 * q + 8)
                sp.dma_start(ov[:, 8 * q:8 * q + 8, :], X[:, 8 * q:8 * q + 8, :]).then_inc(stored, 16)
            sp.wait_ge(stored, 64)

        @block.gpsimd
        def _(pool):
            for i in range(2):
                pool.memset(on[i][:, :, :], 0.0).then_inc(consts_ready, 1)
            pool.memset(onesr[:, :], 1.0).then_inc(consts_ready, 1)
            pool.memset(ones_row[:, :], 1.0).then_inc(consts_ready, 1)
            pool.memset(ones128[:, :], 1.0).then_inc(consts_ready, 1)
            pool.memset(th[0][:, 0:128], 0.0).then_inc(zero_ready, 1)
            pool.wait_ge(cst_loaded, CST_DMAS * 16)
            pool.tensor_copy(VB[:, :, :].rearrange("p b (g w) -> p b g w", w=VW)[:, :, :, VW - 1],
                             v_ones.unsqueeze(1).broadcast_to([128, B, G])).then_inc(consts_ready, 1)

            def attention(l):
                wb = units_before[l]
                passes = PASSES[l]

                def step(k, turn, u, live):
                    if not live(0):
                        return
                    s = u % 2
                    at = unit(turn, u, passes) * S
                    wait_reuse(pool, scores_ready, wb + k - 1)
                    pool.sem_inc(slot_free, 1)
                    pool.tensor_tensor(
                        kbd[s][:, :].rearrange("p (g k) -> p g k", g=G),
                        KT[:, bass.ds(at, S)].unsqueeze(1).broadcast_to([128, G, S]),
                        g_mask[:, :].unsqueeze(2).broadcast_to([128, G, S]), ALU.mult).then_inc(staged, 1)
                    pool.tensor_tensor(
                        qbd[s][:, :].rearrange("p (g k) -> p g k", g=2),
                        QT[:, bass.ds(at, S)].unsqueeze(1).broadcast_to([128, 2, S]),
                        hp_mask[:, :].unsqueeze(2).broadcast_to([128, 2, S]), ALU.mult).then_inc(staged, 1)
                    if u % 2 == 1 and (passes == 1 or u == 3):
                        t = turn * 2 + u // 2 if passes == 1 else turn
                        pool.tensor_tensor(X[:, bass.ds(t, 1), :].rearrange("p o d -> p (o d)"),
                                           X[:, bass.ds(t, 1), :].rearrange("p o d -> p (o d)"),
                                           bo[:, l, :], ALU.add).then_inc(bo_added, 1)

                pool.wait_ge(w_loaded, W_DMAS * 16)
                pool.wait_ge(q_ready, CHUNKS * (l + 1))
                pool.wait_ge(bo_ready, 1)
                pool.wait_ge(k_ready, CHUNKS * (l + 1))
                pipeline(pool, B * passes, 4, 0, step)

            def prepare(l, ln, cross):
                def step(k, turn, u, live):
                    wait_reuse(pool, proj_ready, 4 * (CHUNKS * l + k - 1))
                    if cross:
                        src = ctxT[:, bass.ds(k * CHUNK, CHUNK)]
                    else:
                        pool.wait_ge(xt_ready, CHUNKS * ln + k + 1)
                        src = xts[u][:, :]
                    pool.sem_inc(slot_free, 1)
                    pool.tensor_copy(xd[u][:, :, :, :], src.rearrange("p (b s) -> p b s", b=BPC).unsqueeze(2)
                                     .broadcast_to([128, BPC, 2, S])).then_inc(doubled, 1)

                if cross:
                    pool.wait_ge(ctx_loaded, 64)
                pipeline(pool, CHUNKS, 2, 0, step)

            for i in range(2):
                pool.memset(addL[i][:, :], 1.0).then_inc(consts_ready, 1)

            def classes():
                pool.wait_ge(q_ready, 2 * CHUNKS)
                pool.memset(clsb[:, 1, :], -BIG).then_inc(sim_pool, 1)
                pool.wait_ge(sim_pool, 1)
                pool.memset(by_batch(clsb[:, 1, :])[:, :, 0:REG], 0.0).then_inc(sim_pool, 1)
                pool.wait_ge(sim_step, 6)
                pool.partition_all_reduce(ext[:, 2:4], ext[:, 0:2], CHUNKS, bass.bass_isa.ReduceOp.max).then_inc(sim_pool, 2)

            prepare(0, 0, True)
            attention(0)
            prepare(1, 1, False)
            classes()
            attention(1)
            prepare(2, 2, True)
            attention(2)

            pool.wait_ge(keep_ready, 2)
            tiles = [128, TILES, 128]
            idx = own_idx.unsqueeze(1).broadcast_to(tiles)
            k3 = keep.rearrange("p (t l) -> p t l", l=128)
            g3 = gauss.rearrange("p (t l) -> p t l", l=128)
            per = lambda j: win[:, j, :].unsqueeze(2).broadcast_to(tiles)
            pool.tensor_tensor(k3, k3, g3, ALU.mult).then_inc(keep_ready, 1)
            pool.wait_ge(keep_ready, 3)
            pool.tensor_scalar(k3, k3, 3e38, None, ALU.mult).then_inc(keep_ready, 1)
            pool.tensor_tensor(g3, idx, per(0), ALU.subtract).then_inc(keep_ready, 1)
            pool.wait_ge(keep_ready, 5)
            pool.tensor_tensor(k3, k3, far.unsqueeze(1).broadcast_to(tiles), ALU.add).then_inc(keep_ready, 1)
            pool.tensor_tensor(g3, g3, g3, ALU.mult).then_inc(keep_ready, 1)

            def mixture(m):
                ln, F, tiles, before = MOE[m]
                if m == 0:
                    pool.wait_ge(cx_in_psum, CHUNKS)

                def step(k, turn, u, live):
                    pool.wait_ge(xn_ready, TPC * (CHUNKS * ln + k + 1))
                    pool.sem_inc(slot_free, 1)
                    pool.tensor_copy(QT[:, bass.ds(k * CHUNK, CHUNK)], xn[:, :, :].rearrange("p t d -> p (t d)")).then_inc(xn_kept, 1)

                pipeline(pool, CHUNKS, 2, 0, step)
                pool.wait_ge(xn_kept, CHUNKS * (m + 1))
                pool.wait_ge(zeroed, 16)
                pool.wait_ge(place_step, PLACE_STEPS[m + 1])
                for t in range(TILES):
                    pool.indirect_dma_start(xs_dram[0:SLOTS * 128, :], bass.IndirectOffsetOnAxis(dest[:, t:t + 1], 0),
                                            QT[:, D * t:D * t + D], None).then_inc(scattered, 16)
                for i in range(4):
                    pool.wait_ge(tile_stored[i], 4 * (before + tiles))
                pool.wait_ge(scattered, 16 * TILES * (m + 1))
                for t in range(TILES):
                    pool.indirect_dma_start(QT[:, D * t:D * t + D], None, ys_dram[0:SLOTS * 128, :],
                                            bass.IndirectOffsetOnAxis(dest[:, t:t + 1], 0)).then_inc(gathered, 16)

            mixture(0)
            pool.wait_ge(e_hidden, MOE[0][2])
            pool.wait_ge(e_out, MOE[0][2])
            pool.tensor_copy(VB[:, :, :].rearrange("p b (g w) -> p b g w", w=VW)[:, :, :, VW - 1],
                             v_ones.unsqueeze(1).broadcast_to([128, B, G])).then_inc(ones_again, 1)
            prepare(3, 6, True)
            attention(3)
            mixture(1)



        @block.vector
        def _(v):
            v.wait_ge(side_loaded, 32)
            v.tensor_scalar(tau_s[:, :], tau_b[:, :], float(E) ** -0.5, None, ALU.mult).then_inc(ln_step, 1)
            v.tensor_scalar(dl[:, 1, :], dl[:, 0, :], float(E) ** -0.5, None, ALU.mult).then_inc(ln_step, 1)
            v.wait_ge(ln_step, 2)

            def split3(x, parts, counter, n):
                v.tensor_copy(parts[:, 0, :], x[:, 1, :]).then_inc(counter, 1)
                v.wait_ge(counter, n + 1)
                v.tensor_tensor(x[:, 2, :], x[:, 1, :], parts[:, 0, :], ALU.subtract).then_inc(counter, 1)
                v.wait_ge(counter, n + 2)
                v.tensor_copy(parts[:, 1, :], x[:, 2, :]).then_inc(counter, 1)
                v.wait_ge(counter, n + 3)
                v.tensor_tensor(x[:, 1, :], x[:, 2, :], parts[:, 1, :], ALU.subtract).then_inc(counter, 1)
                v.wait_ge(counter, n + 4)
                v.tensor_copy(parts[:, 2, :], x[:, 1, :]).then_inc(counter, 1)

            split3(dl, dlb, delta_split, 0)
            n_ln = 2
            v.wait_ge(w_loaded, W_DMAS * 16)
            v.wait_ge(bias_through, 1)
            v.tensor_tensor(bo[:, :, :].rearrange("p l d -> p (l d)"), psY[:, :],
                            bo[:, :, :].rearrange("p l d -> p (l d)"), ALU.add).then_inc(bo_ready, 1)

            def norms(l):
                nonlocal n_ln
                if l == 0:
                    v.wait_ge(x_loaded, 64)
                else:
                    v.wait_ge(x_updated, TILES * l)

                with v.Fori(0, TILES // 4) as t:
                    for u in range(4):
                        v.bn_stats(stats[:, bass.ds(t * 4 + u, 1), :].rearrange("p o c -> p (o c)"),
                                   X[:, bass.ds(t * 4 + u, 1), :].rearrange("p o d -> p (o d)")).then_inc(stats_ready, 1)
                v.wait_ge(stats_ready, TILES * (l + 1))
                me, mo, se, so = stats[:, :, 1], stats[:, :, 4], stats[:, :, 2], stats[:, :, 5]
                n = n_ln
                v.tensor_tensor(lnw[:, 0, :], me, mo, ALU.add).then_inc(ln_step, 1)
                v.tensor_tensor(lnw[:, 1, :], me, mo, ALU.subtract).then_inc(ln_step, 1)
                v.tensor_tensor(lnw[:, 2, :], se, so, ALU.add).then_inc(ln_step, 1)
                v.wait_ge(ln_step, n + 3)
                v.tensor_tensor(lnw[:, 1, :], lnw[:, 1, :], lnw[:, 1, :], ALU.mult).then_inc(ln_step, 1)
                v.tensor_scalar(lnw[:, 2, :], lnw[:, 2, :], 1.0 / D, EPS, ALU.mult, ALU.add).then_inc(ln_step, 1)
                v.wait_ge(ln_step, n + 5)
                v.scalar_tensor_tensor(lnw[:, 3, :], lnw[:, 1, :], 0.25, lnw[:, 2, :], ALU.mult, ALU.add).then_inc(ln_step, 1)
                v.wait_ge(ln_step, n + 6)
                v.wait_ge(rsqrt_ready, 2 * l + 2)
                y, t = lnw[:, 5, :], lnw[:, 1, :]
                v.tensor_tensor(t, y, y, ALU.mult).then_inc(ln_step, 1)
                v.wait_ge(ln_step, n + 7)
                v.tensor_tensor(t, t, lnw[:, 3, :], ALU.mult).then_inc(ln_step, 1)
                v.wait_ge(ln_step, n + 8)
                v.tensor_scalar(t, t, -0.5, 1.5, ALU.mult, ALU.add).then_inc(ln_step, 1)
                v.wait_ge(ln_step, n + 9)
                v.tensor_tensor(rstd[:, :], t, y, ALU.mult).then_inc(norm_ready, 1)
                v.wait_ge(norm_ready, 2 * l + 1)
                v.scalar_tensor_tensor(nmr[:, :], lnw[:, 0, :], -0.5, rstd[:, :], ALU.mult, ALU.mult).then_inc(norm_ready, 1)
                n_ln = n + 9

            def prepare(l, ln, tau):
                norms(ln)

                def step(k, turn, u, live):
                    s = u % 2
                    if live(0):
                        v.wait_ge(xt_in_psum, CHUNKS * ln + k + 1)
                        v.tensor_copy(xts[s][:, :], (psT, psY)[s][:, :]).then_inc(xt_ready, 1)
                    if live(1):
                        c = k - 1
                        r = (s + 1) % 2
                        v.wait_ge(proj_ready, 4 * (CHUNKS * l + c) + 1)
                        if tau is None:
                            v.tensor_scalar(QT[:, bass.ds(c * CHUNK, CHUNK)], psS[r][:, :], bqkv[:, l, 0:1],
                                            float(E) ** -0.5, ALU.add, ALU.mult).then_inc(q_ready, 1)
                        else:
                          v.scalar_tensor_tensor(
                            QT[:, bass.ds(c * CHUNK, CHUNK)].rearrange("p (b s) -> p b s", b=BPC),
                            psS[r][:, :].rearrange("p (b s) -> p b s", b=BPC), bqkv[:, l, 0:1],
                            tau_s[:, bass.ds(c * BPC, BPC)].unsqueeze(2).broadcast_to([128, BPC, S]),
                            ALU.add, ALU.mult).then_inc(q_ready, 1)
                        for h in range(2):
                            v.wait_ge(proj_ready, 4 * (CHUNKS * l + c) + 3 + h)
                            v.tensor_tensor(
                                VB[:, bass.ds(c * BPC + 4 * h, 4), :].rearrange("p b (g w) -> p b g w", w=VW)[:, :, :, 0:2 * E],
                                psO[h][:, :].rearrange("p (b g w) -> p b g w", b=4, w=2 * E),
                                v_mask.rearrange("p (g w) -> p g w", w=2 * E).unsqueeze(1).broadcast_to([128, 4, G, 2 * E]),
                                ALU.mult).then_inc(v_ready, 1)

                v.wait_ge(w_loaded, W_DMAS * 16)
                pipeline(v, CHUNKS, 2, 1, step)

            def attention(l):
                wb = units_before[l]
                passes = PASSES[l]
                behind = passes - 1
                if passes == 2:
                    v.wait_ge(cls_rows, 64)

                def step(k, turn, u, live):
                    if passes == 2 and live(0):
                        wait_reuse(v, scores_ready, wb + k - 1)
                        v.tensor_copy(addL[u % 2][0:1, :].rearrange("o (j s) -> o j s", j=2),
                                      clsrow[u // 2][:, bass.ds(unit(turn, u, passes) * S, S)]
                                      .unsqueeze(1).broadcast_to([1, 2, S])).then_inc(class_staged, 1)
                    if live(behind):
                        s = (u - behind) % 2
                        n = wb + k - behind
                        sc = psS[s][:, :].rearrange("p (g k) -> p g k", g=G)
                        v.wait_ge(scores_ready, n + 1)
                        v.tensor_reduce(mx[s][:, :], sc, AX.X, ALU.max).then_inc(max_ready, 1)
                        wait_reuse(v, p_turned, n - 1)
                        v.wait_ge(max_ready, n + 1)
                        v.tensor_tensor(Pr[s][:, :].rearrange("p (g k) -> p g k", g=G), sc,
                                        mx[s][:, :].unsqueeze(2).broadcast_to([128, G, S]),
                                        ALU.subtract).then_inc(shifted, 1)
                    if u % 2 == 0 and live(4):
                        m2 = k - 4
                        m = turn * 2 + u // 2 - 2
                        ps = (u // 2) % 2
                        v.wait_ge(pv_ready, wb + m2 + 2)
                        oo = psO[ps][:, 0:2 * G * VW].rearrange("p (g w) -> p g w", w=VW)
                        wait_reuse(v, on_ready, wb + m2)
                        v.reciprocal(rden[:, :].unsqueeze(2), oo[:, :, VW - 1:VW]).then_inc(rden_ready, 1)
                        v.wait_ge(rden_ready, wb // 2 + m + 1)
                        wait_reuse(v, ot_ready, TILES * l + (m - 1 if passes == 1 else turn - 1))
                        dst = on[ps][:, :, :].rearrange("p b (g w) -> p (b g) w", w=2 * E)
                        for hp in range(2):
                            r = slice(64 * hp, 64 * hp + 64)
                            v.tensor_tensor(dst[r, :, E * hp:E * hp + E], oo[r, :, E * hp:E * hp + E],
                                            rden[r, :].unsqueeze(2).broadcast_to([64, 2 * G, E]),
                                            ALU.mult).then_inc(on_ready, 1)
                    if (u == 0 or (u == 2 and passes == 1)) and live(6):
                        t = turn * 2 + u // 2 - 3 if passes == 1 else turn - 2
                        v.wait_ge(y_ready, TILES * l + t + 1)
                        v.wait_ge(bo_added, TILES * l + t + 1)
                        xt = X[:, bass.ds(t, 1), :].rearrange("p o d -> p (o d)")
                        v.tensor_tensor(xt, psY[:, 0:128], xt, ALU.add).then_inc(x_updated, 1)

                pipeline(v, B * passes, 4, 5, step)

            def classes():
                v.wait_ge(g_loaded, 16)
                v.wait_ge(cst_loaded, 16 * CST_DMAS)
                v.tensor_scalar(guide_pad[:, :], heads_pad, gcol[:, 0:1], None, ALU.mult).then_inc(sim_step, 1)
                v.tensor_tensor(gcol[:, 1:2], gcol[:, 0:1], gcol[:, 0:1], ALU.mult).then_inc(sim_step, 1)
                v.wait_ge(sim_pe, 1)
                v.tensor_copy(n2g[:, :], psY[:, 0:1]).then_inc(sim_step, 1)
                v.wait_ge(sim_step, 3)
                v.wait_ge(sim_pe, 3)
                v.tensor_scalar(n2[0][:, :], psS[0][:, :], n2g[:, 0:1], None, ALU.mult).then_inc(sim_act, 1)
                v.wait_ge(sim_act, 3)
                y, t = n2[2][:, :], n2[3][:, :]
                v.tensor_tensor(t, y, y, ALU.mult).then_inc(sim_newton, 1)
                v.wait_ge(sim_newton, 1)
                v.tensor_tensor(t, t, n2[0][:, :], ALU.mult).then_inc(sim_newton, 1)
                v.wait_ge(sim_newton, 2)
                v.tensor_scalar(t, t, -0.5, 1.5, ALU.mult, ALU.add).then_inc(sim_newton, 1)
                v.wait_ge(sim_newton, 3)
                v.tensor_tensor(t, t, y, ALU.mult).then_inc(sim_newton, 1)
                v.wait_ge(sim_newton, 4)
                v.tensor_tensor(n2[4][:, :], psS[1][:, :], t, ALU.mult).then_inc(sim_step, 1)
                v.wait_ge(sim_pe, 4)
                sim = by_batch(psP[0][0:CHUNKS, :])[:, :, REG:S]
                v.tensor_reduce(ext[:, 0:1], sim, AX.XY, ALU.max).then_inc(sim_step, 1)
                v.tensor_reduce(ext[:, 1:2], sim, AX.XY, ALU.min, negate=True).then_inc(sim_step, 1)
                v.wait_ge(sim_pool, 4)
                v.tensor_scalar(ext[:, 4:5], ext[:, 2:3], ext[:, 3:4], 0.9, ALU.add, ALU.mult).then_inc(sim_step, 1)
                v.wait_ge(sim_step, 7)
                v.tensor_scalar(simr, psP[0][0:CHUNKS, :], ext[:, 3:4], ext[:, 4:5], ALU.add, ALU.is_gt).then_inc(sim_step, 1)
                v.wait_ge(sim_step, 8)
                v.tensor_scalar(clsb[:, 0, :], simr, 2.0 * BIG, -BIG, ALU.mult, ALU.add).then_inc(sim_newton, 1)
                v.tensor_scalar(clsb[:, 2, :], simr, 2.0, -1.0, ALU.mult, ALU.add).then_inc(sim_newton, 1)
                v.tensor_scalar(clsb[:, 3, :], simr, 2.0, -1.0, ALU.mult, ALU.add).then_inc(sim_newton, 1)
                v.wait_ge(sim_newton, 7)
                for j, c in ((0, 0.0), (2, 1.0), (3, -1.0)):
                    v.memset(by_batch(clsb[:, j, :])[:, :, 0:REG], c).then_inc(sim_step, 1)

            prepare(0, 0, tau_s)
            attention(0)
            prepare(1, 1, None)
            classes()
            attention(1)
            prepare(2, 2, tau_s)
            attention(2)

            def xt_evac(ln, k, u):
                v.wait_ge(xt_in_psum, CHUNKS * ln + k + 1)
                v.tensor_copy(xts[u][:, :], (psT, psY)[u][:, :]).then_inc(xt_ready, 1)

            def routing(r):
                n = ROUTE_STEPS * r
                by_tile = lambda x: x.rearrange("p e t -> p t e")
                best = lambda j: gate[:, j, :].unsqueeze(1).broadcast_to([128, NE, TILES])
                v.wait_ge(logit_ready, CHUNKS * (r + 1))
                v.tensor_reduce(gate[:, 0, :], by_tile(logit[:, :, :]), AX.X, ALU.max).then_inc(route_step, 1)
                v.wait_ge(route_step, n + 1)
                v.tensor_tensor(rt[:, 0, :, :], logit[:, :, :], best(0), ALU.subtract).then_inc(route_step, 1)
                v.wait_ge(route_step, n + 2)
                v.scalar_tensor_tensor(rt[:, 1, :, :], rt[:, 0, :, :], 0.0, first_w.rearrange("p (e t) -> p e t", e=NE),
                                       ALU.is_equal, ALU.mult).then_inc(route_step, 1)
                v.wait_ge(route_step, n + 3)
                v.tensor_reduce(gate[:, 1, :], by_tile(rt[:, 1, :, :]), AX.X, ALU.max).then_inc(route_step, 1)
                v.wait_ge(route_step, n + 4)
                v.tensor_tensor(oh[:, :, :], rt[:, 1, :, :], best(1), ALU.is_equal).then_inc(route_step, 1)
                v.wait_ge(rank_ready, 2 * r + 2)
                v.tensor_copy(rt[:, 2, :, :], psO[0][:, 0:256].rearrange("p (e t) -> p e t", e=NE)).then_inc(route_step, 1)
                v.wait_ge(route_step, n + 6)
                flat = lambda j: rt[:, j, :, :].rearrange("p e t -> p (e t)")
                v.tensor_tensor_scan(flat(1), not_first, flat(2), 0.0, ALU.mult, ALU.add).then_inc(route_step, 1)
                v.wait_ge(route_step, n + 7)
                v.tensor_tensor(flat(3), flat(1), flat(2), ALU.subtract).then_inc(route_step, 1)
                v.wait_ge(route_step, n + 8)
                v.tensor_tensor(flat(3), flat(3), psO[1][:, 0:256], ALU.add).then_inc(route_step, 1)
                v.wait_ge(route_step, n + 9)

            def mixture1():
                norms(3)

                def step(k, turn, u, live):
                    if live(0):
                        xt_evac(3, k, u)
                    if live(1):
                        r = (u + 1) % 2
                        v.wait_ge(route_pe, k)
                        v.tensor_copy(logit[:, :, bass.ds((k - 1) * TPC, TPC)],
                                      psO[r][:, 0:NE * TPC].rearrange("p (t e) -> p e t", e=NE)).then_inc(logit_ready, 1)
                        v.tensor_tensor(Yt[:, bass.ds((k - 1) * CHUNK, CHUNK)].rearrange("p (t d) -> p t d", d=D),
                                        psS[r][:, :].rearrange("p (t d) -> p t d", d=D),
                                        be[:, :].unsqueeze(1).broadcast_to([128, TPC, D]), ALU.add).then_inc(y_kept, 1)

                pipeline(v, CHUNKS, 2, 1, step)
                routing(0)
                v.scalar_tensor_tensor(rt[:, 1, :, :], rt[:, 3, :, :], float(CAP), oh[:, :, :], ALU.is_le, ALU.mult).then_inc(win_step, 1)
                v.wait_ge(win_step, 5)
                v.tensor_reduce(gate[:, 1, :], rt[:, 1, :, :].rearrange("p e t -> p t e"), AX.X, ALU.add).then_inc(win_step, 1)
                v.wait_ge(route_act, 1)
                v.tensor_reduce(gate[:, 2, :], rt[:, 2, :, :].rearrange("p e t -> p t e"), AX.X, ALU.add).then_inc(win_step, 1)
                v.wait_ge(win_step, 7)
                v.reciprocal(gate[:, 3, :], gate[:, 2, :]).then_inc(win_step, 1)
                v.wait_ge(win_step, 8)
                v.tensor_tensor(gate[:, 1, :], gate[:, 1, :], gate[:, 3, :], ALU.mult).then_inc(win_step, 1)
                v.wait_ge(win_step, 9)
                v.wait_ge(y_kept, CHUNKS)
                with v.Fori(0, TILES // 4) as turn:
                    for u in range(4):
                        t = turn * 4 + u
                        row = lambda x: x[:, bass.ds(t * D, D)]
                        xt = X[:, bass.ds(t, 1), :].rearrange("p o d -> p (o d)")
                        v.scalar_tensor_tensor(xt, row(Yt), gate[:, 1, bass.ds(t, 1)], xt, ALU.mult, ALU.add).then_inc(x_updated, 1)

            def attention2():
                norms(4)

                def step(k, turn, u, live):
                    s, r = u, (u + 1) % 2
                    if live(0):
                        xt_evac(4, k, u)
                    if live(1):
                        c = k - 1
                        v.wait_ge(s2_ready, k)
                        wait_reuse(v, at_turned, k - 2)
                        v.tensor_tensor(sc2[r][:, :], psS[r][:, :], keep[:, bass.ds(c * CHUNK, CHUNK)], ALU.min).then_inc(capped, 1)
                        v.wait_ge(capped, k)
                        wait_reuse(v, e2_ready, TPC * (k - 2))
                        v.tensor_reduce(nmx[r][:, :], sc2[r][:, :].rearrange("p (t l) -> p t l", l=128), AX.X, ALU.max,
                                        negate=True).then_inc(nmx_ready, 1)
                        v.wait_ge(e2_ready, TPC * k)
                        v.tensor_tensor(sc2[r][:, :], sc2[r][:, :], gauss[:, bass.ds(c * CHUNK, CHUNK)], ALU.mult).then_inc(g2_ready, 1)
                        v.reciprocal(den[r][:, 1, :], den[r][:, 0, :]).then_inc(rd2_ready, 1)
                        v.wait_ge(rd2_ready, k)
                        v.wait_ge(cx_in_psum, k)
                        wait_reuse(v, cx_turned, k - 2)
                        v.tensor_tensor(cx[r][:, :].rearrange("p (t d) -> p t d", d=D),
                                        psO[0][:, :].rearrange("p (t d) -> p t d", d=D),
                                        den[r][:, 1, :].unsqueeze(2).broadcast_to([128, TPC, D]), ALU.mult).then_inc(cx_ready, 1)
                    if live(2):
                        c = k - 2
                        v.wait_ge(th_ready, k - 1)
                        xc = X[:, bass.ds(c * TPC, TPC), :].rearrange("p t d -> p (t d)")
                        v.tensor_tensor(xc, th[s][:, :], xc, ALU.add).then_inc(x_updated, TPC)

                v.wait_ge(keep_ready, 7)
                v.wait_ge(gauss_ready, 1)
                pipeline(v, CHUNKS, 2, 2, step)

            v.wait_ge(l2_loaded, 80)
            v.tensor_scalar(win[:, 2, :], win[:, 0, :], -WINDOW, 0.0, ALU.add, ALU.max).then_inc(win_step, 1)
            v.tensor_scalar(win[:, 4, :], win[:, 0, :], WINDOW, None, ALU.add).then_inc(win_step, 1)
            v.tensor_copy(win[:, 1, :], leni[:, :]).then_inc(win_step, 1)
            v.wait_ge(win_step, 3)
            v.tensor_tensor(win[:, 3, :], win[:, 4, :], win[:, 1, :], ALU.min).then_inc(win_step, 1)
            v.wait_ge(win_step, 4)
            v.wait_ge(pv_ready, units_before[3])
            for dst, j, cmp in ((keep, 2, ALU.is_ge), (gauss, 3, ALU.is_le)):
                v.tensor_tensor(dst.rearrange("p (t l) -> p t l", l=128),
                                own_idx.unsqueeze(1).broadcast_to([128, TILES, 128]),
                                win[:, j, :].unsqueeze(2).broadcast_to([128, TILES, 128]), cmp).then_inc(keep_ready, 1)
            mixture1()
            def mixture(m):
                ln, F, tiles, before = MOE[m]
                norms(ln)
                v.wait_ge(mw_loaded, 48)

                def step(k, turn, u, live):
                    if live(0):
                        xt_evac(ln, k, u)
                    if live(1):
                        r = (u + 1) % 2
                        v.wait_ge(route_pe, CHUNKS * (m + 1) + k)
                        src = psO[r][:, 0:NE * TPC].rearrange("p (t e) -> p e t", e=NE)
                        dst = logit[:, :, bass.ds((k - 1) * TPC, TPC)]
                        if m == 0:
                            v.tensor_copy(dst, src).then_inc(logit_ready, 1)
                        else:
                            v.tensor_tensor(dst, src, rb[:, :].unsqueeze(2).broadcast_to([128, NE, TPC]), ALU.add).then_inc(logit_ready, 1)

                pipeline(v, CHUNKS, 2, 1, step)
                routing(m + 1)
                n = PLACE_STEPS[m]

                def done(ins):
                    nonlocal n
                    ins.then_inc(place_step, 1)
                    n += 1

                done(v.tensor_scalar(ei[:, 0, :], rt[:, 1, :, TILES - 1], 127.0, None, ALU.add))
                v.wait_ge(place_step, n)
                done(v.tensor_scalar(ei[:, 1, :], ei[:, 0, :], 7, None, ALU.arith_shift_right))
                v.wait_ge(place_step, n)
                done(v.tensor_copy(ef[:, 0, :], ei[:, 1, :]))
                v.wait_ge(place_step, n)
                done(v.tensor_tensor_scan(ef[:, 1, :], ones128[:, 0:NE], ef[:, 0, :], 0.0, ALU.mult, ALU.add))
                v.wait_ge(place_step, n)
                done(v.tensor_tensor(slots[:, :, :], slot_no.unsqueeze(2).broadcast_to([128, SLOTS, NE]),
                                     ef[:, 1, :].unsqueeze(1).broadcast_to([128, SLOTS, NE]), ALU.is_ge))
                done(v.tensor_tensor(ef[:, 2, :], ef[:, 1, :], ef[:, 0, :], ALU.subtract))
                v.wait_ge(place_step, n)
                done(v.tensor_reduce(slotf[:, :], slots[:, :, :], AX.X, ALU.add))
                done(v.scalar_tensor_tensor(rt[:, 0, :, :], ef[:, 2, :].unsqueeze(2).broadcast_to([128, NE, TILES]), 128.0,
                                            rt[:, 3, :, :], ALU.mult, ALU.add))
                v.wait_ge(place_step, n)
                done(v.tensor_scalar(slot_e[:, 0:SLOTS], slotf[:, :], float(NE - 1), None, ALU.min))
                done(v.scalar_tensor_tensor(rt[:, 1, :, :], rt[:, 0, :, :], -1.0, oh[:, :, :], ALU.add, ALU.mult))
                v.wait_ge(place_step, n)
                if m == 0:
                    v.wait_ge(score_act, 1)
                    done(v.tensor_scalar(gate[:, 2, :], gate[:, 1, :], 1.0, None, ALU.add))
                    done(v.memset(slot_e[:, SLOTS:], NE))
                    v.wait_ge(place_step, n)
                    done(v.reciprocal(gate[:, 3, :], gate[:, 2, :]))
                    v.wait_ge(place_step, n)
                    v.wait_ge(shared_rows, 16)
                    rows = QT[:, :].rearrange("p (t d) -> p t d", d=D)
                    done(v.tensor_tensor(rows, rows, gate[:, 3, :].unsqueeze(2).broadcast_to([128, TILES, D]), ALU.mult))
                done(v.tensor_reduce(gate[:, 2, :], rt[:, 1, :, :].rearrange("p e t -> p t e"), AX.X, ALU.add))
                v.wait_ge(place_step, n)
                done(v.tensor_copy(dest[:, :], gate[:, 2, :]))
                assert n == PLACE_STEPS[m + 1], n

                def expert_step(k, turn, u, live):
                    s = u % 2
                    if live(0):
                        v.wait_ge(e_turned, before + k + 1)
                        wait_reuse(v, e_hidden, before + k - 1)
                        v.tensor_copy(xT[s], psT[:, 0:128]).then_inc(e_xT, 1)
                    if live(1):
                        r = (s + 1) % 2
                        if m == 0:
                            v.wait_ge(e_act, before + k)
                            wait_reuse(v, e_hturned, before + k - 2)
                            v.tensor_tensor(hb[r][:, 0:F], act2[r][:, 0:F], psS[r][:, F:2 * F], ALU.mult).then_inc(e_h, 1)
                    if live(2):
                        v.wait_ge(e_hturned, before + k - 1)
                        wait_reuse(v, e_out, before + k - 3)
                        v.tensor_copy(hT[s][:, 0:F], psP[s][:, 0:F]).then_inc(e_hT, 1)

                pipeline(v, tiles, 4, 2, expert_step)
                v.wait_ge(gathered, 16 * TILES * (m + 1))
                v.wait_ge(shared_back, 16)
                with v.Fori(0, TILES // 4) as turn:
                    for part in ((QT, KT) if m == 0 else (QT,)):
                        xc = X[:, bass.ds(turn * 4, 4), :].rearrange("p t d -> p (t d)")
                        ins = v.tensor_tensor(xc, part[:, bass.ds(turn * 4 * D, 4 * D)], xc, ALU.add)
                        if m == 0 and part is QT:
                            ins.then_inc(routed_added, 1)
                            v.wait_ge(routed_added, turn + 1)
                        else:
                            ins.then_inc(x_updated, 4)

            attention2()
            mixture(0)
            v.wait_ge(b_loaded, 32)
            split3(dl, dlb, b_split, 0)
            split3(b2l, b2b, b_split, 5)
            prepare(3, 6, tau_s)
            attention(3)
            mixture(1)

        @block.scalar
        def _(act):
            act.dma_start(tau_b[:, :], a["condB_tau"].rearrange("(o b) -> o b", o=1).broadcast_to([128, B])).then_inc(side_loaded, 16)
            act.dma_start(gcol[:, 0:1], a["g_first"]).then_inc(g_loaded, 16)
            act.dma_start(dl[:, 0, :], a["fside_BxS2_0"]).then_inc(side_loaded, 16)
            for i, n in enumerate(("L0_xcond", "L0_ffn", "L1_xcond", "L3_xcond")):
                act.dma_start(W[str(i)][:, :, :], a[n + "_W"].rearrange("j d e -> d j e")).then_inc(w_loaded, 16)
                act.dma_start(bqkv[:, i, :], a[n + "_bT"]).then_inc(w_loaded, 16)
                act.dma_start(bo[:, i, :], a[n + "_b"][3:4, :].broadcast_to([128, D])).then_inc(w_loaded, 16)

            def rstds(ln):
                act.wait_ge(ln_step, 2 + 9 * ln + 6)
                act.activation(lnw[:, 4, :], lnw[:, 3, :], ACT.Ln).then_inc(rsqrt_ready, 1)
                act.wait_ge(rsqrt_ready, 2 * ln + 1)
                act.activation(lnw[:, 5, :], lnw[:, 4, :], ACT.Exp, scale=-0.5).then_inc(rsqrt_ready, 1)
                act.wait_ge(norm_ready, 2 * ln + 2)

            def normalise(ln, k):
                wait_reuse(act, xt_in_psum, CHUNKS * ln + k)
                for j in range(TPC):
                    t = k * TPC + j
                    act.activation(xn[:, j, :], X[:, bass.ds(t, 1), :].rearrange("p o d -> p (o d)"),
                                   ACT.Identity, bias=nmr[:, bass.ds(t, 1)],
                                   scale=rstd[:, bass.ds(t, 1)]).then_inc(xn_ready, 1)

            def prepare(l, ln):
                rstds(ln)
                act.wait_ge(w_loaded, W_DMAS * 16)

                def step(k, turn, u, live):
                    if live(0):
                        normalise(ln, k)
                    if live(1):
                        c = k - 1
                        r = (u + 1) % 2
                        act.wait_ge(proj_ready, 4 * (CHUNKS * l + c) + 2)
                        act.activation(KT[:, bass.ds(c * CHUNK, CHUNK)], psP[r][:, :], ACT.Identity,
                                       bias=bqkv[:, l, 1:2]).then_inc(k_ready, 1)

                pipeline(act, CHUNKS, 2, 1, step)

            def attention(l):
                wb = units_before[l]
                passes = PASSES[l]

                def step(k, turn, u, live):
                    s = u % 2
                    if live(0):
                        act.wait_ge(shifted, wb + k + 1)
                        act.activation(Pr[s][:, :], Pr[s][:, :], ACT.Exp).then_inc(exp_ready, 1)
                    if live(1):
                        r = (s + 1) % 2
                        act.wait_ge(p_turned, wb + k)
                        wait_reuse(act, pv_ready, wb + k - 2)
                        act.activation(Pt[r][:, :], psP[r][:, :], ACT.Copy).then_inc(p_evac, 1)
                    if (u == 3 or (u == 1 and passes == 1)) and live(5):
                        m = turn * 2 + u // 2 - 2 if passes == 1 else turn - 1
                        o = (u // 2) % 2 if passes == 1 else 0
                        act.wait_ge(ot_ready, TILES * l + m + 1)
                        wait_reuse(act, y_ready, TILES * l + m - (1 if passes == 1 else 0))
                        act.activation(ots[o][:, :], psT[:, 0:128], ACT.Copy).then_inc(ot_evac, 1)

                pipeline(act, B * passes, 4, 5, step)

            def classes():
                act.wait_ge(q_ready, 2 * CHUNKS)
                for c in range(CHUNKS):
                    wait_reuse(act, sq_summed, c - 1)
                    act.activation(sq[c % 2][:, :], QT[:, CHUNK * c:CHUNK * c + CHUNK], ACT.Square).then_inc(squared, 1)
                act.wait_ge(sim_act, 1)
                act.activation(n2[1][:, :], n2[0][:, :], ACT.Ln).then_inc(sim_act, 1)
                act.wait_ge(sim_act, 2)
                act.activation(n2[2][:, :], n2[1][:, :], ACT.Exp, scale=-0.5).then_inc(sim_act, 1)

            prepare(0, 0)
            attention(0)
            prepare(1, 1)
            classes()
            attention(1)
            prepare(2, 2)
            attention(2)

            def mixture1():
                rstds(3)

                def step(k, turn, u, live):
                    normalise(3, k)

                pipeline(act, CHUNKS, 2, 0, step)
                act.wait_ge(route_step, ROUTE_STEPS)
                act.activation(rt[:, 2, :, :], rt[:, 0, :, :], ACT.Exp).then_inc(route_act, 1)

            def attention2():
                rstds(4)
                act.wait_ge(keep_ready, 7)
                act.activation(gauss, gauss, ACT.Exp, scale=-1.0 / DEV_POW).then_inc(gauss_ready, 1)

                def step(k, turn, u, live):
                    s, r = u, (u + 1) % 2
                    if live(0):
                        act.wait_ge(a_in_psum, k + 1)
                        act.activation(KT[:, bass.ds(k * CHUNK, CHUNK)], psP[s][:, :], ACT.Copy).then_inc(a_ready, 1)
                        normalise(4, k)
                    if live(1):
                        act.wait_ge(nmx_ready, k)
                        wait_reuse(act, rd2_ready, k - 2)
                        for t in range(TPC):
                            col = sc2[r][:, 128 * t:128 * t + 128]
                            act.activation(col, col, ACT.Exp, bias=nmx[r][:, t:t + 1],
                                           accum_out=den[r][:, 0, t:t + 1]).then_inc(e2_ready, 1)
                        act.wait_ge(at_turned, k)
                        wait_reuse(act, cx_in_psum, k - 2)
                        act.activation(at2[r][:, :], psO[1][:, :], ACT.Copy).then_inc(at_ready, 1)
                        act.wait_ge(cx_turned, k)
                        wait_reuse(act, c_in_psum, k - 2)
                        act.activation(cxT[r][:, :], psO[1][:, :], ACT.Copy).then_inc(cxT_ready, 1)
                        act.wait_ge(c_in_psum, k)
                        wait_reuse(act, x_updated, TILES * 4 + TPC * (k - 2))
                        act.activation(th[r][:, :], psO[0][:, :], ACT.Tanh).then_inc(th_ready, 1)

                pipeline(act, CHUNKS, 2, 1, step)

            mixture1()
            def mixture(m):
                ln, F, tiles, before = MOE[m]
                rstds(ln)

                def step(k, turn, u, live):
                    wait_reuse(act, xn_kept, CHUNKS * m + k)
                    normalise(ln, k)

                pipeline(act, CHUNKS, 2, 0, step)
                if m == 0:
                    act.wait_ge(route_step, ROUTE_STEPS * 2)
                    act.activation(gate[:, 1, :], gate[:, 0, :], ACT.Exp, scale=-1.0).then_inc(score_act, 1)

                def expert_step(k, turn, u, live):
                    s = u % 2
                    if live(1):
                        r = (s + 1) % 2
                        act.wait_ge(e_hidden, before + k)
                        if m == 0:
                            wait_reuse(act, e_h, before + k - 2)
                            act.activation(act2[r][:, 0:F], psS[r][:, 0:F], ACT.Silu).then_inc(e_act, 1)
                        else:
                            wait_reuse(act, e_hturned, before + k - 2)
                            act.activation(hb[r][:, 0:F], psS[r][:, 0:F], ACT.Relu).then_inc(e_h, 1)
                    if live(3):
                        act.wait_ge(e_out, before + k - 2)
                        us = (u + 1) % 4
                        wait_reuse(act, tile_stored[us], 4 * before + 16 * (turn - (1 if us else 0)) )
                        act.activation(ys[us], psO[(s + 1) % 2][:, 0:128], ACT.Copy).then_inc(e_y, 1)

                pipeline(act, tiles, 4, 3, expert_step)

            attention2()
            mixture(0)
            prepare(3, 6)
            attention(3)
            mixture(1)

        @block.tensor
        def _(pe):
            pe.wait_ge(w_loaded, W_DMAS * 16)
            for l in range(4):
                mm = pe.matmul(psY[:, D * l:D * l + D], bqkv[:, l, 2:3].broadcast_to([128, 128]), W[str(l)][:, 3, :],
                               start=True, stop=True)
            mm.then_inc(bias_through, 1)

            def prepare(l, ln, cross):
                w = W[str(l)]
                pe.wait_ge(bo_ready, 1)
                pe.wait_ge(w_loaded, W_DMAS * 16)
                pe.wait_ge(cst_loaded, CST_DMAS * 16)
                pe.wait_ge(consts_ready, CONSTS)
                if cross:
                    pe.wait_ge(ctx_loaded, 64)

                def step(k, turn, u, live):
                    s = u % 2
                    if live(0):
                        pe.wait_ge(xn_ready, TPC * (CHUNKS * ln + k + 1))
                        wait_reuse(pe, xt_ready, CHUNKS * ln + k - 1)
                        for j in range(TPC):
                            mm = pe.transpose((psT, psY)[s][:, 128 * j:128 * j + 128], xn[:, j, :], ident)
                        mm.then_inc(xt_in_psum, 1)
                    if live(1):
                        c = k - 1
                        r = (s + 1) % 2
                        pe.wait_ge(xt_ready, CHUNKS * ln + k)
                        wait_reuse(pe, q_ready, CHUNKS * l + k - 2)
                        wait_reuse(pe, k_ready, CHUNKS * l + k - 2)
                        src = ctxT[:, bass.ds(c * CHUNK, CHUNK)] if cross else xts[r][:, :]
                        pe.matmul(psS[r][:, :], w[:, 0, :], xts[r][:, :], start=True, stop=True).then_inc(proj_ready, 1)
                        pe.matmul(psP[r][:, :], w[:, 1, :], src, start=True, stop=True).then_inc(proj_ready, 1)
                        wait_reuse(pe, v_ready, 2 * (CHUNKS * l + c))
                        pe.wait_ge(doubled, CHUNKS * l + k)
                        for h in range(2):
                            for j in range(4):
                                mm = pe.matmul(psO[h][:, 128 * j:128 * j + 128],
                                               xd[r][:, 4 * h + j, :, :].rearrange("p j s -> p (j s)"),
                                               w[:, 2, :], start=True, stop=True)
                            mm.then_inc(proj_ready, 1)

                pipeline(pe, CHUNKS, 2, 1, step)

            def attention(l, add):
                wb = units_before[l]
                passes = PASSES[l]
                w = W[str(l)]
                pe.wait_ge(v_ready, 2 * CHUNKS * (l + 1))

                def step(k, turn, u, live):
                    s = u % 2
                    if live(0):
                        pe.wait_ge(staged, 2 * (wb + k + 1))
                        if passes == 2:
                            pe.wait_ge(class_staged, k + 1)
                        wait_reuse(pe, shifted, wb + k - 1)
                        pe.matmul(psS[s][:, :], qbd[s][:, :], kbd[s][:, :], start=True, stop=False)
                        rows, left = (3, onesr) if passes == 1 else (2, addL[s])
                        row = add[0:rows, bass.ds(unit(turn, u, passes) * S, S)]
                        pe.matmul(psS[s][:, :].rearrange("p (g k) -> p g k", g=G), left[:, :],
                                  row.unsqueeze(1).broadcast_to([rows, G, S]),
                                  start=False, stop=True).then_inc(scores_ready, 1)
                    if live(1):
                        r = (s + 1) % 2
                        pe.wait_ge(exp_ready, wb + k)
                        wait_reuse(pe, p_evac, wb + k - 2)
                        for g in range(4):
                            mm = pe.transpose(psP[r][:, 128 * g:128 * g + 128], Pr[r][:, 128 * g:128 * g + 128], ident)
                        mm.then_inc(p_turned, 1)
                    if live(2):
                        r = s
                        pe.wait_ge(p_evac, wb + k - 1)
                        us = (u + 2) % 4
                        batch = unit(turn, u + 2, passes) - (4 if passes == 1 else 2)
                        vb = VB[:, bass.ds(batch, 1), :].rearrange("p o c -> p (o c)")
                        if us % 2 == 0:
                            wait_reuse(pe, on_ready, wb + k - 4)
                        o = psO[us // 2]
                        c0 = (us % 2) * G * VW
                        for g in range(4):
                            mm = pe.matmul(o[:, c0 + 2 * VW * g:c0 + 2 * VW * (g + 1)],
                                           Pt[r][:, 128 * g:128 * g + 128],
                                           vb[:, 2 * VW * g:2 * VW * (g + 1)], start=True, stop=True)
                        mm.then_inc(pv_ready, 1)
                    if (u == 3 or (u == 1 and passes == 1)) and live(5):
                        m = turn * 2 + u // 2 - 2 if passes == 1 else turn - 1
                        folds = [(on[(u // 2) % 2], fold2)] if passes == 1 else [(on[p], foldp[p]) for p in range(2)]
                        pe.wait_ge(on_ready, wb + k - 3)
                        wait_reuse(pe, ot_evac, TILES * l + m)
                        for b in range(2):
                            for n, (o, fold) in enumerate(folds):
                                mm = pe.matmul(psT[:, 64 * b:64 * b + 64], o[:, b, :], fold,
                                               start=(n == 0), stop=(n == passes - 1))
                        mm.then_inc(ot_ready, 1)
                    if (u == 0 or (u == 2 and passes == 1)) and live(6):
                        m = turn * 2 + u // 2 - 3 if passes == 1 else turn - 2
                        o = (u // 2 + 1) % 2 if passes == 1 else 0
                        pe.wait_ge(ot_evac, TILES * l + m + 1)
                        wait_reuse(pe, x_updated, TILES * UPD_OF[l] + m)
                        pe.matmul(psY[:, 0:128], ots[o][:, :], w[:, 3, :],
                                  start=True, stop=True).then_inc(y_ready, 1)

                pipeline(pe, B * passes, 4, 5, step)

            def turn_x(ln, k, u):
                pe.wait_ge(xn_ready, TPC * (CHUNKS * ln + k + 1))
                wait_reuse(pe, xt_ready, CHUNKS * ln + k - 1)
                for j in range(TPC):
                    mm = pe.transpose((psT, psY)[u][:, 128 * j:128 * j + 128], xn[:, j, :], ident)
                mm.then_inc(xt_in_psum, 1)

            def ranks(r):
                pe.wait_ge(route_step, ROUTE_STEPS * r + 5)
                cols = oh[:, :, :].rearrange("p e t -> p (e t)")
                pe.matmul(psO[0][:, 0:256], ones128[:, :], cols, start=True, stop=True).then_inc(rank_ready, 1)
                pe.matmul(psO[1][:, 0:256], upto, cols, start=True, stop=True).then_inc(rank_ready, 1)

            def mixture1():
                pe.wait_ge(w1f_loaded, 48)

                def step(k, turn, u, live):
                    if live(0):
                        turn_x(3, k, u)
                    if live(1):
                        r = (u + 1) % 2
                        pe.wait_ge(xt_ready, CHUNKS * 3 + k)
                        wait_reuse(pe, y_kept, k - 2)
                        for j in range(TPC):
                            pe.matmul(psO[r][:, NE * j:NE * j + NE], xts[r][:, 128 * j:128 * j + 128], w1f[:, 0:NE],
                                      start=True, stop=True)
                        for j in range(TPC):
                            mm = pe.matmul(psS[r][:, 128 * j:128 * j + 128], xts[r][:, 128 * j:128 * j + 128],
                                           w1f[:, NE:NE + D], start=True, stop=True)
                        mm.then_inc(route_pe, 1)

                pipeline(pe, CHUNKS, 2, 1, step)
                ranks(0)

            def attention2():
                pe.wait_ge(l2_loaded, 80)
                pe.wait_ge(ctx2_loaded, 16)

                def step(k, turn, u, live):
                    s, r = u, (u + 1) % 2
                    if live(0):
                        wait_reuse(pe, a_ready, k - 1)
                        pe.matmul(psP[s][:, :], wa[:, 0, :], ctxT[:, bass.ds(k * CHUNK, CHUNK)], start=True, stop=True).then_inc(a_in_psum, 1)
                        turn_x(4, k, u)
                    if live(1):
                        c = k - 1
                        pe.wait_ge(xt_ready, CHUNKS * 4 + k)
                        pe.wait_ge(a_ready, k)
                        wait_reuse(pe, capped, k - 2)
                        for j in range(TPC):
                            mm = pe.matmul(psS[r][:, 128 * j:128 * j + 128], xts[r][:, 128 * j:128 * j + 128],
                                           KT[:, bass.ds(c * CHUNK + 128 * j, 128)], start=True, stop=True)
                        mm.then_inc(s2_ready, 1)
                        pe.wait_ge(g2_ready, k)
                        wait_reuse(pe, cxT_ready, k - 1)
                        for j in range(TPC):
                            mm = pe.transpose(psO[1][:, 128 * j:128 * j + 128], sc2[r][:, 128 * j:128 * j + 128], ident)
                        mm.then_inc(at_turned, 1)
                        pe.wait_ge(at_ready, k)
                        wait_reuse(pe, th_ready, k - 1)
                        for j in range(TPC):
                            mm = pe.matmul(psO[0][:, 128 * j:128 * j + 128], at2[r][:, 128 * j:128 * j + 128],
                                           QT[:, bass.ds(c * CHUNK + 128 * j, 128)], start=True, stop=True)
                        mm.then_inc(cx_in_psum, 1)
                        pe.wait_ge(cx_ready, k)
                        for j in range(TPC):
                            mm = pe.transpose(psO[1][:, 128 * j:128 * j + 128], cx[r][:, 128 * j:128 * j + 128], ident)
                        mm.then_inc(cx_turned, 1)
                        pe.wait_ge(cxT_ready, k)
                        for j in range(TPC):
                            pe.matmul(psO[0][:, 128 * j:128 * j + 128], cxT[r][:, 128 * j:128 * j + 128], wa[:, 1, :],
                                      start=True, stop=False)
                            mm = pe.matmul(psO[0][:, 128 * j:128 * j + 128], xts[r][:, 128 * j:128 * j + 128], wa[:, 2, :],
                                           start=False, stop=True)
                        mm.then_inc(c_in_psum, 1)

                pipeline(pe, CHUNKS, 2, 1, step)

            def mixture(m):
                ln, F, tiles, before = MOE[m]
                pe.wait_ge(mw_loaded, 48)

                def step(k, turn, u, live):
                    if live(0):
                        turn_x(ln, k, u)
                    if live(1):
                        r = (u + 1) % 2
                        pe.wait_ge(xt_ready, CHUNKS * ln + k)
                        wait_reuse(pe, logit_ready, CHUNKS * (m + 1) + k - 2)
                        for j in range(TPC):
                            mm = pe.matmul(psO[r][:, NE * j:NE * j + NE], xts[r][:, 128 * j:128 * j + 128], rw[:, m, :],
                                           start=True, stop=True)
                        mm.then_inc(route_pe, 1)

                pipeline(pe, CHUNKS, 2, 1, step)
                ranks(m + 1)
                pe.wait_ge(experts_loaded, 16 * (6 if m == 0 else 10))
                pe.wait_ge(place_step, PLACE_STEPS[m + 1])
                if m == 1:
                    pe.wait_ge(b_rows, 96)
                w_out_at = (NE + 1) * 512 if m == 0 else NE * 512

                def expert_step(k, turn, u, live):
                    s = u % 2
                    if live(0):
                        pe.wait_ge(tile_loaded[u], 4 * before + 16 * (turn + 1))
                        wait_reuse(pe, e_xT, before + k)
                        pe.transpose(psT[:, 0:128], xl[u], ident).then_inc(e_turned, 1)
                    if live(1):
                        r = (s + 1) % 2
                        e = pe.value_load(slot_e[0:1, bass.ds(k - 1, 1)], min_val=0, max_val=NE if m == 0 else NE - 1)
                        pe.wait_ge(e_xT, before + k)
                        wait_reuse(pe, e_h, before + k - 2)
                        mm = pe.matmul(psS[r][:, :], xT[r], wv[:, bass.ds(e * 512, 512)], start=True, stop=(m == 0))
                        if m == 1:
                            mm = pe.matmul(psS[r][:, :], onesr[:, :], b1r[:, bass.ds(e * 512, 512)], start=False, stop=True)
                        mm.then_inc(e_hidden, 1)
                    if live(2):
                        pe.wait_ge(e_h, before + k - 1)
                        wait_reuse(pe, e_hT, before + k - 3)
                        for j in range(F // 128):
                            mm = pe.transpose(psP[s][:, 128 * j:128 * j + 128], hb[s][:, 128 * j:128 * j + 128], ident)
                        mm.then_inc(e_hturned, 1)
                    if live(3):
                        r = (s + 1) % 2
                        e = pe.value_load(slot_e[0:1, bass.ds(k - 3, 1)], min_val=0, max_val=NE if m == 0 else NE - 1)
                        pe.wait_ge(e_hT, before + k - 2)
                        wait_reuse(pe, e_y, before + k - 4)
                        for j in range(F // 128):
                            mm = pe.matmul(psO[r][:, 0:128], hT[r][:, 128 * j:128 * j + 128],
                                           wv[:, bass.ds(e * F + (w_out_at + 128 * j), 128)], start=(j == 0),
                                           stop=(m == 0 and j == F // 128 - 1))
                        if m == 1:
                            mm = pe.matmul(psO[r][:, 0:128], onesr[:, :], b2r[:, bass.ds(e * D, D)], start=False, stop=True)
                        mm.then_inc(e_out, 1)

                pipeline(pe, tiles, 4, 3, expert_step)

            def classes():
                pe.wait_ge(sim_step, 2)
                pe.wait_ge(k_ready, 2 * CHUNKS)
                pe.matmul(psY[:, 0:1], heads_rep, gcol[:, 1:2], start=True, stop=True).then_inc(sim_pe, 1)
                pe.wait_ge(q_ready, 2 * CHUNKS)
                for c in range(CHUNKS):
                    mm = pe.matmul(psS[1][:, :], guide_pad[:, 112 - H * c:240 - H * c], QT[:, CHUNK * c:CHUNK * c + CHUNK],
                                   start=(c == 0), stop=(c == CHUNKS - 1))
                mm.then_inc(sim_pe, 1)
                for c in range(CHUNKS):
                    pe.wait_ge(squared, c + 1)
                    mm = pe.matmul(psS[0][:, :], heads_pad[:, 112 - H * c:240 - H * c], sq[c % 2][:, :],
                                   start=(c == 0), stop=(c == CHUNKS - 1)).then_inc(sq_summed, 1)
                pe.wait_ge(sq_summed, CHUNKS)
                pe.sem_inc(sim_pe, 1)
                pe.wait_ge(sim_step, 4)
                pe.matmul(psP[0][0:CHUNKS, :], mean_h, n2[4][:, :], start=True, stop=True).then_inc(sim_pe, 1)
                pe.wait_ge(cls_rows, 64)
                pe.wait_ge(sim_step, 8)

            prepare(0, 0, True)
            pe.wait_ge(rows_moved, 48)
            attention(0, addR)
            prepare(1, 1, False)
            classes()
            attention(1, maskR)
            prepare(2, 2, True)
            attention(2, addR)
            mixture1()
            attention2()
            mixture(0)
            prepare(3, 6, True)
            pe.wait_ge(ones_again, 1)
            attention(3, addR)
            mixture(1)


LAYERS = ("L0_xcond", "L1_xcond", "L3_xcond")


def kernel(**inputs):
    import concourse.bacc as bacc
    from concourse.bass_utils import run_bass_kernel_spmd

    i = {k: np.asarray(v) for k, v in inputs.items()}
    arrays = {"x": i["x"], "ctxT": np.ascontiguousarray(i["ctx_1024"].reshape(TOK, D).T),
              "condB_tau": i["condB_tau"], "fside_BxS2_0": i["fside_BxS2_0"]}
    for n in LAYERS:
        arrays[n + "_W"] = np.stack([np.ascontiguousarray(i[f"{n}_W{c}"].T) for c in "qkvo"])
        arrays[n + "_b"] = np.stack([i[f"{n}_b{c}"] for c in "qkvo"])
    qkv = i["L0_ffn_W_qkv"]
    arrays["L0_ffn_W"] = np.stack([qkv[:, 0:D], qkv[:, D:2 * D], qkv[:, 2 * D:3 * D], i["L0_ffn_W_proj"]])
    zero = np.zeros(D, np.float32)
    arrays["g_first"] = np.ascontiguousarray(i["L0_ffn_g_info"][0, 0].reshape(D, 1))
    arrays["cst"] = constants()
    arrays["L0_ffn_b"] = np.stack([zero, zero, zero, i["L0_ffn_b_proj"]])

    arrays["ctx_1024"] = i["ctx_1024"]
    arrays["L1_ffn_Wg"], arrays["L1_ffn_We"], arrays["L1_ffn_be"] = i["L1_ffn_Wg"], i["L1_ffn_We"], i["L1_ffn_be"].reshape(1, D)
    wc = i["L2_xcond_W_c"].T
    arrays["L2_W"] = np.stack([np.ascontiguousarray(i["L2_xcond_W_a"].T), wc[0:D], wc[D:2 * D]])
    arrays["pt2"] = np.ascontiguousarray(i["condB_pt"].reshape(TILES, 2).T)
    arrays["len2"] = np.ascontiguousarray(i["_lenS2"].reshape(TILES, 2).T)
    for n in ("gate_w", "sh_gate", "sh_up", "sh_down", "rt_gate", "rt_up", "rt_down"):
        arrays["L2_ffn_" + n] = i["L2_ffn_" + n]
    arrays["L3_ffn_WrT"] = np.ascontiguousarray(i["L3_ffn_Wr"].T)
    arrays["L3_ffn_br"] = i["L3_ffn_br"].reshape(1, NE)
    arrays["L3_ffn_W1T"] = np.ascontiguousarray(i["L3_ffn_W1"].transpose(0, 2, 1))
    arrays["L3_ffn_W2T"] = np.ascontiguousarray(i["L3_ffn_W2"].transpose(0, 2, 1))
    arrays["L3_ffn_b1"] = i["L3_ffn_b1"].reshape(64, 64)
    arrays["L3_ffn_b2"] = i["L3_ffn_b2"].reshape(64, 16)
    for n in LAYERS + ("L0_ffn",):
        arrays[n + "_bT"] = np.ascontiguousarray(arrays[n + "_b"].T)

    nc = bacc.Bacc("TRN2", target_bir_lowering=False, num_devices=1)
    handles = {k: nc.dram_tensor(k + "_in", v.shape, mybir.dt.from_np(v.dtype), kind="ExternalInput").ap()
               for k, v in arrays.items()}
    out = nc.dram_tensor("out", (B, S, D), F32, kind="ExternalOutput").ap()
    build(nc, handles, out)
    r = run_bass_kernel_spmd(nc, [{k + "_in": np.ascontiguousarray(v) for k, v in arrays.items()}], core_ids=[0])
    return r.results[0]["out"]
```

```python
from contextlib import ExitStack

import numpy as np

import concourse.bass as bass
from concourse import mybir
from concourse.alu_op_type import AluOpType as ALU

ACT = mybir.ActivationFunctionType
AX = mybir.AxisListType
F32 = mybir.dt.float32
BF16 = mybir.dt.bfloat16
I32 = mybir.dt.int32
U32 = mybir.dt.uint32

B, S, D = 64, 64, 128
H, E = 16, 8
G = H // 2
TOK = B * S
TILES = TOK // 128
CHUNK = 512
CHUNKS = TOK // CHUNK
TPC = CHUNK // 128
BPC = CHUNK // S
REG = 5
EPS = 1e-5
VW = E * 2 + 1
NE = 8
CAP = TOK // NE
WINDOW, DEV_POW = 16.0, 128.0
BIG = float(2 ** 60)


SLOTS = -(-(TOK // 128 + 8 - 1) // 4) * 4
CST_COLS = 332 + 128 + G + 240 + 128 + 8 + 256 + 256 + 128 + 128 + 128 + SLOTS + 128 + REG


def constants():
    p = np.arange(128)
    head, pair = p // E, p // (2 * E)
    fold = (p[:, None] % S == np.arange(S)[None, :]).astype(np.float32)
    is_reg = (np.arange(S) < REG)[None, :]
    cst = np.concatenate([
        np.eye(128), fold, fold * np.where(is_reg, 0.5, 1.0), np.zeros((128, 64)),
        head[:, None] % 2 == np.arange(2)[None, :], pair[:, None] % 2 == np.arange(2)[None, :],
        pair[:, None] == np.arange(G)[None, :],
        p[:, None] // S == pair[None, :] % 2, p[:, None] // S == np.arange(G)[None, :] % 2,
        np.zeros((128, 112)), head[:, None] == np.arange(H)[None, :], np.zeros((128, 112)),
        head[:, None] == p[None, :] % H, (p[:, None] // H == np.arange(CHUNKS)[None, :]) / H,
        np.repeat(NE - np.arange(NE), TILES)[None, :] + 0 * p[:, None],
        np.tile(np.arange(TILES) > 0, NE)[None, :] + 0 * p[:, None],
        p[:, None] <= p[None, :],
        np.where(p[:, None] // S == p[None, :] // S, p[None, :] % S, 10 ** 6),
        np.where(p[:, None] // S == p[None, :] // S, -1e9, -1e30),
        np.arange(SLOTS)[None, :] + 0 * p[:, None],
        p[:, None] // REG == head[None, :], 0.5 * (p[:, None] % REG == np.arange(REG)[None, :]),
    ], axis=1).astype(np.float32)
    return cst


def wait_reuse(eng, semaphore, value):
    if not isinstance(value, int) or value > 0:
        eng.wait_ge(semaphore, value)


def pipeline(eng, count, period, lag, step):
    first = -(-max(lag + 1, period) // period)
    for k in range(first * period):
        step(k, k // period, k % period, lambda l, k=k: k - l >= 0)
    with eng.Fori(first, count // period) as turn:
        for u in range(period):
            step(turn * period + u, turn, u, lambda l: True)
    for k in range(count, count + lag):
        step(k, k // period, k % period, lambda l, k=k: k - l < count)


def build(nc, a, out):
    ctx = ExitStack()
    with ctx:
        def sb(name, shape, dt=F32):
            return ctx.enter_context(nc.sbuf_tensor(name, shape, dt))

        def pb(name):
            return ctx.enter_context(nc.psum_tensor(name, [128, 512], F32))

        def sem(name):
            return ctx.enter_context(nc.semaphore(name))

        X = sb("X", [128, TILES, D])
        ctxT = sb("ctxT", [128, TOK])
        QT = sb("QT", [128, TOK])
        KT = sb("KT", [128, TOK])
        VB = sb("VB", [128, B, G * VW])
        xd = [sb(f"xd{i}", [128, BPC, 2, S]) for i in range(2)]
        cst = sb("cst", [128, CST_COLS])
        ident = cst[:, 0:128]
        fold2 = cst[:, 128:192]
        fold_self = cst[:, 192:256]
        hp_mask = cst[:, 320:322]
        g2_mask = cst[:, 322:324]
        g_mask = cst[:, 324:332]
        v_mask = cst[:, 332:460]
        v_ones = cst[:, 460:468]
        heads_pad = cst[:, 468:708]
        heads_rep = cst[:, 708:836]
        mean_h = cst[:, 836:844]
        first_w = cst[:, 844:1100]
        not_first = cst[:, 1100:1356]
        upto = cst[:, 1356:1484]
        own_idx = cst[:, 1484:1612]
        far = cst[:, 1612:1740]
        slot_no = cst[:, 1740:1740 + SLOTS]
        own_head = cst[0:H * REG, 1740 + SLOTS:1868 + SLOTS]
        fold_reg = cst[0:H * REG, 1868 + SLOTS:1868 + SLOTS + REG]
        gcol = sb("gcol", [128, 2])
        guide_pad = sb("guide_pad", [128, 240])
        n2g = sb("n2g", [128, 1])
        ext = sb("ext", [CHUNKS, 6])
        clsb = sb("clsb", [CHUNKS, 3, CHUNK], BF16)
        neg_class = sb("neg_class", [2, H * REG], BF16)
        reg_den = [sb(f"reg_den{i}", [128, 2, 4]) for i in range(2)]
        reg_out = sb("reg_out", [128, B, REG])
        onesr = sb("onesr", [3, 128], BF16)
        ones_row = sb("ones_row", [1, 128])
        stats = sb("stats", [128, TILES, 6])
        lnw = sb("lnw", [128, 6, TILES])
        rstd = sb("rstd", [128, TILES])
        nmr = sb("nmr", [128, TILES])
        xn = sb("xn", [128, TPC, D])
        xts = [sb(f"xts{i}", [128, CHUNK]) for i in range(2)]
        tau_b = sb("tau_b", [128, B])
        tau_s = sb("tau_s", [128, B])
        dl = sb("dl", [64, 3, 64])
        dlb = sb("dlb", [64, 3, 64], BF16)
        rows_sb = sb("rows_sb", [65, TOK], BF16)
        addR = rows_sb[0:3, :]
        clsrow = rows_sb[32:33, :]
        maskR = sb("maskR", [3, TOK], BF16)
        W = {}
        for n in ("0", "1", "2", "3"):
            W[n] = sb(f"W{n}", [128, 4, 128])
        bqkv = sb("bqkv", [128, 4, 4])
        bo = sb("bo", [128, 4, D])
        qbd = [sb(f"qbd{i}", [128, 128]) for i in range(2)]
        kbd = [sb(f"kbd{i}", [128, 512]) for i in range(2)]
        addL = [sb(f"addL{i}", [2, 128], BF16) for i in range(2)]
        mx = [sb(f"mx{i}", [128, G]) for i in range(2)]
        Pr = [sb(f"Pr{i}", [128, 512]) for i in range(2)]
        Pt = [sb(f"Pt{i}", [128, 512]) for i in range(2)]
        rden = sb("rden", [128, 2 * G])
        on = [sb(f"on{i}", [128, 2, H * E]) for i in range(2)]
        ots = [sb(f"ots{i}", [128, 128]) for i in range(2)]

        th = [sb(f"th{i}", [128, CHUNK]) for i in range(2)]
        n2 = [kbd[0], kbd[1], Pt[0], Pt[1], Pr[0]]
        sq = [Pr[1], th[1]]
        simr = th[0][0:CHUNKS, :]
        logit = sb("logit", [128, NE, TILES])
        oh = sb("oh", [128, NE, TILES])
        rt = sb("rt", [128, 4, NE, TILES])
        gate = sb("gate", [128, 4, TILES])
        ones128 = sb("ones128", [128, 128])
        w1f = sb("w1f", [128, NE + D])
        be = sb("be", [128, D])
        Yt = QT
        wa = sb("wa", [128, 3, 128])
        win = sb("win", [128, 8, TILES])
        leni = sb("leni", [128, TILES], I32)
        keep = VB[:, :, :].rearrange("p b c -> p (b c)")[:, 0:TOK]
        gauss = VB[:, :, :].rearrange("p b c -> p (b c)")[:, TOK:2 * TOK]
        sc2 = [sb(f"sc2{i}", [128, CHUNK]) for i in range(2)]
        nmx = [sb(f"nmx{i}", [128, TPC]) for i in range(2)]
        den = [sb(f"den{i}", [128, 2, TPC]) for i in range(2)]
        at2 = [kbd[i] for i in range(2)]
        cx = [Pr[i] for i in range(2)]
        cxT = [Pt[i] for i in range(2)]
        rw = sb("rw", [128, 2, NE])
        rb = sb("rb", [128, NE])
        dest = sb("dest", [128, TILES], U32)
        ei = sb("ei", [128, 2, NE], I32)
        ef = sb("ef", [128, 3, NE])
        slots = sb("slots", [128, SLOTS, NE])
        slotf = sb("slotf", [128, SLOTS])
        slot_e = sb("slot_e", [128, SLOTS], I32)
        wv = VB[:, :, :].rearrange("p b c -> p (b c)")
        xl, ys = th, xts
        xT = [Pr[i][:, 0:128] for i in range(2)]
        sh_h = [kbd, Pt]
        hb, hT, act2 = kbd, Pt, sc2
        b1r = maskR[0:3, :]
        b2r = sb("b2r", [3, NE * D], BF16)
        b2l = sb("b2l", [64, 3, 16])
        b2b = sb("b2b", [64, 3, 16], BF16)
        xs_dram = nc.dram_tensor("xs_dram", [SLOTS * 128, D], F32).ap()
        ys_dram = nc.dram_tensor("ys_dram", [SLOTS * 128, D], F32).ap()

        psS = [pb("psS0"), pb("psS1")]
        psP = [pb("psP0"), pb("psP1")]
        psO = [pb("psO0"), pb("psO1")]
        psT = pb("psT")
        psY = pb("psY")

        x_loaded = sem("x_loaded")
        ctx_loaded = sem("ctx_loaded")
        w_loaded = sem("w_loaded")
        side_loaded = sem("side_loaded")
        rows_moved = sem("rows_moved")
        consts_ready = sem("consts_ready")
        cst_loaded = sem("cst_loaded")
        CST_DMAS, CONSTS, W_DMAS = 1, 10, 12
        ROUTE_STEPS = 9
        setup_step = sem("setup_step")
        delta_split = sem("delta_split")
        stats_ready = sem("stats_ready")
        ln_step = sem("ln_step")
        rsqrt_ready = sem("rsqrt_ready")
        norm_ready = sem("norm_ready")
        xn_ready = sem("xn_ready")
        xt_in_psum = sem("xt_in_psum")
        xt_ready = sem("xt_ready")
        proj_ready = sem("proj_ready")
        q_ready = sem("q_ready")
        k_ready = sem("k_ready")
        v_ready = sem("v_ready")
        doubled = sem("doubled")
        class_staged = sem("class_staged")
        staged = sem("staged")
        bo_added = sem("bo_added")
        bias_through = sem("bias_through")
        bo_ready = sem("bo_ready")
        v_turned = sem("v_turned")
        scores_ready = sem("scores_ready")
        max_ready = sem("max_ready")
        shifted = sem("shifted")
        exp_ready = sem("exp_ready")
        p_turned = sem("p_turned")
        p_evac = sem("p_evac")
        v_evac = sem("v_evac")
        pv_ready = sem("pv_ready")
        rden_ready = sem("rden_ready")
        on_ready = sem("on_ready")
        ot_ready = sem("ot_ready")
        ot_evac = sem("ot_evac")
        y_ready = sem("y_ready")
        x_updated = sem("x_updated")
        slot_free = sem("slot_free")
        stored = sem("stored")
        w1f_loaded = sem("w1f_loaded")
        route_pe = sem("route_pe")
        logit_ready = sem("logit_ready")
        y_kept = sem("y_kept")
        route_step = sem("route_step")
        route_act = sem("route_act")
        rank_ready = sem("rank_ready")
        l2_loaded = sem("l2_loaded")
        win_step = sem("win_step")
        keep_ready = sem("keep_ready")
        ctx2_loaded = sem("ctx2_loaded")
        a_in_psum = sem("a_in_psum")
        a_ready = sem("a_ready")
        s2_ready = sem("s2_ready")
        capped = sem("capped")
        nmx_ready = sem("nmx_ready")
        e2_ready = sem("e2_ready")
        g2_ready = sem("g2_ready")
        rd2_ready = sem("rd2_ready")
        at_turned = sem("at_turned")
        at_ready = sem("at_ready")
        cx_in_psum = sem("cx_in_psum")
        cx_ready = sem("cx_ready")
        cx_turned = sem("cx_turned")
        cxT_ready = sem("cxT_ready")
        c_in_psum = sem("c_in_psum")
        th_ready = sem("th_ready")
        mw_loaded = sem("mw_loaded")
        zero_ready = sem("zero_ready")
        zeroed = sem("zeroed")
        xn_kept = sem("xn_kept")
        place_step = sem("place_step")
        score_act = sem("score_act")
        scattered = sem("scattered")
        experts_loaded = sem("experts_loaded")
        tiles_loaded = [sem(f"tiles_loaded{i}") for i in range(2)]
        tiles_stored = [sem(f"tiles_stored{i}") for i in range(2)]
        scored = sem("scored")
        rows_scaled = sem("rows_scaled")
        xT_kept = sem("xT_kept")
        sh_gate = sem("sh_gate")
        sh_up = sem("sh_up")
        sh_act = sem("sh_act")
        sh_hid = sem("sh_hid")
        sh_out = sem("sh_out")
        sh_added = sem("sh_added")
        e_turned = sem("e_turned")
        e_xT = sem("e_xT")
        e_hidden = sem("e_hidden")
        e_act = sem("e_act")
        e_h = sem("e_h")
        e_hturned = sem("e_hturned")
        e_hT = sem("e_hT")
        e_out = sem("e_out")
        e_y = sem("e_y")
        gathered = sem("gathered")
        b_split = sem("b_split")
        b_rows = sem("b_rows")
        b_loaded = sem("b_loaded")
        ones_again = sem("ones_again")
        routed_added = sem("routed_added")
        PLACE_STEPS = [0, 12, 24]
        gauss_ready = sem("gauss_ready")
        g_loaded = sem("g_loaded")
        sim_step = sem("sim_step")
        sim_pe = sem("sim_pe")
        sim_act = sem("sim_act")
        sim_pool = sem("sim_pool")
        squared = sem("squared")
        sq_summed = sem("sq_summed")
        sim_newton = sem("sim_newton")
        cls_rows = sem("cls_rows")
        reg_staged = sem("reg_staged")
        reg_scores = sem("reg_scores")
        reg_max = sem("reg_max")
        reg_shifted = sem("reg_shifted")
        reg_exp = sem("reg_exp")
        reg_summed = sem("reg_summed")
        reg_rden = sem("reg_rden")
        reg_probs = sem("reg_probs")
        reg_turned = sem("reg_turned")
        reg_evac = sem("reg_evac")
        reg_pv = sem("reg_pv")
        reg_masked = sem("reg_masked")
        reg_folded = sem("reg_folded")
        reg_kept = sem("reg_kept")

        REG_STEPS = B // 4
        LN_OF = [0, 1, 2, 6]
        UPD_OF = [0, 1, 2, 6]
        units_before = [B * l for l in range(5)]

        MOE = [(5, 256, SLOTS, 0), (7, 512, SLOTS, SLOTS)]

        def rows_of(dram, tile, n=1):
            return dram[bass.ds(tile * 128, 128 * n), :]

        def by_batch(row):
            return row.rearrange("c (b s) -> c b s", s=S)

        block = ctx.enter_context(nc.Block())

        @block.sync
        def _(sp):
            sp.dma_start(cst[:, :], a["cst"]).then_inc(cst_loaded, 16)
            xv = a["x"].rearrange("b s d -> (b s) d").rearrange("(t p) d -> p t d", p=128)
            for q in range(4):
                sp.dma_start(X[:, 8 * q:8 * q + 8, :], xv[:, 8 * q:8 * q + 8, :]).then_inc(x_loaded, 16)
            for q in range(4):
                sp.dma_start(ctxT[:, 1024 * q:1024 * q + 1024],
                             a["ctxT"][:, 1024 * q:1024 * q + 1024]).then_inc(ctx_loaded, 16)
            sp.dma_start(w1f[:, 0:NE], a["L1_ffn_Wg"]).then_inc(w1f_loaded, 16)
            sp.dma_start(w1f[:, NE:NE + D], a["L1_ffn_We"]).then_inc(w1f_loaded, 16)
            sp.dma_start(be[:, :], a["L1_ffn_be"].broadcast_to([128, D])).then_inc(w1f_loaded, 16)
            sp.dma_start(wa[:, :, :], a["L2_W"].rearrange("j d e -> d j e")).then_inc(l2_loaded, 16)
            for h in range(2):
                sp.dma_start(win[64 * h:64 * h + 64, 0, :], a["pt2"][h:h + 1, :].broadcast_to([64, TILES])).then_inc(l2_loaded, 16)
                sp.dma_start(leni[64 * h:64 * h + 64, :], a["len2"][h:h + 1, :].broadcast_to([64, TILES])).then_inc(l2_loaded, 16)
            sp.dma_start(rw[:, 0, :], a["L2_ffn_gate_w"]).then_inc(mw_loaded, 16)
            sp.dma_start(rw[:, 1, :], a["L3_ffn_WrT"]).then_inc(mw_loaded, 16)
            sp.dma_start(rb[:, :], a["L3_ffn_br"].broadcast_to([128, NE])).then_inc(mw_loaded, 16)
            sp.wait_ge(zero_ready, 1)
            sp.dma_start(xs_dram.rearrange("(t p) d -> p t d", p=128),
                         th[0][:, 0:128].unsqueeze(1).broadcast_to([128, SLOTS, 128])).then_inc(zeroed, 16)
            sp.wait_ge(delta_split, 5)
            for j in range(3):
                sp.dma_start(addR[j:j + 1, :].rearrange("o (b k) -> o b k", b=B), dlb[:, j, :]).then_inc(rows_moved, 16)
            sp.wait_ge(rows_moved, 48)
            sp.dma_start(dl[:, 1, :], a["L3_ffn_b1"]).then_inc(b_loaded, 16)
            sp.dma_start(b2l[:, 1, :], a["L3_ffn_b2"]).then_inc(b_loaded, 16)
            sp.wait_ge(sim_step, 10)
            sp.wait_ge(sim_pool, 4)
            for dst, j in ((maskR[0:1, :], 0), (maskR[1:2, :], 1), (clsrow, 2)):
                sp.dma_start(dst.rearrange("o (c k) -> o c k", c=CHUNKS), clsb[:, j, :]).then_inc(cls_rows, 16)
            sp.wait_ge(x_updated, TILES * 4)
            sp.dma_start(QT[:, :].rearrange("p (t d) -> p t d", d=D),
                         a["ctx_1024"].rearrange("b s d -> (b s) d").rearrange("(t p) d -> p t d", p=128)).then_inc(ctx2_loaded, 16)
            def mixture(m):
                ln, F, tiles, before = MOE[m]
                if m == 0:
                    sp.wait_ge(g2_ready, CHUNKS)
                    w_in = wv[:, 0:(NE + 1) * 512]
                    w_out = wv[:, (NE + 1) * 512:(NE + 1) * 768]
                    for j, n in enumerate(("rt_gate", "rt_up")):
                        sp.dma_start(w_in[:, 0:NE * 512].rearrange("p (e j f) -> p e j f", e=NE, j=2)[:, :, j, :],
                                     a["L2_ffn_" + n].rearrange("e p f -> p e f")).then_inc(experts_loaded, 16)
                    for j, n in enumerate(("sh_gate", "sh_up")):
                        sp.dma_start(w_in[:, NE * 512 + 256 * j:NE * 512 + 256 * j + 256], a["L2_ffn_" + n]).then_inc(experts_loaded, 16)
                    sp.dma_start(w_out[:, 0:NE * 256].rearrange("p (e j d) -> p e j d", e=NE, j=2),
                                 a["L2_ffn_rt_down"].rearrange("e (j p) d -> p e j d", p=128)).then_inc(experts_loaded, 16)
                    sp.dma_start(w_out[:, NE * 256:(NE + 1) * 256].rearrange("p (j d) -> p j d", j=2),
                                 a["L2_ffn_sh_down"].rearrange("(j p) d -> p j d", p=128)).then_inc(experts_loaded, 16)
                else:
                    sp.wait_ge(b_split, 10)
                    for j in range(3):
                        sp.dma_start(b1r[j:j + 1, :].rearrange("o (b k) -> o b k", b=64), dlb[:, j, :]).then_inc(b_rows, 16)
                        sp.dma_start(b2r[j:j + 1, :].rearrange("o (b k) -> o b k", b=64), b2b[:, j, :]).then_inc(b_rows, 16)
                    sp.wait_ge(pv_ready, units_before[4])
                    for h in range(2):
                        e = slice(4 * h, 4 * h + 4)
                        sp.dma_start(wv[:, 2048 * h:2048 * h + 2048].rearrange("p (e f) -> p e f", e=4),
                                     a["L3_ffn_W1T"][e].rearrange("e p f -> p e f")).then_inc(experts_loaded, 16)
                        sp.dma_start(wv[:, 4096 + 2048 * h:6144 + 2048 * h].rearrange("p (e j d) -> p e j d", e=4, j=4),
                                     a["L3_ffn_W2T"][e].rearrange("e (j p) d -> p e j d", p=128)).then_inc(experts_loaded, 16)
                sp.wait_ge(scattered, 16 * TILES * (m + 1))

                def groups(dram, k):
                    return dram[bass.ds(k * 512, 512), :].rearrange("(t p) d -> p t d", p=128)

                def step(k, turn, u, live):
                    if live(0):
                        wait_reuse(sp, e_turned, (before + 4 * k - 4) if not isinstance(k, int) or k > 1 else 0)
                        sp.dma_start(xl[u][:, :].rearrange("p (t d) -> p t d", d=D), groups(xs_dram, k)).then_inc(tiles_loaded[u], 16)
                    if live(2):
                        sp.wait_ge(e_y, before + 4 * k - 4)
                        sp.dma_start(groups(ys_dram, k - 2), ys[u][:, :].rearrange("p (t d) -> p t d", d=D)).then_inc(tiles_stored[u], 16)

                pipeline(sp, tiles // 4, 2, 2, step)

            mixture(0)
            mixture(1)
            ov = out.rearrange("b s d -> (b s) d").rearrange("(t p) d -> p t d", p=128)
            for q in range(4):
                sp.wait_ge(x_updated, TILES * 7 + 8 * q + 8)
                sp.dma_start(ov[:, 8 * q:8 * q + 8, :], X[:, 8 * q:8 * q + 8, :]).then_inc(stored, 16)
            sp.wait_ge(stored, 64)

        @block.gpsimd
        def _(pool):
            for i in range(2):
                pool.memset(on[i][:, :, :], 0.0).then_inc(consts_ready, 1)
            pool.memset(onesr[:, :], 1.0).then_inc(consts_ready, 1)
            pool.memset(ones_row[:, :], 1.0).then_inc(consts_ready, 1)
            pool.memset(ones128[:, :], 1.0).then_inc(consts_ready, 1)
            pool.memset(th[0][:, 0:128], 0.0).then_inc(zero_ready, 1)
            pool.wait_ge(cst_loaded, CST_DMAS * 16)
            pool.tensor_copy(VB[:, :, :].rearrange("p b (g w) -> p b g w", w=VW)[:, :, :, VW - 1],
                             v_ones.unsqueeze(1).broadcast_to([128, B, G])).then_inc(consts_ready, 1)

            def attention(l):
                wb = units_before[l]

                def step(k, turn, u, live):
                    s = u % 2
                    at = k * S
                    wait_reuse(pool, scores_ready, wb + k - 1)
                    pool.sem_inc(slot_free, 1)
                    pool.tensor_tensor(
                        kbd[s][:, :].rearrange("p (g k) -> p g k", g=G),
                        KT[:, bass.ds(at, S)].unsqueeze(1).broadcast_to([128, G, S]),
                        g_mask[:, :].unsqueeze(2).broadcast_to([128, G, S]), ALU.mult).then_inc(staged, 1)
                    pool.tensor_tensor(
                        qbd[s][:, :].rearrange("p (g k) -> p g k", g=2),
                        QT[:, bass.ds(at, S)].unsqueeze(1).broadcast_to([128, 2, S]),
                        hp_mask[:, :].unsqueeze(2).broadcast_to([128, 2, S]), ALU.mult).then_inc(staged, 1)
                    if u % 2 == 1:
                        t = turn * 2 + u // 2
                        pool.tensor_tensor(X[:, bass.ds(t, 1), :].rearrange("p o d -> p (o d)"),
                                           X[:, bass.ds(t, 1), :].rearrange("p o d -> p (o d)"),
                                           bo[:, l, :], ALU.add).then_inc(bo_added, 1)

                pool.wait_ge(w_loaded, W_DMAS * 16)
                pool.wait_ge(q_ready, CHUNKS * (l + 1))
                pool.wait_ge(bo_ready, 1)
                pool.wait_ge(k_ready, CHUNKS * (l + 1))
                pipeline(pool, B, 4, 0, step)

            def prepare(l, ln, cross):
                def step(k, turn, u, live):
                    wait_reuse(pool, proj_ready, 4 * (CHUNKS * l + k - 1))
                    if cross:
                        src = ctxT[:, bass.ds(k * CHUNK, CHUNK)]
                    else:
                        pool.wait_ge(xt_ready, CHUNKS * ln + k + 1)
                        src = xts[u][:, :]
                    pool.sem_inc(slot_free, 1)
                    pool.tensor_copy(xd[u][:, :, :, :], src.rearrange("p (b s) -> p b s", b=BPC).unsqueeze(2)
                                     .broadcast_to([128, BPC, 2, S])).then_inc(doubled, 1)

                if cross:
                    pool.wait_ge(ctx_loaded, 64)
                pipeline(pool, CHUNKS, 2, 0, step)

            for i in range(2):
                pool.memset(addL[i][:, :], 1.0).then_inc(consts_ready, 1)
            pool.memset(neg_class[:, :], 1.0).then_inc(consts_ready, 1)
            pool.wait_ge(consts_ready, CONSTS - 1)
            pool.memset(neg_class[0:1, :], -1.0).then_inc(consts_ready, 1)

            def classes():
                pool.wait_ge(q_ready, 2 * CHUNKS)
                pool.memset(clsb[:, 1, :], -BIG).then_inc(sim_pool, 1)
                pool.wait_ge(sim_pool, 1)
                pool.memset(by_batch(clsb[:, 1, :])[:, :, 0:REG], 0.0).then_inc(sim_pool, 1)
                pool.wait_ge(sim_step, 6)
                pool.partition_all_reduce(ext[:, 2:4], ext[:, 0:2], CHUNKS, bass.bass_isa.ReduceOp.max).then_inc(sim_pool, 2)

            def registers():
                def step(k, turn, u, live):
                    s, r = u, (u + 1) % 2
                    if live(0):
                        wait_reuse(pool, reg_scores, k - 1)
                        pool.sem_inc(slot_free, 1)
                        pool.tensor_tensor(
                            kbd[s][:, 0:4 * H * REG].rearrange("p (b h q) -> p b h q", b=4, h=H),
                            QT[:, bass.ds(k * 4 * S, 4 * S)].rearrange("p (b s) -> p b s", b=4)[:, :, 0:REG]
                            .unsqueeze(2).broadcast_to([128, 4, H, REG]),
                            heads_pad[:, 112:128].unsqueeze(1).unsqueeze(3).broadcast_to([128, 4, H, REG]),
                            ALU.mult).then_inc(reg_staged, 1)
                    if live(1):
                        wait_reuse(pool, reg_turned, k - 2)
                        pool.wait_ge(reg_rden, k)
                        pool.sem_inc(slot_free, 1)
                        pool.tensor_tensor(
                            th[r][0:H * REG, :].rearrange("p (b j s) -> p b j s", b=4, j=2),
                            Pr[r][0:H * REG, 0:4 * S].rearrange("p (b s) -> p b s", b=4).unsqueeze(2)
                            .broadcast_to([H * REG, 4, 2, S]),
                            reg_den[r][0:H * REG, 1, :].unsqueeze(2).unsqueeze(3).broadcast_to([H * REG, 4, 2, S]),
                            ALU.mult).then_inc(reg_probs, 1)

                pool.wait_ge(sim_step, 10)
                pipeline(pool, REG_STEPS, 2, 1, step)
                pool.wait_ge(reg_scores, REG_STEPS)
                pool.wait_ge(cls_rows, 48)

            prepare(0, 0, True)
            attention(0)
            prepare(1, 1, False)
            classes()
            registers()
            attention(1)
            prepare(2, 2, True)
            attention(2)

            pool.wait_ge(keep_ready, 2)
            tiles = [128, TILES, 128]
            idx = own_idx.unsqueeze(1).broadcast_to(tiles)
            k3 = keep.rearrange("p (t l) -> p t l", l=128)
            g3 = gauss.rearrange("p (t l) -> p t l", l=128)
            per = lambda j: win[:, j, :].unsqueeze(2).broadcast_to(tiles)
            pool.tensor_tensor(k3, k3, g3, ALU.mult).then_inc(keep_ready, 1)
            pool.wait_ge(keep_ready, 3)
            pool.tensor_scalar(k3, k3, 3e38, None, ALU.mult).then_inc(keep_ready, 1)
            pool.tensor_tensor(g3, idx, per(0), ALU.subtract).then_inc(keep_ready, 1)
            pool.wait_ge(keep_ready, 5)
            pool.tensor_tensor(k3, k3, far.unsqueeze(1).broadcast_to(tiles), ALU.add).then_inc(keep_ready, 1)
            pool.tensor_tensor(g3, g3, g3, ALU.mult).then_inc(keep_ready, 1)

            def mixture(m):
                ln, F, tiles, before = MOE[m]
                if m == 0:
                    pool.wait_ge(cx_in_psum, CHUNKS)

                def step(k, turn, u, live):
                    pool.wait_ge(xn_ready, TPC * (CHUNKS * ln + k + 1))
                    pool.sem_inc(slot_free, 1)
                    pool.tensor_copy(QT[:, bass.ds(k * CHUNK, CHUNK)], xn[:, :, :].rearrange("p t d -> p (t d)")).then_inc(xn_kept, 1)

                pipeline(pool, CHUNKS, 2, 0, step)
                pool.wait_ge(xn_kept, CHUNKS * (m + 1))
                pool.wait_ge(zeroed, 16)
                if m == 0:
                    pool.wait_ge(scored, 2)
                    rows = QT[:, :].rearrange("p (t d) -> p t d", d=D)
                    pool.tensor_tensor(rows, rows, gate[:, 3, :].unsqueeze(2).broadcast_to([128, TILES, D]),
                                       ALU.mult).then_inc(rows_scaled, 1)
                    pool.wait_ge(rows_scaled, 1)
                pool.wait_ge(place_step, PLACE_STEPS[m + 1])
                for t in range(TILES):
                    pool.indirect_dma_start(xs_dram[:, :], bass.IndirectOffsetOnAxis(dest[:, t:t + 1], 0),
                                            QT[:, D * t:D * t + D], None).then_inc(scattered, 16)
                for i in range(2):
                    pool.wait_ge(tiles_stored[i], 16 * (tiles // 8) * (m + 1))
                pool.wait_ge(scattered, 16 * TILES * (m + 1))
                for t in range(TILES):
                    pool.indirect_dma_start(QT[:, D * t:D * t + D], None, ys_dram[:, :],
                                            bass.IndirectOffsetOnAxis(dest[:, t:t + 1], 0)).then_inc(gathered, 16)

            mixture(0)
            pool.wait_ge(e_hidden, MOE[0][2])
            pool.wait_ge(e_out, MOE[0][2])
            pool.tensor_copy(VB[:, :, :].rearrange("p b (g w) -> p b g w", w=VW)[:, :, :, VW - 1],
                             v_ones.unsqueeze(1).broadcast_to([128, B, G])).then_inc(ones_again, 1)
            prepare(3, 6, True)
            attention(3)
            mixture(1)



        @block.vector
        def _(v):
            v.wait_ge(side_loaded, 32)
            v.tensor_scalar(tau_s[:, :], tau_b[:, :], float(E) ** -0.5, None, ALU.mult).then_inc(ln_step, 1)
            v.tensor_scalar(dl[:, 1, :], dl[:, 0, :], float(E) ** -0.5, None, ALU.mult).then_inc(ln_step, 1)
            v.wait_ge(ln_step, 2)

            def split3(x, parts, counter, n):
                v.tensor_copy(parts[:, 0, :], x[:, 1, :]).then_inc(counter, 1)
                v.wait_ge(counter, n + 1)
                v.tensor_tensor(x[:, 2, :], x[:, 1, :], parts[:, 0, :], ALU.subtract).then_inc(counter, 1)
                v.wait_ge(counter, n + 2)
                v.tensor_copy(parts[:, 1, :], x[:, 2, :]).then_inc(counter, 1)
                v.wait_ge(counter, n + 3)
                v.tensor_tensor(x[:, 1, :], x[:, 2, :], parts[:, 1, :], ALU.subtract).then_inc(counter, 1)
                v.wait_ge(counter, n + 4)
                v.tensor_copy(parts[:, 2, :], x[:, 1, :]).then_inc(counter, 1)

            split3(dl, dlb, delta_split, 0)
            n_ln = 2
            v.wait_ge(w_loaded, W_DMAS * 16)
            v.wait_ge(bias_through, 1)
            v.tensor_tensor(bo[:, :, :].rearrange("p l d -> p (l d)"), psY[:, :],
                            bo[:, :, :].rearrange("p l d -> p (l d)"), ALU.add).then_inc(bo_ready, 1)

            def norms(l):
                nonlocal n_ln
                if l == 0:
                    v.wait_ge(x_loaded, 64)
                else:
                    v.wait_ge(x_updated, TILES * l)

                with v.Fori(0, TILES // 4) as t:
                    for u in range(4):
                        v.bn_stats(stats[:, bass.ds(t * 4 + u, 1), :].rearrange("p o c -> p (o c)"),
                                   X[:, bass.ds(t * 4 + u, 1), :].rearrange("p o d -> p (o d)")).then_inc(stats_ready, 1)
                v.wait_ge(stats_ready, TILES * (l + 1))
                me, mo, se, so = stats[:, :, 1], stats[:, :, 4], stats[:, :, 2], stats[:, :, 5]
                n = n_ln
                v.tensor_tensor(lnw[:, 0, :], me, mo, ALU.add).then_inc(ln_step, 1)
                v.tensor_tensor(lnw[:, 1, :], me, mo, ALU.subtract).then_inc(ln_step, 1)
                v.tensor_tensor(lnw[:, 2, :], se, so, ALU.add).then_inc(ln_step, 1)
                v.wait_ge(ln_step, n + 3)
                v.tensor_tensor(lnw[:, 1, :], lnw[:, 1, :], lnw[:, 1, :], ALU.mult).then_inc(ln_step, 1)
                v.tensor_scalar(lnw[:, 2, :], lnw[:, 2, :], 1.0 / D, EPS, ALU.mult, ALU.add).then_inc(ln_step, 1)
                v.wait_ge(ln_step, n + 5)
                v.scalar_tensor_tensor(lnw[:, 3, :], lnw[:, 1, :], 0.25, lnw[:, 2, :], ALU.mult, ALU.add).then_inc(ln_step, 1)
                v.wait_ge(ln_step, n + 6)
                v.wait_ge(rsqrt_ready, 2 * l + 2)
                y, t = lnw[:, 5, :], lnw[:, 1, :]
                v.tensor_tensor(t, y, y, ALU.mult).then_inc(ln_step, 1)
                v.wait_ge(ln_step, n + 7)
                v.tensor_tensor(t, t, lnw[:, 3, :], ALU.mult).then_inc(ln_step, 1)
                v.wait_ge(ln_step, n + 8)
                v.tensor_scalar(t, t, -0.5, 1.5, ALU.mult, ALU.add).then_inc(ln_step, 1)
                v.wait_ge(ln_step, n + 9)
                v.tensor_tensor(rstd[:, :], t, y, ALU.mult).then_inc(norm_ready, 1)
                v.wait_ge(norm_ready, 2 * l + 1)
                v.scalar_tensor_tensor(nmr[:, :], lnw[:, 0, :], -0.5, rstd[:, :], ALU.mult, ALU.mult).then_inc(norm_ready, 1)
                n_ln = n + 9

            def prepare(l, ln, tau):
                norms(ln)

                def step(k, turn, u, live):
                    s = u % 2
                    if live(0):
                        v.wait_ge(xt_in_psum, CHUNKS * ln + k + 1)
                        v.tensor_copy(xts[s][:, :], (psT, psY)[s][:, :]).then_inc(xt_ready, 1)
                    if live(1):
                        c = k - 1
                        r = (s + 1) % 2
                        v.wait_ge(proj_ready, 4 * (CHUNKS * l + c) + 1)
                        if tau is None:
                            v.tensor_scalar(QT[:, bass.ds(c * CHUNK, CHUNK)], psS[r][:, :], bqkv[:, l, 0:1],
                                            float(E) ** -0.5, ALU.add, ALU.mult).then_inc(q_ready, 1)
                        else:
                          v.scalar_tensor_tensor(
                            QT[:, bass.ds(c * CHUNK, CHUNK)].rearrange("p (b s) -> p b s", b=BPC),
                            psS[r][:, :].rearrange("p (b s) -> p b s", b=BPC), bqkv[:, l, 0:1],
                            tau_s[:, bass.ds(c * BPC, BPC)].unsqueeze(2).broadcast_to([128, BPC, S]),
                            ALU.add, ALU.mult).then_inc(q_ready, 1)
                        for h in range(2):
                            v.wait_ge(proj_ready, 4 * (CHUNKS * l + c) + 3 + h)
                            v.tensor_tensor(
                                VB[:, bass.ds(c * BPC + 4 * h, 4), :].rearrange("p b (g w) -> p b g w", w=VW)[:, :, :, 0:2 * E],
                                psO[h][:, :].rearrange("p (b g w) -> p b g w", b=4, w=2 * E),
                                v_mask.rearrange("p (g w) -> p g w", w=2 * E).unsqueeze(1).broadcast_to([128, 4, G, 2 * E]),
                                ALU.mult).then_inc(v_ready, 1)

                v.wait_ge(w_loaded, W_DMAS * 16)
                pipeline(v, CHUNKS, 2, 1, step)

            def attention(l):
                wb = units_before[l]
                masked = l == 1
                behind = 1 if masked else 0

                def step(k, turn, u, live):
                    if masked and live(0):
                        wait_reuse(v, scores_ready, wb + k - 1)
                        v.tensor_copy(addL[u % 2][0:1, :].rearrange("o (j s) -> o j s", j=2),
                                      clsrow[:, bass.ds(k * S, S)]
                                      .unsqueeze(1).broadcast_to([1, 2, S])).then_inc(class_staged, 1)
                    if live(behind):
                        s = (u - behind) % 2
                        n = wb + k - behind
                        sc = psS[s][:, :].rearrange("p (g k) -> p g k", g=G)
                        v.wait_ge(scores_ready, n + 1)
                        v.tensor_reduce(mx[s][:, :], sc, AX.X, ALU.max).then_inc(max_ready, 1)
                        wait_reuse(v, p_turned, n - 1)
                        v.wait_ge(max_ready, n + 1)
                        v.tensor_tensor(Pr[s][:, :].rearrange("p (g k) -> p g k", g=G), sc,
                                        mx[s][:, :].unsqueeze(2).broadcast_to([128, G, S]),
                                        ALU.subtract).then_inc(shifted, 1)
                    if u % 2 == 0 and live(4):
                        m2 = k - 4
                        m = turn * 2 + u // 2 - 2
                        ps = (u // 2) % 2
                        v.wait_ge(pv_ready, wb + m2 + 2)
                        oo = psO[ps][:, 0:2 * G * VW].rearrange("p (g w) -> p g w", w=VW)
                        wait_reuse(v, on_ready, wb + m2)
                        v.reciprocal(rden[:, :].unsqueeze(2), oo[:, :, VW - 1:VW]).then_inc(rden_ready, 1)
                        v.wait_ge(rden_ready, wb // 2 + m + 1)
                        wait_reuse(v, ot_ready, TILES * l + m - 1)
                        dst = on[ps][:, :, :].rearrange("p b (g w) -> p (b g) w", w=2 * E)
                        for hp in range(2):
                            r = slice(64 * hp, 64 * hp + 64)
                            v.tensor_tensor(dst[r, :, E * hp:E * hp + E], oo[r, :, E * hp:E * hp + E],
                                            rden[r, :].unsqueeze(2).broadcast_to([64, 2 * G, E]),
                                            ALU.mult).then_inc(on_ready, 1)
                    if u % 2 == 1 and live(7):
                        t = turn * 2 + u // 2 - 3
                        v.wait_ge(y_ready, TILES * l + t + 1)
                        v.wait_ge(bo_added, TILES * l + t + 1)
                        xt = X[:, bass.ds(t, 1), :].rearrange("p o d -> p (o d)")
                        v.tensor_tensor(xt, psY[:, 0:128], xt, ALU.add).then_inc(x_updated, 1)

                pipeline(v, B, 4, 6, step)

            def classes():
                v.wait_ge(g_loaded, 16)
                v.wait_ge(cst_loaded, 16 * CST_DMAS)
                v.tensor_scalar(guide_pad[:, :], heads_pad, gcol[:, 0:1], None, ALU.mult).then_inc(sim_step, 1)
                v.tensor_tensor(gcol[:, 1:2], gcol[:, 0:1], gcol[:, 0:1], ALU.mult).then_inc(sim_step, 1)
                v.wait_ge(sim_pe, 1)
                v.tensor_copy(n2g[:, :], psY[:, 0:1]).then_inc(sim_step, 1)
                v.wait_ge(sim_step, 3)
                v.wait_ge(sim_pe, 3)
                v.tensor_scalar(n2[0][:, :], psS[0][:, :], n2g[:, 0:1], None, ALU.mult).then_inc(sim_act, 1)
                v.wait_ge(sim_act, 3)
                y, t = n2[2][:, :], n2[3][:, :]
                v.tensor_tensor(t, y, y, ALU.mult).then_inc(sim_newton, 1)
                v.wait_ge(sim_newton, 1)
                v.tensor_tensor(t, t, n2[0][:, :], ALU.mult).then_inc(sim_newton, 1)
                v.wait_ge(sim_newton, 2)
                v.tensor_scalar(t, t, -0.5, 1.5, ALU.mult, ALU.add).then_inc(sim_newton, 1)
                v.wait_ge(sim_newton, 3)
                v.tensor_tensor(t, t, y, ALU.mult).then_inc(sim_newton, 1)
                v.wait_ge(sim_newton, 4)
                v.tensor_tensor(n2[4][:, :], psS[1][:, :], t, ALU.mult).then_inc(sim_step, 1)
                v.wait_ge(sim_pe, 4)
                sim = by_batch(psP[0][0:CHUNKS, :])[:, :, REG:S]
                v.tensor_reduce(ext[:, 0:1], sim, AX.XY, ALU.max).then_inc(sim_step, 1)
                v.tensor_reduce(ext[:, 1:2], sim, AX.XY, ALU.min, negate=True).then_inc(sim_step, 1)
                v.wait_ge(sim_pool, 4)
                v.tensor_scalar(ext[:, 4:5], ext[:, 2:3], ext[:, 3:4], 0.9, ALU.add, ALU.mult).then_inc(sim_step, 1)
                v.wait_ge(sim_step, 7)
                v.tensor_scalar(simr, psP[0][0:CHUNKS, :], ext[:, 3:4], ext[:, 4:5], ALU.add, ALU.is_gt).then_inc(sim_step, 1)
                v.wait_ge(sim_step, 8)
                v.tensor_scalar(clsb[:, 0, :], simr, 2.0 * BIG, -BIG, ALU.mult, ALU.add).then_inc(sim_newton, 1)
                v.tensor_scalar(clsb[:, 2, :], simr, 2.0, -1.0, ALU.mult, ALU.add).then_inc(sim_newton, 1)
                v.wait_ge(sim_newton, 6)
                for j, c in ((0, 0.0), (2, 1.0)):
                    v.memset(by_batch(clsb[:, j, :])[:, :, 0:REG], c).then_inc(sim_step, 1)

            def registers():
                rows = slice(0, H * REG)

                def step(k, turn, u, live):
                    s, r = u, (u + 1) % 2
                    if live(0):
                        sc = psS[s][rows, 0:4 * S].rearrange("p (b s) -> p b s", b=4)
                        v.wait_ge(reg_scores, k + 1)
                        wait_reuse(v, reg_shifted, k - 1)
                        v.tensor_reduce(mx[s][rows, 0:4], sc, AX.X, ALU.max).then_inc(reg_max, 1)
                        wait_reuse(v, reg_probs, k - 1)
                        v.wait_ge(reg_max, k + 1)
                        v.tensor_tensor(Pr[s][rows, 0:4 * S].rearrange("p (b s) -> p b s", b=4), sc,
                                        mx[s][rows, 0:4].unsqueeze(2).broadcast_to([H * REG, 4, S]),
                                        ALU.subtract).then_inc(reg_shifted, 1)
                    if live(1):
                        v.wait_ge(reg_exp, k)
                        v.tensor_reduce(reg_den[r][rows, 0, :], Pr[r][rows, 0:4 * S].rearrange("p (b s) -> p b s", b=4),
                                        AX.X, ALU.add).then_inc(reg_summed, 1)
                        wait_reuse(v, reg_probs, k - 2)
                        v.wait_ge(reg_summed, k)
                        v.reciprocal(reg_den[r][rows, 1, :], reg_den[r][rows, 0, :]).then_inc(reg_rden, 1)
                    if live(3):
                        v.wait_ge(reg_pv, k - 2)
                        wait_reuse(v, reg_folded, k - 4)
                        v.tensor_tensor(sc2[r][rows, :].rearrange("p (b c) -> p b c", b=4),
                                        psO[r][rows, :].rearrange("p (b c) -> p b c", b=4),
                                        own_head.unsqueeze(1).broadcast_to([H * REG, 4, 128]), ALU.mult).then_inc(reg_masked, 1)
                    if live(4):
                        v.wait_ge(reg_folded, k - 3)
                        v.tensor_copy(reg_out[:, bass.ds((k - 4) * 4, 4), :].rearrange("p b q -> p (b q)"),
                                      (psT, psY)[s][:, 0:4 * REG]).then_inc(reg_kept, 1)

                pipeline(v, REG_STEPS, 2, 4, step)
                v.wait_ge(cls_rows, 48)

            prepare(0, 0, tau_s)
            attention(0)
            prepare(1, 1, None)
            classes()
            registers()
            attention(1)
            prepare(2, 2, tau_s)
            attention(2)

            def xt_evac(ln, k, u):
                v.wait_ge(xt_in_psum, CHUNKS * ln + k + 1)
                v.tensor_copy(xts[u][:, :], (psT, psY)[u][:, :]).then_inc(xt_ready, 1)

            def routing(r):
                n = ROUTE_STEPS * r
                by_tile = lambda x: x.rearrange("p e t -> p t e")
                best = lambda j: gate[:, j, :].unsqueeze(1).broadcast_to([128, NE, TILES])
                v.wait_ge(logit_ready, CHUNKS * (r + 1))
                v.tensor_reduce(gate[:, 0, :], by_tile(logit[:, :, :]), AX.X, ALU.max).then_inc(route_step, 1)
                v.wait_ge(route_step, n + 1)
                v.tensor_tensor(rt[:, 0, :, :], logit[:, :, :], best(0), ALU.subtract).then_inc(route_step, 1)
                v.wait_ge(route_step, n + 2)
                v.scalar_tensor_tensor(rt[:, 1, :, :], rt[:, 0, :, :], 0.0, first_w.rearrange("p (e t) -> p e t", e=NE),
                                       ALU.is_equal, ALU.mult).then_inc(route_step, 1)
                v.wait_ge(route_step, n + 3)
                v.tensor_reduce(gate[:, 1, :], by_tile(rt[:, 1, :, :]), AX.X, ALU.max).then_inc(route_step, 1)
                v.wait_ge(route_step, n + 4)
                v.tensor_tensor(oh[:, :, :], rt[:, 1, :, :], best(1), ALU.is_equal).then_inc(route_step, 1)
                if r == 1:
                    v.wait_ge(score_act, 1)
                    v.tensor_scalar(gate[:, 3, :], gate[:, 2, :], 1.0, None, ALU.add).then_inc(scored, 1)
                    v.wait_ge(scored, 1)
                    v.reciprocal(gate[:, 3, :], gate[:, 3, :]).then_inc(scored, 1)
                v.wait_ge(rank_ready, 2 * r + 2)
                v.tensor_copy(rt[:, 2, :, :], psO[0][:, 0:256].rearrange("p (e t) -> p e t", e=NE)).then_inc(route_step, 1)
                v.wait_ge(route_step, n + 6)
                flat = lambda j: rt[:, j, :, :].rearrange("p e t -> p (e t)")
                v.tensor_tensor_scan(flat(1), not_first, flat(2), 0.0, ALU.mult, ALU.add).then_inc(route_step, 1)
                v.wait_ge(route_step, n + 7)
                v.tensor_tensor(flat(3), flat(1), flat(2), ALU.subtract).then_inc(route_step, 1)
                v.wait_ge(route_step, n + 8)
                v.tensor_tensor(flat(3), flat(3), psO[1][:, 0:256], ALU.add).then_inc(route_step, 1)
                v.wait_ge(route_step, n + 9)

            def mixture1():
                norms(3)

                def step(k, turn, u, live):
                    if live(0):
                        xt_evac(3, k, u)
                    if live(1):
                        r = (u + 1) % 2
                        v.wait_ge(route_pe, k)
                        v.tensor_copy(logit[:, :, bass.ds((k - 1) * TPC, TPC)],
                                      psO[r][:, 0:NE * TPC].rearrange("p (t e) -> p e t", e=NE)).then_inc(logit_ready, 1)
                        v.tensor_tensor(Yt[:, bass.ds((k - 1) * CHUNK, CHUNK)].rearrange("p (t d) -> p t d", d=D),
                                        psS[r][:, :].rearrange("p (t d) -> p t d", d=D),
                                        be[:, :].unsqueeze(1).broadcast_to([128, TPC, D]), ALU.add).then_inc(y_kept, 1)

                pipeline(v, CHUNKS, 2, 1, step)
                routing(0)
                v.scalar_tensor_tensor(rt[:, 1, :, :], rt[:, 3, :, :], float(CAP), oh[:, :, :], ALU.is_le, ALU.mult).then_inc(win_step, 1)
                v.wait_ge(win_step, 5)
                v.tensor_reduce(gate[:, 1, :], rt[:, 1, :, :].rearrange("p e t -> p t e"), AX.X, ALU.add).then_inc(win_step, 1)
                v.wait_ge(route_act, 1)
                v.tensor_reduce(gate[:, 2, :], rt[:, 2, :, :].rearrange("p e t -> p t e"), AX.X, ALU.add).then_inc(win_step, 1)
                v.wait_ge(win_step, 7)
                v.reciprocal(gate[:, 3, :], gate[:, 2, :]).then_inc(win_step, 1)
                v.wait_ge(win_step, 8)
                v.tensor_tensor(gate[:, 1, :], gate[:, 1, :], gate[:, 3, :], ALU.mult).then_inc(win_step, 1)
                v.wait_ge(win_step, 9)
                v.wait_ge(y_kept, CHUNKS)
                with v.Fori(0, TILES // 4) as turn:
                    for u in range(4):
                        t = turn * 4 + u
                        row = lambda x: x[:, bass.ds(t * D, D)]
                        xt = X[:, bass.ds(t, 1), :].rearrange("p o d -> p (o d)")
                        v.scalar_tensor_tensor(xt, row(Yt), gate[:, 1, bass.ds(t, 1)], xt, ALU.mult, ALU.add).then_inc(x_updated, 1)

            def attention2():
                norms(4)

                def step(k, turn, u, live):
                    s, r = u, (u + 1) % 2
                    if live(0):
                        xt_evac(4, k, u)
                    if live(1):
                        c = k - 1
                        v.wait_ge(s2_ready, k)
                        wait_reuse(v, at_turned, k - 2)
                        v.tensor_tensor(sc2[r][:, :], psS[r][:, :], keep[:, bass.ds(c * CHUNK, CHUNK)], ALU.min).then_inc(capped, 1)
                        v.wait_ge(capped, k)
                        wait_reuse(v, e2_ready, TPC * (k - 2))
                        v.tensor_reduce(nmx[r][:, :], sc2[r][:, :].rearrange("p (t l) -> p t l", l=128), AX.X, ALU.max,
                                        negate=True).then_inc(nmx_ready, 1)
                        v.wait_ge(e2_ready, TPC * k)
                        v.tensor_tensor(sc2[r][:, :], sc2[r][:, :], gauss[:, bass.ds(c * CHUNK, CHUNK)], ALU.mult).then_inc(g2_ready, 1)
                        v.reciprocal(den[r][:, 1, :], den[r][:, 0, :]).then_inc(rd2_ready, 1)
                        v.wait_ge(rd2_ready, k)
                        v.wait_ge(cx_in_psum, k)
                        wait_reuse(v, cx_turned, k - 2)
                        v.tensor_tensor(cx[r][:, :].rearrange("p (t d) -> p t d", d=D),
                                        psO[0][:, :].rearrange("p (t d) -> p t d", d=D),
                                        den[r][:, 1, :].unsqueeze(2).broadcast_to([128, TPC, D]), ALU.mult).then_inc(cx_ready, 1)
                    if live(2):
                        c = k - 2
                        v.wait_ge(th_ready, k - 1)
                        xc = X[:, bass.ds(c * TPC, TPC), :].rearrange("p t d -> p (t d)")
                        v.tensor_tensor(xc, th[s][:, :], xc, ALU.add).then_inc(x_updated, TPC)

                v.wait_ge(keep_ready, 7)
                v.wait_ge(gauss_ready, 1)
                pipeline(v, CHUNKS, 2, 2, step)

            v.wait_ge(l2_loaded, 80)
            v.tensor_scalar(win[:, 2, :], win[:, 0, :], -WINDOW, 0.0, ALU.add, ALU.max).then_inc(win_step, 1)
            v.tensor_scalar(win[:, 4, :], win[:, 0, :], WINDOW, None, ALU.add).then_inc(win_step, 1)
            v.tensor_copy(win[:, 1, :], leni[:, :]).then_inc(win_step, 1)
            v.wait_ge(win_step, 3)
            v.tensor_tensor(win[:, 3, :], win[:, 4, :], win[:, 1, :], ALU.min).then_inc(win_step, 1)
            v.wait_ge(win_step, 4)
            v.wait_ge(pv_ready, units_before[3])
            for dst, j, cmp in ((keep, 2, ALU.is_ge), (gauss, 3, ALU.is_le)):
                v.tensor_tensor(dst.rearrange("p (t l) -> p t l", l=128),
                                own_idx.unsqueeze(1).broadcast_to([128, TILES, 128]),
                                win[:, j, :].unsqueeze(2).broadcast_to([128, TILES, 128]), cmp).then_inc(keep_ready, 1)
            mixture1()
            def mixture(m):
                ln, F, tiles, before = MOE[m]
                norms(ln)
                v.wait_ge(mw_loaded, 48)

                def step(k, turn, u, live):
                    if live(0):
                        if m == 0:
                            wait_reuse(v, xT_kept, k - 1)
                        xt_evac(ln, k, u)
                    if live(1):
                        r = (u + 1) % 2
                        if m == 0:
                            v.wait_ge(xt_ready, CHUNKS * ln + k)
                            v.tensor_copy(KT[:, bass.ds((k - 1) * CHUNK, CHUNK)], xts[r][:, :]).then_inc(xT_kept, 1)
                        v.wait_ge(route_pe, CHUNKS * (m + 1) + k)
                        src = psO[r][:, 0:NE * TPC].rearrange("p (t e) -> p e t", e=NE)
                        dst = logit[:, :, bass.ds((k - 1) * TPC, TPC)]
                        if m == 0:
                            v.tensor_copy(dst, src).then_inc(logit_ready, 1)
                        else:
                            v.tensor_tensor(dst, src, rb[:, :].unsqueeze(2).broadcast_to([128, NE, TPC]), ALU.add).then_inc(logit_ready, 1)

                pipeline(v, CHUNKS, 2, 1, step)
                routing(m + 1)
                n = PLACE_STEPS[m]

                def done(ins):
                    nonlocal n
                    ins.then_inc(place_step, 1)
                    n += 1

                done(v.tensor_scalar(ei[:, 0, :], rt[:, 1, :, TILES - 1], 127.0, None, ALU.add))
                v.wait_ge(place_step, n)
                done(v.tensor_scalar(ei[:, 1, :], ei[:, 0, :], 7, None, ALU.arith_shift_right))
                v.wait_ge(place_step, n)
                done(v.tensor_copy(ef[:, 0, :], ei[:, 1, :]))
                v.wait_ge(place_step, n)
                done(v.tensor_tensor_scan(ef[:, 1, :], ones128[:, 0:NE], ef[:, 0, :], 0.0, ALU.mult, ALU.add))
                v.wait_ge(place_step, n)
                done(v.tensor_tensor(slots[:, :, :], slot_no.unsqueeze(2).broadcast_to([128, SLOTS, NE]),
                                     ef[:, 1, :].unsqueeze(1).broadcast_to([128, SLOTS, NE]), ALU.is_ge))
                done(v.tensor_tensor(ef[:, 2, :], ef[:, 1, :], ef[:, 0, :], ALU.subtract))
                v.wait_ge(place_step, n)
                done(v.tensor_reduce(slotf[:, :], slots[:, :, :], AX.X, ALU.add))
                done(v.scalar_tensor_tensor(rt[:, 0, :, :], ef[:, 2, :].unsqueeze(2).broadcast_to([128, NE, TILES]), 128.0,
                                            rt[:, 3, :, :], ALU.mult, ALU.add))
                v.wait_ge(place_step, n)
                done(v.tensor_scalar(slot_e[:, :], slotf[:, :], float(NE - 1), None, ALU.min))
                done(v.scalar_tensor_tensor(rt[:, 1, :, :], rt[:, 0, :, :], -1.0, oh[:, :, :], ALU.add, ALU.mult))
                v.wait_ge(place_step, n)
                done(v.tensor_reduce(gate[:, 2, :], rt[:, 1, :, :].rearrange("p e t -> p t e"), AX.X, ALU.add))
                v.wait_ge(place_step, n)
                done(v.tensor_copy(dest[:, :], gate[:, 2, :]))
                assert n == PLACE_STEPS[m + 1], n

                def shared_step(k, turn, u, live):
                    if live(0):
                        for j in range(2):
                            v.wait_ge(sh_act, 2 * k + j + 1)
                            v.wait_ge(sh_up, 2 * k + j + 1)
                            wait_reuse(v, sh_out, k - 1)
                            v.tensor_tensor(sh_h[u][j][:, :], sc2[j][:, :], psP[j][:, :], ALU.mult).then_inc(sh_hid, 1)
                    if live(1):
                        v.wait_ge(sh_out, k)
                        xc = X[:, bass.ds((k - 1) * TPC, TPC), :].rearrange("p t d -> p (t d)")
                        v.tensor_tensor(xc, psO[(u + 1) % 2][:, :], xc, ALU.add).then_inc(sh_added, 1)

                if m == 0:
                    pipeline(v, CHUNKS, 2, 1, shared_step)

                def expert_step(k, turn, u, live):
                    s = u % 2
                    if live(0):
                        v.wait_ge(e_turned, before + k + 1)
                        wait_reuse(v, e_hidden, before + k - 1)
                        v.tensor_copy(xT[s], (psT, psY)[s][:, 0:128]).then_inc(e_xT, 1)
                    if live(1):
                        r = (s + 1) % 2
                        if m == 0:
                            v.wait_ge(e_act, before + k)
                            wait_reuse(v, e_hturned, before + k - 2)
                            v.tensor_tensor(hb[r][:, 0:F], act2[r][:, 0:F], psS[r][:, F:2 * F], ALU.mult).then_inc(e_h, 1)
                    if live(2):
                        v.wait_ge(e_hturned, before + k - 1)
                        wait_reuse(v, e_out, before + k - 3)
                        v.tensor_copy(hT[s][:, 0:F], psP[s][:, 0:F]).then_inc(e_hT, 1)

                pipeline(v, tiles, 8, 2, expert_step)
                if m == 0:
                    v.wait_ge(sh_added, CHUNKS)
                v.wait_ge(gathered, 16 * TILES * (m + 1))
                with v.Fori(0, TILES // 4) as turn:
                    xc = X[:, bass.ds(turn * 4, 4), :].rearrange("p t d -> p (t d)")
                    v.tensor_tensor(xc, QT[:, bass.ds(turn * 4 * D, 4 * D)], xc, ALU.add).then_inc(x_updated, 4)

            attention2()
            mixture(0)
            v.wait_ge(b_loaded, 32)
            split3(dl, dlb, b_split, 0)
            split3(b2l, b2b, b_split, 5)
            prepare(3, 6, tau_s)
            attention(3)
            mixture(1)

        @block.scalar
        def _(act):
            act.dma_start(tau_b[:, :], a["condB_tau"].rearrange("(o b) -> o b", o=1).broadcast_to([128, B])).then_inc(side_loaded, 16)
            act.dma_start(gcol[:, 0:1], a["g_first"]).then_inc(g_loaded, 16)
            act.dma_start(dl[:, 0, :], a["fside_BxS2_0"]).then_inc(side_loaded, 16)
            for i, n in enumerate(("L0_xcond", "L0_ffn", "L1_xcond", "L3_xcond")):
                act.dma_start(W[str(i)][:, :, :], a[n + "_W"].rearrange("j d e -> d j e")).then_inc(w_loaded, 16)
                act.dma_start(bqkv[:, i, :], a[n + "_bT"]).then_inc(w_loaded, 16)
                act.dma_start(bo[:, i, :], a[n + "_b"][3:4, :].broadcast_to([128, D])).then_inc(w_loaded, 16)

            def rstds(ln):
                act.wait_ge(ln_step, 2 + 9 * ln + 6)
                act.activation(lnw[:, 4, :], lnw[:, 3, :], ACT.Ln).then_inc(rsqrt_ready, 1)
                act.wait_ge(rsqrt_ready, 2 * ln + 1)
                act.activation(lnw[:, 5, :], lnw[:, 4, :], ACT.Exp, scale=-0.5).then_inc(rsqrt_ready, 1)
                act.wait_ge(norm_ready, 2 * ln + 2)

            def normalise(ln, k):
                wait_reuse(act, xt_in_psum, CHUNKS * ln + k)
                for j in range(TPC):
                    t = k * TPC + j
                    act.activation(xn[:, j, :], X[:, bass.ds(t, 1), :].rearrange("p o d -> p (o d)"),
                                   ACT.Identity, bias=nmr[:, bass.ds(t, 1)],
                                   scale=rstd[:, bass.ds(t, 1)]).then_inc(xn_ready, 1)

            def prepare(l, ln):
                rstds(ln)
                act.wait_ge(w_loaded, W_DMAS * 16)

                def step(k, turn, u, live):
                    if live(0):
                        normalise(ln, k)
                    if live(1):
                        c = k - 1
                        r = (u + 1) % 2
                        act.wait_ge(proj_ready, 4 * (CHUNKS * l + c) + 2)
                        act.activation(KT[:, bass.ds(c * CHUNK, CHUNK)], psP[r][:, :], ACT.Identity,
                                       bias=bqkv[:, l, 1:2]).then_inc(k_ready, 1)

                pipeline(act, CHUNKS, 2, 1, step)

            def attention(l):
                wb = units_before[l]

                def step(k, turn, u, live):
                    s = u % 2
                    if live(0):
                        act.wait_ge(shifted, wb + k + 1)
                        act.activation(Pr[s][:, :], Pr[s][:, :], ACT.Exp).then_inc(exp_ready, 1)
                    if live(1):
                        r = (s + 1) % 2
                        act.wait_ge(p_turned, wb + k)
                        wait_reuse(act, pv_ready, wb + k - 2)
                        act.activation(Pt[r][:, :], psP[r][:, :], ACT.Copy).then_inc(p_evac, 1)
                    if u % 2 == 1 and live(5):
                        m = turn * 2 + u // 2 - 2
                        o = u // 2
                        act.wait_ge(ot_ready, TILES * l + m + 1)
                        wait_reuse(act, y_ready, TILES * l + m - 1)
                        act.activation(ots[o][:, :], psT[:, 0:128], ACT.Copy).then_inc(ot_evac, 1)

                pipeline(act, B, 4, 5, step)

            def classes():
                act.wait_ge(q_ready, 2 * CHUNKS)
                for c in range(CHUNKS):
                    wait_reuse(act, sq_summed, c - 1)
                    act.activation(sq[c % 2][:, :], QT[:, CHUNK * c:CHUNK * c + CHUNK], ACT.Square).then_inc(squared, 1)
                act.wait_ge(sim_act, 1)
                act.activation(n2[1][:, :], n2[0][:, :], ACT.Ln).then_inc(sim_act, 1)
                act.wait_ge(sim_act, 2)
                act.activation(n2[2][:, :], n2[1][:, :], ACT.Exp, scale=-0.5).then_inc(sim_act, 1)

            def registers():
                rows = slice(0, H * REG)

                def step(k, turn, u, live):
                    s = u
                    if live(0):
                        act.wait_ge(reg_shifted, k + 1)
                        act.activation(Pr[s][rows, 0:4 * S], Pr[s][rows, 0:4 * S], ACT.Exp).then_inc(reg_exp, 1)
                    if live(2):
                        act.wait_ge(reg_turned, k - 1)
                        wait_reuse(act, reg_pv, k - 3)
                        act.activation(Pt[s][:, 0:4 * H * REG], psP[s][:, 0:4 * H * REG], ACT.Copy).then_inc(reg_evac, 1)

                pipeline(act, REG_STEPS, 2, 2, step)
                act.wait_ge(reg_pv, REG_STEPS)

            prepare(0, 0)
            attention(0)
            prepare(1, 1)
            classes()
            registers()
            attention(1)
            prepare(2, 2)
            attention(2)

            def mixture1():
                rstds(3)

                def step(k, turn, u, live):
                    normalise(3, k)

                pipeline(act, CHUNKS, 2, 0, step)
                act.wait_ge(route_step, ROUTE_STEPS)
                act.activation(rt[:, 2, :, :], rt[:, 0, :, :], ACT.Exp).then_inc(route_act, 1)

            def attention2():
                rstds(4)
                act.wait_ge(keep_ready, 7)
                act.activation(gauss, gauss, ACT.Exp, scale=-1.0 / DEV_POW).then_inc(gauss_ready, 1)

                def step(k, turn, u, live):
                    s, r = u, (u + 1) % 2
                    if live(0):
                        act.wait_ge(a_in_psum, k + 1)
                        act.activation(KT[:, bass.ds(k * CHUNK, CHUNK)], psP[s][:, :], ACT.Copy).then_inc(a_ready, 1)
                        normalise(4, k)
                    if live(1):
                        act.wait_ge(nmx_ready, k)
                        wait_reuse(act, rd2_ready, k - 2)
                        for t in range(TPC):
                            col = sc2[r][:, 128 * t:128 * t + 128]
                            act.activation(col, col, ACT.Exp, bias=nmx[r][:, t:t + 1],
                                           accum_out=den[r][:, 0, t:t + 1]).then_inc(e2_ready, 1)
                        act.wait_ge(at_turned, k)
                        wait_reuse(act, cx_in_psum, k - 2)
                        act.activation(at2[r][:, :], psO[1][:, :], ACT.Copy).then_inc(at_ready, 1)
                        act.wait_ge(cx_turned, k)
                        wait_reuse(act, c_in_psum, k - 2)
                        act.activation(cxT[r][:, :], psO[1][:, :], ACT.Copy).then_inc(cxT_ready, 1)
                        act.wait_ge(c_in_psum, k)
                        wait_reuse(act, x_updated, TILES * 4 + TPC * (k - 2))
                        act.activation(th[r][:, :], psO[0][:, :], ACT.Tanh).then_inc(th_ready, 1)

                pipeline(act, CHUNKS, 2, 1, step)

            mixture1()
            def mixture(m):
                ln, F, tiles, before = MOE[m]
                rstds(ln)

                def step(k, turn, u, live):
                    wait_reuse(act, xn_kept, CHUNKS * m + k)
                    normalise(ln, k)

                pipeline(act, CHUNKS, 2, 0, step)
                if m == 0:
                    act.wait_ge(route_step, ROUTE_STEPS + 1)
                    act.activation(gate[:, 2, :], gate[:, 0, :], ACT.Exp, scale=-1.0).then_inc(score_act, 1)

                    def shared_step(k, turn, u, live):
                        for j in range(2):
                            act.wait_ge(sh_gate, 2 * k + j + 1)
                            wait_reuse(act, sh_hid, 2 * k + j - 1)
                            act.activation(sc2[j][:, :], psS[j][:, :], ACT.Silu).then_inc(sh_act, 1)

                    pipeline(act, CHUNKS, 2, 0, shared_step)

                def expert_step(k, turn, u, live):
                    s = u % 2
                    if live(1):
                        r = (s + 1) % 2
                        act.wait_ge(e_hidden, before + k)
                        if m == 0:
                            wait_reuse(act, e_h, before + k - 2)
                            act.activation(act2[r][:, 0:F], psS[r][:, 0:F], ACT.Silu).then_inc(e_act, 1)
                        else:
                            wait_reuse(act, e_hturned, before + k - 2)
                            act.activation(hb[r][:, 0:F], psS[r][:, 0:F], ACT.Relu).then_inc(e_h, 1)
                    if live(3):
                        act.wait_ge(e_out, before + k - 2)
                        us = (u + 5) % 8
                        if us % 4 == 0:
                            wait_reuse(act, tiles_stored[us // 4], 16 * (tiles // 8) * m + 16 * (turn - (1 if u < 3 else 0)))
                        act.activation(ys[us // 4][:, 128 * (us % 4):128 * (us % 4) + 128], psO[(s + 1) % 2][:, 0:128],
                                       ACT.Copy).then_inc(e_y, 1)

                if m == 0:
                    act.wait_ge(sh_out, CHUNKS)
                pipeline(act, tiles, 8, 3, expert_step)

            attention2()
            mixture(0)
            prepare(3, 6)
            attention(3)
            mixture(1)

        @block.tensor
        def _(pe):
            pe.wait_ge(w_loaded, W_DMAS * 16)
            for l in range(4):
                mm = pe.matmul(psY[:, D * l:D * l + D], bqkv[:, l, 2:3].broadcast_to([128, 128]), W[str(l)][:, 3, :],
                               start=True, stop=True)
            mm.then_inc(bias_through, 1)

            def prepare(l, ln, cross):
                w = W[str(l)]
                pe.wait_ge(bo_ready, 1)
                pe.wait_ge(w_loaded, W_DMAS * 16)
                pe.wait_ge(cst_loaded, CST_DMAS * 16)
                pe.wait_ge(consts_ready, CONSTS)
                if cross:
                    pe.wait_ge(ctx_loaded, 64)

                def step(k, turn, u, live):
                    s = u % 2
                    if live(0):
                        pe.wait_ge(xn_ready, TPC * (CHUNKS * ln + k + 1))
                        wait_reuse(pe, xt_ready, CHUNKS * ln + k - 1)
                        for j in range(TPC):
                            mm = pe.transpose((psT, psY)[s][:, 128 * j:128 * j + 128], xn[:, j, :], ident)
                        mm.then_inc(xt_in_psum, 1)
                    if live(1):
                        c = k - 1
                        r = (s + 1) % 2
                        pe.wait_ge(xt_ready, CHUNKS * ln + k)
                        wait_reuse(pe, q_ready, CHUNKS * l + k - 2)
                        wait_reuse(pe, k_ready, CHUNKS * l + k - 2)
                        src = ctxT[:, bass.ds(c * CHUNK, CHUNK)] if cross else xts[r][:, :]
                        pe.matmul(psS[r][:, :], w[:, 0, :], xts[r][:, :], start=True, stop=True).then_inc(proj_ready, 1)
                        pe.matmul(psP[r][:, :], w[:, 1, :], src, start=True, stop=True).then_inc(proj_ready, 1)
                        wait_reuse(pe, v_ready, 2 * (CHUNKS * l + c))
                        pe.wait_ge(doubled, CHUNKS * l + k)
                        for h in range(2):
                            for j in range(4):
                                mm = pe.matmul(psO[h][:, 128 * j:128 * j + 128],
                                               xd[r][:, 4 * h + j, :, :].rearrange("p j s -> p (j s)"),
                                               w[:, 2, :], start=True, stop=True)
                            mm.then_inc(proj_ready, 1)

                pipeline(pe, CHUNKS, 2, 1, step)

            def attention(l, add):
                wb = units_before[l]
                masked = l == 1
                w = W[str(l)]
                pe.wait_ge(v_ready, 2 * CHUNKS * (l + 1))

                def step(k, turn, u, live):
                    s = u % 2
                    if live(0):
                        pe.wait_ge(staged, 2 * (wb + k + 1))
                        if masked:
                            pe.wait_ge(class_staged, k + 1)
                        wait_reuse(pe, shifted, wb + k - 1)
                        pe.matmul(psS[s][:, :], qbd[s][:, :], kbd[s][:, :], start=True, stop=False)
                        rows, left = (2, addL[s]) if masked else (3, onesr)
                        row = add[0:rows, bass.ds(k * S, S)]
                        pe.matmul(psS[s][:, :].rearrange("p (g k) -> p g k", g=G), left[:, :],
                                  row.unsqueeze(1).broadcast_to([rows, G, S]),
                                  start=False, stop=True).then_inc(scores_ready, 1)
                    if live(1):
                        r = (s + 1) % 2
                        pe.wait_ge(exp_ready, wb + k)
                        wait_reuse(pe, p_evac, wb + k - 2)
                        for g in range(4):
                            mm = pe.transpose(psP[r][:, 128 * g:128 * g + 128], Pr[r][:, 128 * g:128 * g + 128], ident)
                        mm.then_inc(p_turned, 1)
                    if live(2):
                        r = s
                        pe.wait_ge(p_evac, wb + k - 1)
                        us = (u + 2) % 4
                        batch = turn * 4 + u - 2
                        vb = VB[:, bass.ds(batch, 1), :].rearrange("p o c -> p (o c)")
                        if us % 2 == 0:
                            wait_reuse(pe, on_ready, wb + k - 4)
                        o = psO[us // 2]
                        c0 = (us % 2) * G * VW
                        for g in range(4):
                            mm = pe.matmul(o[:, c0 + 2 * VW * g:c0 + 2 * VW * (g + 1)],
                                           Pt[r][:, 128 * g:128 * g + 128],
                                           vb[:, 2 * VW * g:2 * VW * (g + 1)], start=True, stop=True)
                        mm.then_inc(pv_ready, 1)
                    if u % 2 == 1 and live(5):
                        m = turn * 2 + u // 2 - 2
                        pe.wait_ge(on_ready, wb + k - 3)
                        wait_reuse(pe, ot_evac, TILES * l + m)
                        for b in range(2):
                            mm = pe.matmul(psT[:, 64 * b:64 * b + 64], on[u // 2][:, b, :], fold_self if masked else fold2,
                                           start=(b == 0 or not masked), stop=not masked)
                        if masked:
                            mm = pe.matmul(psT[:, 0:128].rearrange("p (b s) -> p b s", b=2)[:, :, 0:REG], ident,
                                           reg_out[:, bass.ds(2 * m, 2), :], start=False, stop=True)
                        mm.then_inc(ot_ready, 1)
                    if u % 2 == 0 and live(6):
                        m = turn * 2 + u // 2 - 3
                        o = (u // 2 + 1) % 2
                        pe.wait_ge(ot_evac, TILES * l + m + 1)
                        wait_reuse(pe, x_updated, TILES * UPD_OF[l] + m)
                        pe.matmul(psY[:, 0:128], ots[o][:, :], w[:, 3, :],
                                  start=True, stop=True).then_inc(y_ready, 1)

                pipeline(pe, B, 4, 5, step)

            def turn_x(ln, k, u):
                pe.wait_ge(xn_ready, TPC * (CHUNKS * ln + k + 1))
                wait_reuse(pe, xt_ready, CHUNKS * ln + k - 1)
                for j in range(TPC):
                    mm = pe.transpose((psT, psY)[u][:, 128 * j:128 * j + 128], xn[:, j, :], ident)
                mm.then_inc(xt_in_psum, 1)

            def ranks(r):
                pe.wait_ge(route_step, ROUTE_STEPS * r + 5)
                cols = oh[:, :, :].rearrange("p e t -> p (e t)")
                pe.matmul(psO[0][:, 0:256], ones128[:, :], cols, start=True, stop=True).then_inc(rank_ready, 1)
                pe.matmul(psO[1][:, 0:256], upto, cols, start=True, stop=True).then_inc(rank_ready, 1)

            def mixture1():
                pe.wait_ge(w1f_loaded, 48)

                def step(k, turn, u, live):
                    if live(0):
                        turn_x(3, k, u)
                    if live(1):
                        r = (u + 1) % 2
                        pe.wait_ge(xt_ready, CHUNKS * 3 + k)
                        wait_reuse(pe, y_kept, k - 2)
                        for j in range(TPC):
                            pe.matmul(psO[r][:, NE * j:NE * j + NE], xts[r][:, 128 * j:128 * j + 128], w1f[:, 0:NE],
                                      start=True, stop=True)
                        for j in range(TPC):
                            mm = pe.matmul(psS[r][:, 128 * j:128 * j + 128], xts[r][:, 128 * j:128 * j + 128],
                                           w1f[:, NE:NE + D], start=True, stop=True)
                        mm.then_inc(route_pe, 1)

                pipeline(pe, CHUNKS, 2, 1, step)
                ranks(0)

            def attention2():
                pe.wait_ge(l2_loaded, 80)
                pe.wait_ge(ctx2_loaded, 16)

                def step(k, turn, u, live):
                    s, r = u, (u + 1) % 2
                    if live(0):
                        wait_reuse(pe, a_ready, k - 1)
                        pe.matmul(psP[s][:, :], wa[:, 0, :], ctxT[:, bass.ds(k * CHUNK, CHUNK)], start=True, stop=True).then_inc(a_in_psum, 1)
                        turn_x(4, k, u)
                    if live(1):
                        c = k - 1
                        pe.wait_ge(xt_ready, CHUNKS * 4 + k)
                        pe.wait_ge(a_ready, k)
                        wait_reuse(pe, capped, k - 2)
                        for j in range(TPC):
                            mm = pe.matmul(psS[r][:, 128 * j:128 * j + 128], xts[r][:, 128 * j:128 * j + 128],
                                           KT[:, bass.ds(c * CHUNK + 128 * j, 128)], start=True, stop=True)
                        mm.then_inc(s2_ready, 1)
                        pe.wait_ge(g2_ready, k)
                        wait_reuse(pe, cxT_ready, k - 1)
                        for j in range(TPC):
                            mm = pe.transpose(psO[1][:, 128 * j:128 * j + 128], sc2[r][:, 128 * j:128 * j + 128], ident)
                        mm.then_inc(at_turned, 1)
                        pe.wait_ge(at_ready, k)
                        wait_reuse(pe, th_ready, k - 1)
                        for j in range(TPC):
                            mm = pe.matmul(psO[0][:, 128 * j:128 * j + 128], at2[r][:, 128 * j:128 * j + 128],
                                           QT[:, bass.ds(c * CHUNK + 128 * j, 128)], start=True, stop=True)
                        mm.then_inc(cx_in_psum, 1)
                        pe.wait_ge(cx_ready, k)
                        for j in range(TPC):
                            mm = pe.transpose(psO[1][:, 128 * j:128 * j + 128], cx[r][:, 128 * j:128 * j + 128], ident)
                        mm.then_inc(cx_turned, 1)
                        pe.wait_ge(cxT_ready, k)
                        for j in range(TPC):
                            pe.matmul(psO[0][:, 128 * j:128 * j + 128], cxT[r][:, 128 * j:128 * j + 128], wa[:, 1, :],
                                      start=True, stop=False)
                            mm = pe.matmul(psO[0][:, 128 * j:128 * j + 128], xts[r][:, 128 * j:128 * j + 128], wa[:, 2, :],
                                           start=False, stop=True)
                        mm.then_inc(c_in_psum, 1)

                pipeline(pe, CHUNKS, 2, 1, step)

            def mixture(m):
                ln, F, tiles, before = MOE[m]
                pe.wait_ge(mw_loaded, 48)

                def step(k, turn, u, live):
                    if live(0):
                        turn_x(ln, k, u)
                    if live(1):
                        r = (u + 1) % 2
                        pe.wait_ge(xt_ready, CHUNKS * ln + k)
                        wait_reuse(pe, logit_ready, CHUNKS * (m + 1) + k - 2)
                        for j in range(TPC):
                            mm = pe.matmul(psO[r][:, NE * j:NE * j + NE], xts[r][:, 128 * j:128 * j + 128], rw[:, m, :],
                                           start=True, stop=True)
                        mm.then_inc(route_pe, 1)

                pipeline(pe, CHUNKS, 2, 1, step)
                ranks(m + 1)
                pe.wait_ge(experts_loaded, 16 * (6 if m == 0 else 10))

                def shared_step(k, turn, u, live):
                    if live(0):
                        for j in range(2):
                            for half, ps, made, free, n in ((0, psS, sh_gate, sh_act, 2 * k + j - 1), (1, psP, sh_up, sh_hid, 2 * k + j - 1)):
                                wait_reuse(pe, free, n)
                                at = NE * 512 + 256 * half + 128 * j
                                pe.matmul(ps[j][:, :], wv[:, at:at + 128], KT[:, bass.ds(k * CHUNK, CHUNK)],
                                          start=True, stop=True).then_inc(made, 1)
                    if live(1):
                        r = (u + 1) % 2
                        pe.wait_ge(sh_hid, 2 * k)
                        wait_reuse(pe, sh_added, k - 2)
                        for t in range(TPC):
                            for j in range(2):
                                at = (NE + 1) * 512 + NE * 256 + 128 * j
                                mm = pe.matmul(psO[r][:, 128 * t:128 * t + 128], sh_h[r][j][:, 128 * t:128 * t + 128],
                                               wv[:, at:at + 128], start=(j == 0), stop=(j == 1))
                        mm.then_inc(sh_out, 1)

                if m == 0:
                    pe.wait_ge(xT_kept, CHUNKS)
                    pe.wait_ge(route_step, ROUTE_STEPS * 2)
                    pipeline(pe, CHUNKS, 2, 1, shared_step)
                    pe.wait_ge(sh_added, CHUNKS)
                pe.wait_ge(place_step, PLACE_STEPS[m + 1])
                if m == 1:
                    pe.wait_ge(b_rows, 96)
                w_out_at = (NE + 1) * 512 if m == 0 else NE * 512

                expert_of = lambda tile: pe.value_load(slot_e[0:1, bass.ds(tile, 1)], min_val=0, max_val=NE - 1)
                next_e = None

                def expert_step(k, turn, u, live):
                    nonlocal next_e
                    s = u % 2
                    if live(0):
                        if u % 4 == 0:
                            pe.wait_ge(tiles_loaded[u // 4], 16 * (tiles // 8) * m + 16 * (turn + 1))
                        wait_reuse(pe, e_xT, before + k - 1)
                        pe.transpose((psT, psY)[s][:, 0:128], xl[u // 4][:, 128 * (u % 4):128 * (u % 4) + 128],
                                     ident).then_inc(e_turned, 1)
                    if live(1):
                        r = (s + 1) % 2
                        e_in = expert_of(k - 1) if u == 0 or next_e is None else next_e
                        pe.wait_ge(e_xT, before + k)
                        wait_reuse(pe, e_h, before + k - 2)
                        mm = pe.matmul(psS[r][:, :], xT[r], wv[:, bass.ds(e_in * 512, 512)], start=True, stop=(m == 0))
                        if m == 1:
                            mm = pe.matmul(psS[r][:, :], onesr[:, :], b1r[:, bass.ds(e_in * 512, 512)], start=False, stop=True)
                        mm.then_inc(e_hidden, 1)
                        next_e = expert_of(k) if u < 7 and live(0) else None
                    if live(3):
                        e_back = expert_of(k - 3)
                    if live(2):
                        pe.wait_ge(e_h, before + k - 1)
                        wait_reuse(pe, e_hT, before + k - 3)
                        for j in range(F // 128):
                            mm = pe.transpose(psP[s][:, 128 * j:128 * j + 128], hb[s][:, 128 * j:128 * j + 128], ident)
                        mm.then_inc(e_hturned, 1)
                    if live(3):
                        r = (s + 1) % 2
                        pe.wait_ge(e_hT, before + k - 2)
                        wait_reuse(pe, e_y, before + k - 4)
                        for j in range(F // 128):
                            mm = pe.matmul(psO[r][:, 0:128], hT[r][:, 128 * j:128 * j + 128],
                                           wv[:, bass.ds(e_back * F + (w_out_at + 128 * j), 128)], start=(j == 0),
                                           stop=(m == 0 and j == F // 128 - 1))
                        if m == 1:
                            mm = pe.matmul(psO[r][:, 0:128], onesr[:, :], b2r[:, bass.ds(e_back * D, D)], start=False, stop=True)
                        mm.then_inc(e_out, 1)

                pipeline(pe, tiles, 8, 3, expert_step)

            def classes():
                pe.wait_ge(sim_step, 2)
                pe.wait_ge(k_ready, 2 * CHUNKS)
                pe.matmul(psY[:, 0:1], heads_rep, gcol[:, 1:2], start=True, stop=True).then_inc(sim_pe, 1)
                pe.wait_ge(q_ready, 2 * CHUNKS)
                for c in range(CHUNKS):
                    mm = pe.matmul(psS[1][:, :], guide_pad[:, 112 - H * c:240 - H * c], QT[:, CHUNK * c:CHUNK * c + CHUNK],
                                   start=(c == 0), stop=(c == CHUNKS - 1))
                mm.then_inc(sim_pe, 1)
                for c in range(CHUNKS):
                    pe.wait_ge(squared, c + 1)
                    mm = pe.matmul(psS[0][:, :], heads_pad[:, 112 - H * c:240 - H * c], sq[c % 2][:, :],
                                   start=(c == 0), stop=(c == CHUNKS - 1)).then_inc(sq_summed, 1)
                pe.wait_ge(sq_summed, CHUNKS)
                pe.sem_inc(sim_pe, 1)
                pe.wait_ge(sim_step, 4)
                pe.matmul(psP[0][0:CHUNKS, :], mean_h, n2[4][:, :], start=True, stop=True).then_inc(sim_pe, 1)
                pe.wait_ge(cls_rows, 48)
                pe.wait_ge(sim_step, 8)

            def registers():
                rows, cols = slice(0, H * REG), H * REG
                pe.wait_ge(v_ready, 2 * CHUNKS * 2)

                def step(k, turn, u, live):
                    s, r = u, (u + 1) % 2
                    if live(0):
                        pe.wait_ge(reg_staged, k + 1)
                        wait_reuse(pe, reg_shifted, k - 1)
                        pe.matmul(psS[s][rows, 0:4 * S], neg_class[:, :], maskR[0:2, bass.ds(k * 4 * S, 4 * S)],
                                  start=True, stop=False)
                        for b in range(4):
                            mm = pe.matmul(psS[s][rows, S * b:S * b + S], kbd[s][:, cols * b:cols * b + cols],
                                           KT[:, bass.ds(k * 4 * S + S * b, S)], start=False, stop=(b == 3))
                        mm.then_inc(reg_scores, 1)
                    if live(2):
                        pe.wait_ge(reg_probs, k - 1)
                        wait_reuse(pe, reg_evac, k - 3)
                        for b in range(4):
                            mm = pe.transpose(psP[s][:, cols * b:cols * b + cols], th[s][rows, 128 * b:128 * b + 128],
                                              ident[rows, 0:cols])
                        mm.then_inc(reg_turned, 1)
                    if live(3):
                        pe.wait_ge(reg_evac, k - 2)
                        wait_reuse(pe, reg_masked, k - 4)
                        for b in range(4):
                            vb = VB[:, bass.ds((k - 3) * 4 + b, 1), :].rearrange("p o (g w) -> p (o g) w", w=VW)
                            mm = pe.matmul(psO[r][rows, 128 * b:128 * b + 128], Pt[r][:, cols * b:cols * b + cols],
                                           vb[:, :, 0:2 * E], start=True, stop=True)
                        mm.then_inc(reg_pv, 1)
                    if live(4):
                        pe.wait_ge(reg_masked, k - 3)
                        wait_reuse(pe, reg_kept, k - 5)
                        for b in range(4):
                            mm = pe.matmul((psT, psY)[s][:, REG * b:REG * b + REG], sc2[s][rows, 128 * b:128 * b + 128],
                                           fold_reg, start=True, stop=True)
                        mm.then_inc(reg_folded, 1)

                pipeline(pe, REG_STEPS, 2, 4, step)
                pe.wait_ge(reg_kept, REG_STEPS)

            prepare(0, 0, True)
            pe.wait_ge(rows_moved, 48)
            attention(0, addR)
            prepare(1, 1, False)
            classes()
            registers()
            attention(1, maskR)
            prepare(2, 2, True)
            attention(2, addR)
            mixture1()
            attention2()
            mixture(0)
            prepare(3, 6, True)
            pe.wait_ge(ones_again, 1)
            attention(3, addR)
            mixture(1)


LAYERS = ("L0_xcond", "L1_xcond", "L3_xcond")


def kernel(**inputs):
    import concourse.bacc as bacc
    from concourse.bass_utils import run_bass_kernel_spmd

    i = {k: np.asarray(v) for k, v in inputs.items()}
    arrays = {"x": i["x"], "ctxT": np.ascontiguousarray(i["ctx_1024"].reshape(TOK, D).T),
              "condB_tau": i["condB_tau"], "fside_BxS2_0": i["fside_BxS2_0"]}
    for n in LAYERS:
        arrays[n + "_W"] = np.stack([np.ascontiguousarray(i[f"{n}_W{c}"].T) for c in "qkvo"])
        arrays[n + "_b"] = np.stack([i[f"{n}_b{c}"] for c in "qkvo"])
    qkv = i["L0_ffn_W_qkv"]
    arrays["L0_ffn_W"] = np.stack([qkv[:, 0:D], qkv[:, D:2 * D], qkv[:, 2 * D:3 * D], i["L0_ffn_W_proj"]])
    zero = np.zeros(D, np.float32)
    arrays["g_first"] = np.ascontiguousarray(i["L0_ffn_g_info"][0, 0].reshape(D, 1))
    arrays["cst"] = constants()
    arrays["L0_ffn_b"] = np.stack([zero, zero, zero, i["L0_ffn_b_proj"]])

    arrays["ctx_1024"] = i["ctx_1024"]
    arrays["L1_ffn_Wg"], arrays["L1_ffn_We"], arrays["L1_ffn_be"] = i["L1_ffn_Wg"], i["L1_ffn_We"], i["L1_ffn_be"].reshape(1, D)
    wc = i["L2_xcond_W_c"].T
    arrays["L2_W"] = np.stack([np.ascontiguousarray(i["L2_xcond_W_a"].T), wc[0:D], wc[D:2 * D]])
    arrays["pt2"] = np.ascontiguousarray(i["condB_pt"].reshape(TILES, 2).T)
    arrays["len2"] = np.ascontiguousarray(i["_lenS2"].reshape(TILES, 2).T)
    for n in ("gate_w", "sh_gate", "sh_up", "sh_down", "rt_gate", "rt_up", "rt_down"):
        arrays["L2_ffn_" + n] = i["L2_ffn_" + n]
    arrays["L3_ffn_WrT"] = np.ascontiguousarray(i["L3_ffn_Wr"].T)
    arrays["L3_ffn_br"] = i["L3_ffn_br"].reshape(1, NE)
    arrays["L3_ffn_W1T"] = np.ascontiguousarray(i["L3_ffn_W1"].transpose(0, 2, 1))
    arrays["L3_ffn_W2T"] = np.ascontiguousarray(i["L3_ffn_W2"].transpose(0, 2, 1))
    arrays["L3_ffn_b1"] = i["L3_ffn_b1"].reshape(64, 64)
    arrays["L3_ffn_b2"] = i["L3_ffn_b2"].reshape(64, 16)
    for n in LAYERS + ("L0_ffn",):
        arrays[n + "_bT"] = np.ascontiguousarray(arrays[n + "_b"].T)

    nc = bacc.Bacc("TRN2", target_bir_lowering=False, num_devices=1)
    handles = {k: nc.dram_tensor(k + "_in", v.shape, mybir.dt.from_np(v.dtype), kind="ExternalInput").ap()
               for k, v in arrays.items()}
    out = nc.dram_tensor("out", (B, S, D), F32, kind="ExternalOutput").ap()
    build(nc, handles, out)
    r = run_bass_kernel_spmd(nc, [{k + "_in": np.ascontiguousarray(v) for k, v in arrays.items()}], core_ids=[0])
    return r.results[0]["out"]
```

```python
from contextlib import ExitStack

import numpy as np

import concourse.bass as bass
from concourse import mybir
from concourse.alu_op_type import AluOpType as ALU

ACT = mybir.ActivationFunctionType
AX = mybir.AxisListType
F32 = mybir.dt.float32
BF16 = mybir.dt.bfloat16
I32 = mybir.dt.int32
U32 = mybir.dt.uint32

B, S, D = 64, 64, 128
H, E = 16, 8
G = H // 2
TOK = B * S
TILES = TOK // 128
CHUNK = 512
CHUNKS = TOK // CHUNK
TPC = CHUNK // 128
BPC = CHUNK // S
REG = 5
EPS = 1e-5
VW = E * 2 + 1
NE = 8
CAP = TOK // NE
WINDOW, DEV_POW = 16.0, 128.0
BIG = float(2 ** 60)


SLOTS = -(-(TOK // 128 + 8 - 1) // 4) * 4
CST_COLS = 332 + 128 + G + 240 + 128 + 8 + 256 + 256 + 128 + 64 + 1 + 128 + SLOTS + H + TILES + SLOTS


def constants():
    p = np.arange(128)
    head, pair = p // E, p // (2 * E)
    fold = (p[:, None] % S == np.arange(S)[None, :]).astype(np.float32)
    is_reg = (np.arange(S) < REG)[None, :]
    cst = np.concatenate([
        np.eye(128), fold, fold * np.where(is_reg, 0.5, 1.0), np.zeros((128, 64)),
        head[:, None] % 2 == np.arange(2)[None, :], pair[:, None] % 2 == np.arange(2)[None, :],
        pair[:, None] == np.arange(G)[None, :],
        p[:, None] // S == pair[None, :] % 2, p[:, None] // S == np.arange(G)[None, :] % 2,
        np.zeros((128, 112)), head[:, None] == np.arange(H)[None, :], np.zeros((128, 112)),
        head[:, None] == p[None, :] % H, (p[:, None] // H == np.arange(CHUNKS)[None, :]) / H,
        np.repeat(NE - np.arange(NE), TILES)[None, :] + 0 * p[:, None],
        np.tile(np.arange(TILES) > 0, NE)[None, :] + 0 * p[:, None],
        p[:, None] <= p[None, :],
        np.arange(S)[None, :] + 0 * p[:, None], p[:, None] % S,
        p[None, :] // S == p[:, None],
        np.arange(SLOTS)[None, :] + 0 * p[:, None],
        0.5 * (head[:, None] == np.arange(H)[None, :]),
        128 * (SLOTS + np.arange(TILES))[None, :] + p[:, None], 128 * np.arange(SLOTS)[None, :] + p[:, None],
    ], axis=1).astype(np.float32)
    return cst


def wait_reuse(eng, semaphore, value):
    if not isinstance(value, int) or value > 0:
        eng.wait_ge(semaphore, value)


def pipeline(eng, count, period, lag, step):
    first = -(-max(lag + 1, period) // period)
    for k in range(first * period):
        step(k, k // period, k % period, lambda l, k=k: k - l >= 0)
    with eng.Fori(first, count // period) as turn:
        for u in range(period):
            step(turn * period + u, turn, u, lambda l: True)
    for k in range(count, count + lag):
        step(k, k // period, k % period, lambda l, k=k: k - l < count)


def build(nc, a, out):
    ctx = ExitStack()
    with ctx:
        def sb(name, shape, dt=F32):
            return ctx.enter_context(nc.sbuf_tensor(name, shape, dt))

        def pb(name):
            return ctx.enter_context(nc.psum_tensor(name, [128, 512], F32))

        def sem(name):
            return ctx.enter_context(nc.semaphore(name))

        X = sb("X", [128, TILES, D])
        ctxT = sb("ctxT", [128, TOK])
        QT = sb("QT", [128, TILES * (D + 1)])
        rows_of_x = QT[:, :].rearrange("p (t d) -> p t d", d=D + 1)
        KT = sb("KT", [128, TOK])
        VB = sb("VB", [128, B, G * VW])
        xd = [sb(f"xd{i}", [128, BPC, 2, S]) for i in range(2)]
        cst = sb("cst", [128, CST_COLS])
        ident = cst[:, 0:128]
        fold2 = cst[:, 128:192]
        fold_self = cst[:, 192:256]
        hp_mask = cst[:, 320:322]
        g2_mask = cst[:, 322:324]
        g_mask = cst[:, 324:332]
        v_mask = cst[:, 332:460]
        v_ones = cst[:, 460:468]
        heads_pad = cst[:, 468:708]
        heads_rep = cst[:, 708:836]
        mean_h = cst[:, 836:844]
        first_w = cst[:, 844:1100]
        not_first = cst[:, 1100:1356]
        upto = cst[:, 1356:1484]
        idx_row = cst[:, 1484:1548]
        idx_col = cst[:, 1548:1549]
        half_f = cst[0:2, 1549:1677]
        slot_no = cst[:, 1677:1677 + SLOTS]
        half_head = cst[:, 1677 + SLOTS:1677 + SLOTS + H]
        row_no = cst[:, 1677 + SLOTS + H:1677 + SLOTS + H + TILES]
        spare_row = cst[:, 1677 + SLOTS + H + TILES:]
        gcol = sb("gcol", [128, 2])
        guide_pad = sb("guide_pad", [128, 240])
        n2g = sb("n2g", [128, 1])
        ext = sb("ext", [CHUNKS, 6])
        clsb = sb("clsb", [CHUNKS, 3, CHUNK], BF16)
        neg_class = sb("neg_class", [2, H * REG], BF16)
        reg_den = [sb(f"reg_den{i}", [128, 2, 4]) for i in range(2)]
        reg_out = sb("reg_out", [128, B, REG])
        onesr = sb("onesr", [3, 128], BF16)
        stats = sb("stats", [128, TILES, 6])
        lnw = sb("lnw", [128, 6, TILES])
        rstd = sb("rstd", [128, TILES])
        nmr = sb("nmr", [128, TILES])
        xn = [sb(f"xn{i}", [128, TPC, D]) for i in range(2)]
        xts = [sb(f"xts{i}", [128, CHUNK]) for i in range(2)]
        tau_b = sb("tau_b", [128, B])
        tau_s = sb("tau_s", [128, B])
        dl = sb("dl", [64, 3, 64])
        dlb = sb("dlb", [64, 3, 64], BF16)
        rows_sb = sb("rows_sb", [65, TOK], BF16)
        addR = rows_sb[0:3, :]
        clsrow = rows_sb[32:33, :]
        maskR = sb("maskR", [3, TOK], BF16)
        W = [sb(f"W{l}", [128, 4, 128]) for l in range(4)]
        bqkv = sb("bqkv", [128, 4, 4])
        bo = sb("bo", [128, 4, D])
        qbd = [sb(f"qbd{i}", [128, 128]) for i in range(2)]
        kbd = [sb(f"kbd{i}", [128, 512]) for i in range(2)]
        addL = [sb(f"addL{i}", [2, 128], BF16) for i in range(2)]
        mx = [sb(f"mx{i}", [128, G]) for i in range(2)]
        Pr = [sb(f"Pr{i}", [128, 512]) for i in range(2)]
        Pt = [sb(f"Pt{i}", [128, 512]) for i in range(2)]
        rden = sb("rden", [128, 2 * G])
        on = [sb(f"on{i}", [128, 2, H * E]) for i in range(2)]
        ots = [sb(f"ots{i}", [128, 128]) for i in range(2)]

        xl = [sb(f"xl{i}", [128, TPC * (D + 1)]) for i in range(2)]
        th = [xl[i][:, 0:CHUNK] for i in range(2)]
        n2 = [kbd[0], kbd[1], Pt[0], Pt[1], Pr[0]]
        sq = [Pr[1], th[1]]
        simr = th[0][0:CHUNKS, :]
        logit = sb("logit", [128, NE, TILES])
        oh = sb("oh", [128, NE, TILES])
        rt = sb("rt", [128, 4, NE, TILES])
        gate = sb("gate", [128, 4, TILES])
        ones128 = sb("ones128", [128, 128])
        w1f = sb("w1f", [128, NE + D])
        be = sb("be", [128, D])
        Yt = KT
        wa = sb("wa", [128, 3, 128])
        half = sb("half", [2, 128], BF16)
        winb = sb("winb", [64, 4])
        leni = sb("leni", [64, 1], I32)
        wmask = sb("wmask", [64, 2, S])
        wmaskb = sb("wmaskb", [64, S], BF16)
        gcols = sb("gcols", [128, 2, TILES])
        sc2 = [sb(f"sc2{i}", [128, CHUNK]) for i in range(2)]
        nmx = [sb(f"nmx{i}", [128, TPC]) for i in range(2)]
        den = [sb(f"den{i}", [128, 2, TPC]) for i in range(2)]
        xt2 = [xd[i][:, 0:4, :, :].rearrange("p b j s -> p (b j s)") for i in range(2)]
        at2 = [kbd[i] for i in range(2)]
        cx = [Pr[i] for i in range(2)]
        cxT = [Pt[i] for i in range(2)]
        rw = sb("rw", [128, 2, NE])
        rb = sb("rb", [128, NE])
        dest = sb("dest", [128, TILES], U32)
        ei = sb("ei", [128, 2, NE], I32)
        ef = sb("ef", [128, 3, NE])
        slots = sb("slots", [128, SLOTS, NE])
        slotf = sb("slotf", [128, SLOTS])
        slot_e = sb("slot_e", [128, SLOTS], I32)
        wv = VB[:, :, :].rearrange("p b c -> p (b c)")
        ys = xts
        by_row = lambda x: x[:, :].rearrange("p (t d) -> p t d", d=D + 1)
        to_row = [sb(f"to_row{i}", [128, TPC], U32) for i in range(2)]
        xT = [Pr[i][:, 0:128] for i in range(2)]
        sh_h = [kbd, Pt]
        hb, hT, act2 = kbd, Pt, sc2
        b1r = maskR[0:3, :]
        b2r = sb("b2r", [3, NE * D], BF16)
        b2l = sb("b2l", [64, 3, 16])
        b2b = sb("b2b", [64, 3, 16], BF16)
        xs_dram = [nc.dram_tensor(f"xs_dram{m}", [SLOTS * 128, D + 1], F32).ap() for m in range(2)]
        ys_dram = nc.dram_tensor("ys_dram", [SLOTS * 128 + TOK, D], F32).ap()

        psS = [pb("psS0"), pb("psS1")]
        psP = [pb("psP0"), pb("psP1")]
        psO = [pb("psO0"), pb("psO1")]
        psT = pb("psT")
        psY = pb("psY")

        x_loaded = sem("x_loaded")
        ctx_loaded = sem("ctx_loaded")
        w0_loaded = sem("w0_loaded")
        w_loaded = sem("w_loaded")
        side_loaded = sem("side_loaded")
        rows_moved = sem("rows_moved")
        consts_ready = sem("consts_ready")
        cst_loaded = sem("cst_loaded")
        CST_DMAS, CONSTS, W_DMAS = 1, 9, 4
        ROUTE_STEPS = 9
        delta_split = sem("delta_split")
        stats_ready = sem("stats_ready")
        ln_step = sem("ln_step")
        rsqrt_ready = sem("rsqrt_ready")
        root_inverted = sem("root_inverted")
        norm_ready = sem("norm_ready")
        xn_ready = sem("xn_ready")
        xn_half = sem("xn_half")
        xt_in_psum = sem("xt_in_psum")
        xt_ready = sem("xt_ready")
        q_proj = sem("q_proj")
        k_proj = sem("k_proj")
        v_proj = sem("v_proj")
        ctx_first = sem("ctx_first")
        q_ready = sem("q_ready")
        k_ready = sem("k_ready")
        v_ready = sem("v_ready")
        doubled = sem("doubled")
        class_staged = sem("class_staged")
        staged = sem("staged")
        bo_added = sem("bo_added")
        bias_through = sem("bias_through")
        bo_ready = sem("bo_ready")
        scores_ready = sem("scores_ready")
        max_ready = sem("max_ready")
        shifted = sem("shifted")
        exp_ready = sem("exp_ready")
        p_turned = sem("p_turned")
        p_evac = sem("p_evac")
        pv_ready = sem("pv_ready")
        rden_ready = sem("rden_ready")
        on_ready = sem("on_ready")
        ot_ready = sem("ot_ready")
        ot_evac = sem("ot_evac")
        y_ready = sem("y_ready")
        x_updated = sem("x_updated")
        slot_free = sem("slot_free")
        stored = sem("stored")
        w1f_loaded = sem("w1f_loaded")
        route_pe = sem("route_pe")
        logit_half = sem("logit_half")
        logit_ready = sem("logit_ready")
        y_kept = sem("y_kept")
        route_step = sem("route_step")
        route_act = sem("route_act")
        rank_ready = sem("rank_ready")
        l2_loaded = sem("l2_loaded")
        win_step = sem("win_step")
        gcol_step = sem("gcol_step")
        win_rows = sem("win_rows")
        win_filled = sem("win_filled")
        half_ready = sem("half_ready")
        keep_step = sem("keep_step")
        x2_copied = sem("x2_copied")
        y_gated = sem("y_gated")
        ctx2_loaded = sem("ctx2_loaded")
        a_in_psum = sem("a_in_psum")
        a_ready = sem("a_ready")
        s2_ready = sem("s2_ready")
        nmx_ready = sem("nmx_ready")
        e2_ready = sem("e2_ready")
        rd2_ready = sem("rd2_ready")
        at_turned = sem("at_turned")
        at_ready = sem("at_ready")
        cx_in_psum = sem("cx_in_psum")
        cx_ready = sem("cx_ready")
        cx_turned = sem("cx_turned")
        cxT_ready = sem("cxT_ready")
        c_in_psum = sem("c_in_psum")
        th_ready = sem("th_ready")
        mw_loaded = sem("mw_loaded")
        zero_ready = sem("zero_ready")
        zeroed = sem("zeroed")
        xn_kept = sem("xn_kept")
        place_step = sem("place_step")
        score_act = sem("score_act")
        scattered = sem("scattered")
        experts_loaded = sem("experts_loaded")
        tiles_loaded = [sem(f"tiles_loaded{i}") for i in range(2)]
        rows_out = [sem(f"rows_out{i}") for i in range(2)]
        rows_back = [sem(f"rows_back{i}") for i in range(4)]
        numbered = sem("numbered")
        row_nos = sem("row_nos")
        scored = sem("scored")
        rows_scaled = sem("rows_scaled")
        xT_kept = sem("xT_kept")
        sh_gate = sem("sh_gate")
        sh_up = sem("sh_up")
        sh_act = sem("sh_act")
        sh_hid = sem("sh_hid")
        sh_out = sem("sh_out")
        sh_added = sem("sh_added")
        e_turned = sem("e_turned")
        e_xT = sem("e_xT")
        e_hidden = sem("e_hidden")
        e_act = sem("e_act")
        e_h = sem("e_h")
        e_hturned = sem("e_hturned")
        e_hT = sem("e_hT")
        e_out = sem("e_out")
        e_y = sem("e_y")
        b_split = sem("b_split")
        b_rows = sem("b_rows")
        b_loaded = sem("b_loaded")
        ones_again = sem("ones_again")
        PLACE_STEPS = [0, 12, 24]
        gauss_ready = sem("gauss_ready")
        g_loaded = sem("g_loaded")
        sim_step = sem("sim_step")
        sim_pe = sem("sim_pe")
        sim_act = sem("sim_act")
        sim_pool = sem("sim_pool")
        squared = sem("squared")
        sq_summed = sem("sq_summed")
        sim_newton = sem("sim_newton")
        cls_rows = sem("cls_rows")
        reg_staged = sem("reg_staged")
        reg_scores = sem("reg_scores")
        reg_max = sem("reg_max")
        reg_shifted = sem("reg_shifted")
        reg_exp = sem("reg_exp")
        reg_summed = sem("reg_summed")
        reg_rden = sem("reg_rden")
        reg_probs = sem("reg_probs")
        reg_turned = sem("reg_turned")
        reg_evac = sem("reg_evac")
        reg_values = sem("reg_values")
        reg_pv = sem("reg_pv")
        reg_masked = sem("reg_masked")
        reg_kept = sem("reg_kept")

        REG_STEPS = B // 4
        UPD_OF = [0, 1, 2, 6]
        units_before = [B * l for l in range(5)]
        SHARED_LN = [2, 3, 5, 6, 7]

        MOE = [(5, 256, SLOTS, 0), (7, 512, SLOTS, SLOTS)]

        def rows_of(dram, tile, n=1):
            return dram[bass.ds(tile * 128, 128 * n), :]

        def by_batch(row):
            return row.rearrange("c (b s) -> c b s", s=S)

        block = ctx.enter_context(nc.Block())

        @block.sync
        def _(sp):
            sp.dma_start(ctxT[:, 0:1024], a["ctxT"][:, 0:1024]).then_inc(ctx_first, 16)
            sp.dma_start(cst[:, :], a["cst"]).then_inc(cst_loaded, 16)
            sp.dma_start(tau_b[:, :], a["condB_tau"].rearrange("(o b) -> o b", o=1).broadcast_to([128, B])).then_inc(side_loaded, 16)
            sp.dma_start(gcol[:, 0:1], a["g_first"]).then_inc(g_loaded, 16)
            sp.dma_start(dl[:, 0, :], a["fside_BxS2_0"]).then_inc(side_loaded, 16)
            xv = a["x"].rearrange("b s d -> (b s) d").rearrange("(t p) d -> p t d", p=128)
            for q in range(1, 4):
                sp.dma_start(ctxT[:, 1024 * q:1024 * q + 1024],
                             a["ctxT"][:, 1024 * q:1024 * q + 1024]).then_inc(ctx_loaded, 16)
            sp.dma_start(bo[:, :, :].rearrange("p l d -> p (l d)"), a["bo"].broadcast_to([128, 4 * D])).then_inc(w_loaded, 16)
            for l in range(1, 4):
                sp.dma_start(W[l][:, :, :], a["W"][l].rearrange("j d e -> d j e")).then_inc(w_loaded, 16)
            for q in range(4):
                sp.dma_start(X[:, 8 * q:8 * q + 8, :], xv[:, 8 * q:8 * q + 8, :]).then_inc(x_loaded, 16)
            sp.dma_start(w1f[:, 0:NE], a["L1_ffn_Wg"]).then_inc(w1f_loaded, 16)
            sp.dma_start(w1f[:, NE:NE + D], a["L1_ffn_We"]).then_inc(w1f_loaded, 16)
            sp.dma_start(be[:, :], a["L1_ffn_be"].broadcast_to([128, D])).then_inc(w1f_loaded, 16)
            sp.dma_start(wa[:, :, :], a["L2_W"].rearrange("j d e -> d j e")).then_inc(l2_loaded, 16)
            sp.dma_start(winb[:, 0:1], a["condB_pt"]).then_inc(l2_loaded, 16)
            sp.dma_start(leni[:, :], a["lenS2"]).then_inc(l2_loaded, 16)
            for h in range(2):
                sp.dma_start(gcols[64 * h:64 * h + 64, 0, :], a["pt2"][h:h + 1, :].broadcast_to([64, TILES])).then_inc(l2_loaded, 16)
            sp.dma_start(rw[:, 0, :], a["L2_ffn_gate_w"]).then_inc(mw_loaded, 16)
            sp.dma_start(rw[:, 1, :], a["L3_ffn_WrT"]).then_inc(mw_loaded, 16)
            sp.dma_start(rb[:, :], a["L3_ffn_br"].broadcast_to([128, NE])).then_inc(mw_loaded, 16)
            sp.wait_ge(zero_ready, 1)
            for m in range(2):
                sp.dma_start(xs_dram[m].rearrange("(t p) d -> p t d", p=128),
                             xl[0][:, 0:D + 1].unsqueeze(1).broadcast_to([128, SLOTS, D + 1])).then_inc(zeroed, 16)
            wmaskb_by_tile = [wmaskb[32 * j:32 * j + 32, :] for j in range(2)]
            sp.wait_ge(delta_split, 5)
            for j in range(3):
                sp.dma_start(addR[j:j + 1, :].rearrange("o (b k) -> o b k", b=B), dlb[:, j, :]).then_inc(rows_moved, 16)
            sp.wait_ge(rows_moved, 48)
            sp.dma_start(dl[:, 1, :], a["L3_ffn_b1"]).then_inc(b_loaded, 16)
            sp.dma_start(b2l[:, 1, :], a["L3_ffn_b2"]).then_inc(b_loaded, 16)
            sp.wait_ge(sim_step, 10)
            sp.wait_ge(sim_pool, 4)
            for dst, j in ((maskR[0:1, :], 0), (maskR[1:2, :], 1), (clsrow, 2)):
                sp.dma_start(dst.rearrange("o (c k) -> o c k", c=CHUNKS), clsb[:, j, :]).then_inc(cls_rows, 16)
            sp.wait_ge(win_step, 7)
            sp.wait_ge(win_filled, 1)
            for j in range(2):
                sp.dma_start(maskR[j:j + 1, :].rearrange("o (t j k) -> o t j k", j=2, k=S)[:, :, j, :],
                             wmaskb_by_tile[j]).then_inc(win_rows, 16)
            sp.wait_ge(staged, 2 * units_before[3])
            sp.dma_start(QT[:, 0:TOK].rearrange("p (t d) -> p t d", d=D),
                         a["ctx_1024"].rearrange("b s d -> (b s) d").rearrange("(t p) d -> p t d", p=128)).then_inc(ctx2_loaded, 16)
            def mixture(m):
                ln, F, tiles, before = MOE[m]
                if m == 0:
                    sp.wait_ge(pv_ready, units_before[3])
                    w_in = wv[:, 0:(NE + 1) * 512]
                    w_out = wv[:, (NE + 1) * 512:(NE + 1) * 768]
                    for j, n in enumerate(("rt_gate", "rt_up")):
                        sp.dma_start(w_in[:, 0:NE * 512].rearrange("p (e j f) -> p e j f", e=NE, j=2)[:, :, j, :],
                                     a["L2_ffn_" + n].rearrange("e p f -> p e f")).then_inc(experts_loaded, 16)
                    for j, n in enumerate(("sh_gate", "sh_up")):
                        sp.dma_start(w_in[:, NE * 512 + 256 * j:NE * 512 + 256 * j + 256], a["L2_ffn_" + n]).then_inc(experts_loaded, 16)
                    sp.dma_start(w_out[:, 0:NE * 256].rearrange("p (e j d) -> p e j d", e=NE, j=2),
                                 a["L2_ffn_rt_down"].rearrange("e (j p) d -> p e j d", p=128)).then_inc(experts_loaded, 16)
                    sp.dma_start(w_out[:, NE * 256:(NE + 1) * 256].rearrange("p (j d) -> p j d", j=2),
                                 a["L2_ffn_sh_down"].rearrange("(j p) d -> p j d", p=128)).then_inc(experts_loaded, 16)
                else:
                    sp.wait_ge(b_split, 10)
                    sp.wait_ge(s2_ready, CHUNKS)
                    for j in range(3):
                        sp.dma_start(b1r[j:j + 1, :].rearrange("o (b k) -> o b k", b=64), dlb[:, j, :]).then_inc(b_rows, 16)
                        sp.dma_start(b2r[j:j + 1, :].rearrange("o (b k) -> o b k", b=64), b2b[:, j, :]).then_inc(b_rows, 16)
                    sp.wait_ge(pv_ready, units_before[4])
                    for h in range(2):
                        e = slice(4 * h, 4 * h + 4)
                        sp.dma_start(wv[:, 2048 * h:2048 * h + 2048].rearrange("p (e f) -> p e f", e=4),
                                     a["L3_ffn_W1T"][e].rearrange("e p f -> p e f")).then_inc(experts_loaded, 16)
                        sp.dma_start(wv[:, 4096 + 2048 * h:6144 + 2048 * h].rearrange("p (e j d) -> p e j d", e=4, j=4),
                                     a["L3_ffn_W2T"][e].rearrange("e (j p) d -> p e j d", p=128)).then_inc(experts_loaded, 16)
                sp.wait_ge(scattered, 16 * TILES * (m + 1))

                def groups(dram, k):
                    return dram[bass.ds(k * 512, 512), :].rearrange("(t p) d -> p t d", p=128)

                def step(k, turn, u, live):
                    wait_reuse(sp, e_xT, (before + 4 * k - 4) if not isinstance(k, int) or k > 1 else 0)
                    sp.dma_start(by_row(xl[u]), groups(xs_dram[m], k)).then_inc(tiles_loaded[u], 16)

                pipeline(sp, tiles // 4, 2, 0, step)
                for i in range(2):
                    sp.wait_ge(rows_out[i], 16 * (tiles // 2) * (m + 1))
                ys_rows = ys_dram[SLOTS * 128:, :].rearrange("(t p) d -> p t d", p=128)
                for q in range(4):
                    sp.dma_start(QT[:, 0:TOK].rearrange("p (t d) -> p t d", d=D)[:, 8 * q:8 * q + 8, :],
                                 ys_rows[:, 8 * q:8 * q + 8, :]).then_inc(rows_back[q], 16)

            mixture(0)
            mixture(1)
            ov = out.rearrange("b s d -> (b s) d").rearrange("(t p) d -> p t d", p=128)
            for q in range(4):
                sp.wait_ge(x_updated, TILES * 7 + 8 * q + 8)
                sp.dma_start(ov[:, 8 * q:8 * q + 8, :], X[:, 8 * q:8 * q + 8, :]).then_inc(stored, 16)
            sp.wait_ge(stored, 64)

        @block.gpsimd
        def _(pool):
            for i in range(2):
                pool.memset(on[i][:, :, :], 0.0).then_inc(consts_ready, 1)
            pool.memset(onesr[:, :], 1.0).then_inc(consts_ready, 1)
            pool.memset(ones128[:, :], 1.0).then_inc(consts_ready, 1)
            pool.memset(xl[0][:, 0:D + 1], 0.0).then_inc(zero_ready, 1)
            pool.wait_ge(cst_loaded, CST_DMAS * 16)
            pool.tensor_copy(half[:, :], half_f).then_inc(half_ready, 1)
            pool.tensor_copy(VB[:, :, :].rearrange("p b (g w) -> p b g w", w=VW)[:, :, :, VW - 1],
                             v_ones.unsqueeze(1).broadcast_to([128, B, G])).then_inc(consts_ready, 1)

            def attention(l):
                wb = units_before[l]

                def step(k, turn, u, live):
                    s = u % 2
                    at = k * S
                    wait_reuse(pool, scores_ready, wb + k - 1)
                    pool.sem_inc(slot_free, 1)
                    pool.tensor_tensor(
                        kbd[s][:, :].rearrange("p (g k) -> p g k", g=G),
                        KT[:, bass.ds(at, S)].unsqueeze(1).broadcast_to([128, G, S]),
                        g_mask[:, :].unsqueeze(2).broadcast_to([128, G, S]), ALU.mult).then_inc(staged, 1)
                    pool.tensor_tensor(
                        qbd[s][:, :].rearrange("p (g k) -> p g k", g=2),
                        QT[:, bass.ds(at, S)].unsqueeze(1).broadcast_to([128, 2, S]),
                        hp_mask[:, :].unsqueeze(2).broadcast_to([128, 2, S]), ALU.mult).then_inc(staged, 1)
                    if u % 2 == 1:
                        t = turn * 2 + u // 2
                        pool.tensor_tensor(X[:, bass.ds(t, 1), :].rearrange("p o d -> p (o d)"),
                                           X[:, bass.ds(t, 1), :].rearrange("p o d -> p (o d)"),
                                           bo[:, l, :], ALU.add).then_inc(bo_added, 1)

                pool.wait_ge(w_loaded, W_DMAS * 16)
                pool.wait_ge(q_ready, CHUNKS * (l + 1))
                pool.wait_ge(bo_ready, 1)
                pool.wait_ge(k_ready, CHUNKS * (l + 1))
                pipeline(pool, B, 4, 0, step)

            for i in range(2):
                pool.memset(addL[i][:, :], 1.0).then_inc(consts_ready, 1)
            pool.memset(neg_class[:, :], 1.0).then_inc(consts_ready, 1)
            pool.wait_ge(consts_ready, CONSTS - 1)
            pool.memset(neg_class[0:1, :], -1.0).then_inc(consts_ready, 1)

            def classes():
                pool.wait_ge(q_ready, 2 * CHUNKS)
                pool.memset(clsb[:, 1, :], -BIG).then_inc(sim_pool, 1)
                pool.wait_ge(sim_pool, 1)
                pool.memset(by_batch(clsb[:, 1, :])[:, :, 0:REG], 0.0).then_inc(sim_pool, 1)
                pool.wait_ge(sim_step, 6)
                pool.partition_all_reduce(ext[:, 2:4], ext[:, 0:2], CHUNKS, bass.bass_isa.ReduceOp.max).then_inc(sim_pool, 2)

            def registers():
                def step(k, turn, u, live):
                    s, r = u, (u + 1) % 2
                    if live(0):
                        wait_reuse(pool, reg_scores, k - 1)
                        pool.sem_inc(slot_free, 1)
                        pool.tensor_tensor(
                            kbd[s][:, 0:4 * H * REG].rearrange("p (b h q) -> p b h q", b=4, h=H),
                            QT[:, bass.ds(k * 4 * S, 4 * S)].rearrange("p (b s) -> p b s", b=4)[:, :, 0:REG]
                            .unsqueeze(2).broadcast_to([128, 4, H, REG]),
                            heads_pad[:, 112:128].unsqueeze(1).unsqueeze(3).broadcast_to([128, 4, H, REG]),
                            ALU.mult).then_inc(reg_staged, 1)
                    if live(2):
                        wait_reuse(pool, reg_turned, k - 3)
                        pool.wait_ge(reg_rden, k - 1)
                        pool.sem_inc(slot_free, 1)
                        pool.tensor_tensor(
                            th[s][0:H * REG, :].rearrange("p (b j s) -> p b j s", b=4, j=2),
                            Pr[s][0:H * REG, 0:4 * S].rearrange("p (b s) -> p b s", b=4).unsqueeze(2)
                            .broadcast_to([H * REG, 4, 2, S]),
                            reg_den[s][0:H * REG, 1, :].unsqueeze(2).unsqueeze(3).broadcast_to([H * REG, 4, 2, S]),
                            ALU.mult).then_inc(reg_probs, 1)

                pool.wait_ge(sim_step, 10)
                pipeline(pool, REG_STEPS, 2, 2, step)
                pool.wait_ge(reg_scores, REG_STEPS)
                pool.wait_ge(cls_rows, 48)

            attention(0)
            classes()
            registers()
            attention(1)
            attention(2)

            pool.wait_ge(scores_ready, units_before[2])
            pool.memset(maskR[0:2, :], -4.0 * BIG).then_inc(win_filled, 1)
            pool.wait_ge(ctx2_loaded, 16)
            pool.wait_ge(gauss_ready, 1)
            rows = QT[:, 0:TOK].rearrange("p (t d) -> p t d", d=D)
            pool.tensor_tensor(rows, rows, gcols[:, 1, :].unsqueeze(2).broadcast_to([128, TILES, D]), ALU.mult).then_inc(gauss_ready, 1)

            def keep_xt(k, turn, u, live):
                wait_reuse(pool, c_in_psum, k - 1)
                pool.wait_ge(xt_ready, CHUNKS * 4 + k + 1)
                pool.sem_inc(slot_free, 1)
                pool.tensor_copy(xt2[u], xts[u][:, :]).then_inc(x2_copied, 1)

            pipeline(pool, CHUNKS, 2, 0, keep_xt)

            def mixture(m):
                ln, F, tiles, before = MOE[m]
                if m == 0:
                    pool.wait_ge(cx_in_psum, CHUNKS)

                def step(k, turn, u, live):
                    pool.wait_ge(xn_ready, TPC * (CHUNKS * ln + k + 1))
                    pool.wait_ge(xn_half, TPC // 2 * (CHUNKS * SHARED_LN.index(ln) + k + 1))
                    pool.sem_inc(slot_free, 1)
                    pool.tensor_copy(QT[:, bass.ds(k * TPC * (D + 1), TPC * (D + 1))].rearrange("p (t d) -> p t d", d=D + 1)[:, :, 0:D],
                                     xn[u][:, :, :]).then_inc(xn_kept, 1)

                pipeline(pool, CHUNKS, 2, 0, step)
                pool.tensor_copy(rows_of_x[:, :, D], row_no).then_inc(numbered, 1)
                pool.wait_ge(numbered, m + 1)
                pool.wait_ge(xn_kept, CHUNKS * (m + 1))
                pool.wait_ge(zeroed, 32)
                if m == 0:
                    pool.wait_ge(scored, 2)
                    rows = rows_of_x[:, :, 0:D]
                    pool.tensor_tensor(rows, rows, gate[:, 3, :].unsqueeze(2).broadcast_to([128, TILES, D]),
                                       ALU.mult).then_inc(rows_scaled, 1)
                    pool.wait_ge(rows_scaled, 1)
                pool.wait_ge(place_step, PLACE_STEPS[m + 1])
                for t in range(TILES):
                    pool.indirect_dma_start(xs_dram[m][:, :], bass.IndirectOffsetOnAxis(dest[:, t:t + 1], 0),
                                            rows_of_x[:, t, :], None).then_inc(scattered, 16)

                def put_back(k, turn, u, live):
                    if u % 4 == 0:
                        pool.wait_ge(row_nos, before // 4 + 2 * turn + u // 4 + 1)
                    pool.wait_ge(e_y, before + k + 1)
                    pool.sem_inc(slot_free, 1)
                    pool.indirect_dma_start(ys_dram[:, :], bass.IndirectOffsetOnAxis(to_row[u // 4][:, u % 4:u % 4 + 1], 0),
                                            ys[u // 4][:, 128 * (u % 4):128 * (u % 4) + 128], None).then_inc(rows_out[u // 4], 16)

                pipeline(pool, tiles, 8, 0, put_back)

            mixture(0)
            pool.wait_ge(e_hidden, MOE[0][2])
            pool.wait_ge(e_out, MOE[0][2])
            pool.tensor_copy(VB[:, :, :].rearrange("p b (g w) -> p b g w", w=VW)[:, :, :, VW - 1],
                             v_ones.unsqueeze(1).broadcast_to([128, B, G])).then_inc(ones_again, 1)
            attention(3)
            mixture(1)



        @block.vector
        def _(v):
            v.wait_ge(side_loaded, 32)
            v.tensor_scalar(tau_s[:, :], tau_b[:, :], float(E) ** -0.5, None, ALU.mult).then_inc(ln_step, 1)
            v.tensor_scalar(dl[:, 1, :], dl[:, 0, :], float(E) ** -0.5, None, ALU.mult).then_inc(ln_step, 1)
            v.wait_ge(ln_step, 2)

            def split3(x, parts, counter, n):
                v.tensor_copy(parts[:, 0, :], x[:, 1, :]).then_inc(counter, 1)
                v.wait_ge(counter, n + 1)
                v.tensor_tensor(x[:, 2, :], x[:, 1, :], parts[:, 0, :], ALU.subtract).then_inc(counter, 1)
                v.wait_ge(counter, n + 2)
                v.tensor_copy(parts[:, 1, :], x[:, 2, :]).then_inc(counter, 1)
                v.wait_ge(counter, n + 3)
                v.tensor_tensor(x[:, 1, :], x[:, 2, :], parts[:, 1, :], ALU.subtract).then_inc(counter, 1)
                v.wait_ge(counter, n + 4)
                v.tensor_copy(parts[:, 2, :], x[:, 1, :]).then_inc(counter, 1)

            split3(dl, dlb, delta_split, 0)
            n_ln = 2

            def windows():
                v.wait_ge(cst_loaded, CST_DMAS * 16)
                v.wait_ge(l2_loaded, 80)
                v.tensor_scalar(winb[:, 2:3], winb[:, 0:1], -WINDOW, 0.0, ALU.add, ALU.max).then_inc(win_step, 1)
                v.tensor_scalar(winb[:, 3:4], winb[:, 0:1], WINDOW, None, ALU.add).then_inc(win_step, 1)
                v.tensor_copy(winb[:, 1:2], leni[:, :]).then_inc(win_step, 1)
                v.wait_ge(win_step, 3)
                v.tensor_tensor(winb[:, 3:4], winb[:, 3:4], winb[:, 1:2], ALU.min).then_inc(win_step, 1)
                v.tensor_scalar(wmask[:, 0, :], idx_row[0:64, :], winb[:, 2:3], -BIG, ALU.is_lt, ALU.mult).then_inc(win_step, 1)
                v.wait_ge(win_step, 5)
                v.tensor_scalar(wmask[:, 1, :], idx_row[0:64, :], winb[:, 3:4], -BIG, ALU.is_gt, ALU.mult).then_inc(win_step, 1)
                v.wait_ge(win_step, 6)
                v.tensor_tensor(wmaskb[:, :], wmask[:, 0, :], wmask[:, 1, :], ALU.min).then_inc(win_step, 1)
                v.tensor_scalar(gcols[:, 1, :], gcols[:, 0, :], idx_col, None, ALU.subtract).then_inc(gcol_step, 1)
                v.wait_ge(gcol_step, 1)
                v.tensor_tensor(gcols[:, 1, :], gcols[:, 1, :], gcols[:, 1, :], ALU.mult).then_inc(gcol_step, 1)


            def tile_stats(ln, t):
                if ln == 0:
                    v.wait_ge(x_loaded, 64)
                else:
                    v.wait_ge(x_updated, TILES * (ln - 1) + t + 1)
                v.bn_stats(stats[:, bass.ds(t, 1), :].rearrange("p o c -> p (o c)"),
                           X[:, bass.ds(t, 1), :].rearrange("p o d -> p (o d)")).then_inc(stats_ready, 1)

            def norms(l):
                nonlocal n_ln
                v.wait_ge(stats_ready, TILES * (l + 1))
                me, mo, se, so = stats[:, :, 1], stats[:, :, 4], stats[:, :, 2], stats[:, :, 5]
                n = n_ln
                v.tensor_tensor(lnw[:, 0, :], me, mo, ALU.add).then_inc(ln_step, 1)
                v.tensor_tensor(lnw[:, 1, :], me, mo, ALU.subtract).then_inc(ln_step, 1)
                v.tensor_tensor(lnw[:, 2, :], se, so, ALU.add).then_inc(ln_step, 1)
                v.wait_ge(ln_step, n + 3)
                v.tensor_tensor(lnw[:, 1, :], lnw[:, 1, :], lnw[:, 1, :], ALU.mult).then_inc(ln_step, 1)
                v.tensor_scalar(lnw[:, 2, :], lnw[:, 2, :], 1.0 / D, EPS, ALU.mult, ALU.add).then_inc(ln_step, 1)
                v.wait_ge(ln_step, n + 5)
                v.scalar_tensor_tensor(lnw[:, 3, :], lnw[:, 1, :], 0.25, lnw[:, 2, :], ALU.mult, ALU.add).then_inc(ln_step, 1)
                v.wait_ge(ln_step, n + 6)
                v.wait_ge(rsqrt_ready, l + 1)
                y, t = lnw[:, 5, :], lnw[:, 1, :]
                v.reciprocal(y, lnw[:, 4, :]).then_inc(root_inverted, 1)
                v.wait_ge(root_inverted, l + 1)
                v.tensor_tensor(t, y, y, ALU.mult).then_inc(ln_step, 1)
                v.wait_ge(ln_step, n + 7)
                v.tensor_tensor(t, t, lnw[:, 3, :], ALU.mult).then_inc(ln_step, 1)
                v.wait_ge(ln_step, n + 8)
                v.tensor_scalar(t, t, -0.5, 1.5, ALU.mult, ALU.add).then_inc(ln_step, 1)
                v.wait_ge(ln_step, n + 9)
                v.tensor_tensor(rstd[:, :], t, y, ALU.mult).then_inc(norm_ready, 1)
                v.wait_ge(norm_ready, 2 * l + 1)
                v.scalar_tensor_tensor(nmr[:, :], lnw[:, 0, :], -0.5, rstd[:, :], ALU.mult, ALU.mult).then_inc(norm_ready, 1)
                n_ln = n + 9

            def normalise_half(ln, k, u, m=None):
                if ln not in SHARED_LN:
                    return
                wait_reuse(v, xt_in_psum, CHUNKS * ln + k - 1)
                if m is not None:
                    wait_reuse(v, xn_kept, CHUNKS * m + k - 1)
                for j in range(TPC // 2, TPC):
                    t = k * TPC + j
                    v.tensor_scalar(xn[u][:, j, :], X[:, bass.ds(t, 1), :].rearrange("p o d -> p (o d)"),
                                    rstd[:, bass.ds(t, 1)], nmr[:, bass.ds(t, 1)], ALU.mult, ALU.add).then_inc(xn_half, 1)

            def take_values(l, c):
                for h in range(2):
                    v.wait_ge(v_proj, 2 * (CHUNKS * l + c) + 1 + h)
                    v.tensor_tensor(
                        VB[:, bass.ds(c * BPC + 4 * h, 4), :].rearrange("p b (g w) -> p b g w", w=VW)[:, :, :, 0:2 * E],
                        psO[h][:, :].rearrange("p (b g w) -> p b g w", b=4, w=2 * E),
                        v_mask.rearrange("p (g w) -> p g w", w=2 * E).unsqueeze(1).broadcast_to([128, 4, G, 2 * E]),
                        ALU.mult).then_inc(v_ready, 1)

            def keys(l):
                v.wait_ge(cst_loaded, CST_DMAS * 16)

                def step(k, turn, u, live):
                    if live(0):
                        take_values(l, k)
                    if l == 0 and live(4):
                        for t in range(TPC):
                            tile_stats(0, (k - 4) * TPC + t)

                pipeline(v, CHUNKS, 2, 4 if l == 0 else 0, step)

            def prepare(l, ln, tau):
                def step(k, turn, u, live):
                    if live(0):
                        normalise_half(ln, k, u)
                    if live(1):
                        s = (u + 1) % 2
                        v.wait_ge(xt_in_psum, CHUNKS * ln + k)
                        v.tensor_copy(xts[s][:, :], (psT, psY)[s][:, :]).then_inc(xt_ready, 1)
                    if live(2):
                        c = k - 2
                        r = u
                        v.wait_ge(q_proj, CHUNKS * l + c + 1)
                        if tau is None:
                            v.tensor_scalar(QT[:, bass.ds(c * CHUNK, CHUNK)], psS[r][:, :], bqkv[:, l, 0:1],
                                            float(E) ** -0.5, ALU.add, ALU.mult).then_inc(q_ready, 1)
                            take_values(l, c)
                        else:
                            v.scalar_tensor_tensor(
                                QT[:, bass.ds(c * CHUNK, CHUNK)].rearrange("p (b s) -> p b s", b=BPC),
                                psS[r][:, :].rearrange("p (b s) -> p b s", b=BPC), bqkv[:, l, 0:1],
                                tau_s[:, bass.ds(c * BPC, BPC)].unsqueeze(2).broadcast_to([128, BPC, S]),
                                ALU.add, ALU.mult).then_inc(q_ready, 1)

                v.wait_ge(w_loaded, W_DMAS * 16)
                v.wait_ge(norm_ready, 2 * ln + 2)
                pipeline(v, CHUNKS, 2, 2, step)

            def attention(l):
                wb = units_before[l]
                masked = l == 1
                behind = 1 if masked else 0

                def step(k, turn, u, live):
                    if masked and live(0):
                        wait_reuse(v, scores_ready, wb + k - 1)
                        v.tensor_copy(addL[u % 2][0:1, :].rearrange("o (j s) -> o j s", j=2),
                                      clsrow[:, bass.ds(k * S, S)]
                                      .unsqueeze(1).broadcast_to([1, 2, S])).then_inc(class_staged, 1)
                    if live(behind):
                        s = (u - behind) % 2
                        n = wb + k - behind
                        sc = psS[s][:, :].rearrange("p (g k) -> p g k", g=G)
                        v.wait_ge(scores_ready, n + 1)
                        v.tensor_reduce(mx[s][:, :], sc, AX.X, ALU.max).then_inc(max_ready, 1)
                        wait_reuse(v, p_turned, n - 1)
                        v.wait_ge(max_ready, n + 1)
                        v.tensor_tensor(Pr[s][:, :].rearrange("p (g k) -> p g k", g=G), sc,
                                        mx[s][:, :].unsqueeze(2).broadcast_to([128, G, S]),
                                        ALU.subtract).then_inc(shifted, 1)
                    if u % 2 == 0 and live(4):
                        m2 = k - 4
                        m = turn * 2 + u // 2 - 2
                        ps = (u // 2) % 2
                        v.wait_ge(pv_ready, wb + m2 + 2)
                        oo = psO[ps][:, 0:2 * G * VW].rearrange("p (g w) -> p g w", w=VW)
                        wait_reuse(v, on_ready, wb + m2)
                        v.reciprocal(rden[:, :].unsqueeze(2), oo[:, :, VW - 1:VW]).then_inc(rden_ready, 1)
                        v.wait_ge(rden_ready, wb // 2 + m + 1)
                        wait_reuse(v, ot_ready, TILES * l + m - 1)
                        dst = on[ps][:, :, :].rearrange("p b (g w) -> p (b g) w", w=2 * E)
                        for hp in range(2):
                            r = slice(64 * hp, 64 * hp + 64)
                            v.tensor_tensor(dst[r, :, E * hp:E * hp + E], oo[r, :, E * hp:E * hp + E],
                                            rden[r, :].unsqueeze(2).broadcast_to([64, 2 * G, E]),
                                            ALU.mult).then_inc(on_ready, 1)
                    if u % 2 == 1 and live(7):
                        t = turn * 2 + u // 2 - 3
                        v.wait_ge(y_ready, TILES * l + t + 1)
                        v.wait_ge(bo_added, TILES * l + t + 1)
                        xt = X[:, bass.ds(t, 1), :].rearrange("p o d -> p (o d)")
                        v.tensor_tensor(xt, psY[:, 0:128], xt, ALU.add).then_inc(x_updated, 1)
                    if u % 2 == 1 and live(9):
                        tile_stats(UPD_OF[l] + 1, turn * 2 + u // 2 - 4)

                pipeline(v, B, 4, 8, step)

            def classes():
                v.wait_ge(g_loaded, 16)
                v.wait_ge(cst_loaded, 16 * CST_DMAS)
                v.tensor_scalar(guide_pad[:, :], heads_pad, gcol[:, 0:1], None, ALU.mult).then_inc(sim_step, 1)
                v.tensor_tensor(gcol[:, 1:2], gcol[:, 0:1], gcol[:, 0:1], ALU.mult).then_inc(sim_step, 1)
                v.wait_ge(sim_pe, 1)
                v.tensor_copy(n2g[:, :], psY[:, 0:1]).then_inc(sim_step, 1)
                v.wait_ge(sim_step, 3)
                v.wait_ge(sim_pe, 3)
                v.tensor_scalar(n2[0][:, :], psS[0][:, :], n2g[:, 0:1], None, ALU.mult).then_inc(sim_act, 1)
                v.wait_ge(sim_act, 2)
                v.reciprocal(n2[2][:, :], n2[1][:, :]).then_inc(sim_act, 1)
                v.wait_ge(sim_act, 3)
                y, t = n2[2][:, :], n2[3][:, :]
                v.tensor_tensor(t, y, y, ALU.mult).then_inc(sim_newton, 1)
                v.wait_ge(sim_newton, 1)
                v.tensor_tensor(t, t, n2[0][:, :], ALU.mult).then_inc(sim_newton, 1)
                v.wait_ge(sim_newton, 2)
                v.tensor_scalar(t, t, -0.5, 1.5, ALU.mult, ALU.add).then_inc(sim_newton, 1)
                v.wait_ge(sim_newton, 3)
                v.tensor_tensor(t, t, y, ALU.mult).then_inc(sim_newton, 1)
                v.wait_ge(sim_newton, 4)
                v.tensor_tensor(n2[4][:, :], psS[1][:, :], t, ALU.mult).then_inc(sim_step, 1)
                v.wait_ge(sim_pe, 4)
                sim = by_batch(psP[0][0:CHUNKS, :])[:, :, REG:S]
                v.tensor_reduce(ext[:, 0:1], sim, AX.XY, ALU.max).then_inc(sim_step, 1)
                v.tensor_reduce(ext[:, 1:2], sim, AX.XY, ALU.min, negate=True).then_inc(sim_step, 1)
                v.wait_ge(sim_pool, 4)
                v.tensor_scalar(ext[:, 4:5], ext[:, 2:3], ext[:, 3:4], 0.9, ALU.add, ALU.mult).then_inc(sim_step, 1)
                v.wait_ge(sim_step, 7)
                v.tensor_scalar(simr, psP[0][0:CHUNKS, :], ext[:, 3:4], ext[:, 4:5], ALU.add, ALU.is_gt).then_inc(sim_step, 1)
                v.wait_ge(sim_step, 8)
                v.tensor_scalar(clsb[:, 0, :], simr, 2.0 * BIG, -BIG, ALU.mult, ALU.add).then_inc(sim_newton, 1)
                v.tensor_scalar(clsb[:, 2, :], simr, 2.0, -1.0, ALU.mult, ALU.add).then_inc(sim_newton, 1)
                v.wait_ge(sim_newton, 6)
                for j, c in ((0, 0.0), (2, 1.0)):
                    v.memset(by_batch(clsb[:, j, :])[:, :, 0:REG], c).then_inc(sim_step, 1)

            def registers():
                rows = slice(0, H * REG)
                kept = xts

                def step(k, turn, u, live):
                    s, r = u, (u + 1) % 2
                    if live(0):
                        sc = psS[s][rows, 0:4 * S].rearrange("p (b s) -> p b s", b=4)
                        v.wait_ge(reg_scores, k + 1)
                        wait_reuse(v, reg_shifted, k - 1)
                        v.tensor_reduce(mx[s][rows, 0:4], sc, AX.X, ALU.max).then_inc(reg_max, 1)
                        wait_reuse(v, reg_probs, k - 1)
                        v.wait_ge(reg_max, k + 1)
                        v.tensor_tensor(Pr[s][rows, 0:4 * S].rearrange("p (b s) -> p b s", b=4), sc,
                                        mx[s][rows, 0:4].unsqueeze(2).broadcast_to([H * REG, 4, S]),
                                        ALU.subtract).then_inc(reg_shifted, 1)
                    if live(1):
                        v.wait_ge(reg_exp, k)
                        v.tensor_reduce(reg_den[r][rows, 0, :], Pr[r][rows, 0:4 * S].rearrange("p (b s) -> p b s", b=4),
                                        AX.X, ALU.add).then_inc(reg_summed, 1)
                        wait_reuse(v, reg_probs, k - 2)
                        v.wait_ge(reg_summed, k)
                        v.reciprocal(reg_den[r][rows, 1, :], reg_den[r][rows, 0, :]).then_inc(reg_rden, 1)
                    if live(3):
                        v.wait_ge(reg_pv, k - 2)
                        wait_reuse(v, reg_kept, k - 4)
                        cols = lambda x: x[:, 0:4 * H * REG].rearrange("p (b h q) -> p b h q", b=4, h=H)
                        v.tensor_tensor(cols(kept[r]), cols(psO[r]),
                                        half_head.unsqueeze(1).unsqueeze(3).broadcast_to([128, 4, H, REG]),
                                        ALU.mult).then_inc(reg_masked, 1)
                        v.wait_ge(reg_masked, k - 2)
                        v.tensor_reduce(reg_out[:, bass.ds((k - 3) * 4, 4), :],
                                        kept[r][:, 0:4 * H * REG].rearrange("p (b h q) -> p b q h", b=4, h=H),
                                        AX.X, ALU.add).then_inc(reg_kept, 1)

                pipeline(v, REG_STEPS, 2, 3, step)
                v.wait_ge(cls_rows, 48)

            keys(0)
            v.wait_ge(w_loaded, W_DMAS * 16)
            v.wait_ge(bias_through, 1)
            v.tensor_tensor(bo[:, :, :].rearrange("p l d -> p (l d)"), psY[:, :],
                            bo[:, :, :].rearrange("p l d -> p (l d)"), ALU.add).then_inc(bo_ready, 1)
            norms(0)
            prepare(0, 0, tau_s)
            windows()
            attention(0)
            norms(1)
            prepare(1, 1, None)
            classes()
            registers()
            attention(1)
            norms(2)
            keys(2)
            prepare(2, 2, tau_s)
            attention(2)

            def xt_evac(ln, k, u):
                v.wait_ge(xt_in_psum, CHUNKS * ln + k + 1)
                v.tensor_copy(xts[u][:, :], (psT, psY)[u][:, :]).then_inc(xt_ready, 1)

            def routing(r):
                n = ROUTE_STEPS * r
                by_tile = lambda x: x.rearrange("p e t -> p t e")
                best = lambda j: gate[:, j, :].unsqueeze(1).broadcast_to([128, NE, TILES])
                if r == 0:
                    v.wait_ge(logit_half, 2 * CHUNKS)
                else:
                    v.wait_ge(logit_ready, CHUNKS * r)
                v.tensor_reduce(gate[:, 0, :], by_tile(logit[:, :, :]), AX.X, ALU.max).then_inc(route_step, 1)
                v.wait_ge(route_step, n + 1)
                v.tensor_tensor(rt[:, 0, :, :], logit[:, :, :], best(0), ALU.subtract).then_inc(route_step, 1)
                v.wait_ge(route_step, n + 2)
                v.scalar_tensor_tensor(rt[:, 1, :, :], rt[:, 0, :, :], 0.0, first_w.rearrange("p (e t) -> p e t", e=NE),
                                       ALU.is_equal, ALU.mult).then_inc(route_step, 1)
                v.wait_ge(route_step, n + 3)
                v.tensor_reduce(gate[:, 1, :], by_tile(rt[:, 1, :, :]), AX.X, ALU.max).then_inc(route_step, 1)
                v.wait_ge(route_step, n + 4)
                v.tensor_tensor(oh[:, :, :], rt[:, 1, :, :], best(1), ALU.is_equal).then_inc(route_step, 1)
                if r == 1:
                    v.wait_ge(score_act, 1)
                    v.tensor_scalar(gate[:, 3, :], gate[:, 2, :], 1.0, None, ALU.add).then_inc(scored, 1)
                    v.wait_ge(scored, 1)
                    v.reciprocal(gate[:, 3, :], gate[:, 3, :]).then_inc(scored, 1)
                v.wait_ge(rank_ready, 2 * r + 2)
                v.tensor_copy(rt[:, 2, :, :], psO[0][:, 0:256].rearrange("p (e t) -> p e t", e=NE)).then_inc(route_step, 1)
                v.wait_ge(route_step, n + 6)
                flat = lambda j: rt[:, j, :, :].rearrange("p e t -> p (e t)")
                v.tensor_tensor_scan(flat(1), not_first, flat(2), 0.0, ALU.mult, ALU.add).then_inc(route_step, 1)
                v.wait_ge(route_step, n + 7)
                v.tensor_tensor(flat(3), flat(1), flat(2), ALU.subtract).then_inc(route_step, 1)
                v.wait_ge(route_step, n + 8)
                v.tensor_tensor(flat(3), flat(3), psO[1][:, 0:256], ALU.add).then_inc(route_step, 1)
                v.wait_ge(route_step, n + 9)

            def mixture1():
                norms(3)

                def step(k, turn, u, live):
                    if live(0):
                        normalise_half(3, k, u)
                    if live(1):
                        xt_evac(3, k - 1, (u + 1) % 2)
                    if live(2):
                        r = u
                        v.wait_ge(route_pe, k - 1)
                        for h, ps in enumerate((psS[r], psO[r])):
                            two = ps[:, 0:2 * (NE + D)].rearrange("p (t c) -> p t c", c=NE + D)
                            v.tensor_copy(logit[:, :, bass.ds((k - 2) * TPC + 2 * h, 2)],
                                          two[:, :, 0:NE].rearrange("p t e -> p e t")).then_inc(logit_half, 1)
                            v.tensor_tensor(Yt[:, bass.ds((k - 2) * CHUNK + 256 * h, 256)].rearrange("p (t d) -> p t d", d=D),
                                            two[:, :, NE:], be[:, :].unsqueeze(1).broadcast_to([128, 2, D]),
                                            ALU.add).then_inc(y_kept, 1)

                v.wait_ge(norm_ready, 2 * 3 + 2)
                pipeline(v, CHUNKS, 2, 2, step)
                routing(0)
                v.scalar_tensor_tensor(rt[:, 1, :, :], rt[:, 3, :, :], float(CAP), oh[:, :, :], ALU.is_le, ALU.mult).then_inc(keep_step, 1)
                v.wait_ge(keep_step, 1)
                v.tensor_reduce(gate[:, 1, :], rt[:, 1, :, :].rearrange("p e t -> p t e"), AX.X, ALU.add).then_inc(keep_step, 1)
                v.wait_ge(route_act, 1)
                v.tensor_reduce(gate[:, 2, :], rt[:, 2, :, :].rearrange("p e t -> p t e"), AX.X, ALU.add).then_inc(keep_step, 1)
                v.wait_ge(keep_step, 3)
                v.reciprocal(gate[:, 3, :], gate[:, 2, :]).then_inc(keep_step, 1)
                v.wait_ge(keep_step, 4)
                v.tensor_tensor(gate[:, 1, :], gate[:, 1, :], gate[:, 3, :], ALU.mult).then_inc(keep_step, 1)
                v.wait_ge(keep_step, 5)
                v.wait_ge(y_kept, 2 * CHUNKS)

                def update(k, turn, u, live):
                    if live(0):
                        v.wait_ge(y_gated, TPC * (k + 1))
                        xc = X[:, bass.ds(k * TPC, TPC), :].rearrange("p t d -> p (t d)")
                        v.tensor_tensor(xc, Yt[:, bass.ds(k * CHUNK, CHUNK)], xc, ALU.add).then_inc(x_updated, TPC)
                    if live(1):
                        for t in range(TPC):
                            tile_stats(4, (k - 1) * TPC + t)

                pipeline(v, CHUNKS, 2, 1, update)

            def attention2():
                norms(4)

                def step(k, turn, u, live):
                    s, r = u, (u + 1) % 2
                    if live(1):
                        v.wait_ge(s2_ready, k)
                        wait_reuse(v, e2_ready, TPC * (k - 2))
                        v.tensor_reduce(nmx[r][:, :], psS[0][:, :].rearrange("p (t l) -> p t l", l=128), AX.X, ALU.max,
                                        negate=True).then_inc(nmx_ready, 1)
                    if live(0):
                        wait_reuse(v, s2_ready, k - 1)
                        wait_reuse(v, x2_copied, k - 1)
                        xt_evac(4, k, u)
                        v.wait_ge(a_in_psum, k + 1)
                        v.tensor_copy(KT[:, bass.ds(k * CHUNK, CHUNK)], psP[0][:, :]).then_inc(a_ready, 1)
                    if live(4):
                        v.wait_ge(th_ready, k - 3)
                        xc = X[:, bass.ds((k - 4) * TPC, TPC), :].rearrange("p t d -> p (t d)")
                        v.tensor_tensor(xc, th[s][:, :], xc, ALU.add).then_inc(x_updated, TPC)
                    if live(5):
                        for t in range(TPC):
                            tile_stats(5, (k - 5) * TPC + t)
                    if live(2):
                        v.wait_ge(e2_ready, TPC * (k - 1))
                        v.reciprocal(den[s][:, 1, :], den[s][:, 0, :]).then_inc(rd2_ready, 1)
                        v.wait_ge(rd2_ready, k - 1)
                        v.wait_ge(cx_in_psum, k - 1)
                        wait_reuse(v, cx_turned, k - 3)
                        v.tensor_tensor(cx[s][:, :].rearrange("p (t d) -> p t d", d=D),
                                        psO[0][:, :].rearrange("p (t d) -> p t d", d=D),
                                        den[s][:, 1, :].unsqueeze(2).broadcast_to([128, TPC, D]), ALU.mult).then_inc(cx_ready, 1)

                pipeline(v, CHUNKS, 2, 5, step)

            mixture1()
            def mixture(m):
                ln, F, tiles, before = MOE[m]
                norms(ln)
                v.wait_ge(mw_loaded, 48)

                def step(k, turn, u, live):
                    if live(0):
                        normalise_half(ln, k, u, m)
                    if live(1):
                        if m == 0:
                            wait_reuse(v, xT_kept, k - 2)
                        xt_evac(ln, k - 1, (u + 1) % 2)
                    if live(2):
                        r = u
                        if m == 0:
                            v.wait_ge(xt_ready, CHUNKS * ln + k - 1)
                            v.tensor_copy(KT[:, bass.ds((k - 2) * CHUNK, CHUNK)], xts[r][:, :]).then_inc(xT_kept, 1)
                        v.wait_ge(route_pe, CHUNKS * (m + 1) + k - 1)
                        src = psO[r][:, 0:NE * TPC].rearrange("p (t e) -> p e t", e=NE)
                        dst = logit[:, :, bass.ds((k - 2) * TPC, TPC)]
                        if m == 0:
                            v.tensor_copy(dst, src).then_inc(logit_ready, 1)
                        else:
                            v.tensor_tensor(dst, src, rb[:, :].unsqueeze(2).broadcast_to([128, NE, TPC]), ALU.add).then_inc(logit_ready, 1)

                v.wait_ge(norm_ready, 2 * ln + 2)
                pipeline(v, CHUNKS, 2, 2, step)
                routing(m + 1)
                n = PLACE_STEPS[m]

                def done(ins):
                    nonlocal n
                    ins.then_inc(place_step, 1)
                    n += 1

                done(v.tensor_scalar(ei[:, 0, :], rt[:, 1, :, TILES - 1], 127.0, None, ALU.add))
                v.wait_ge(place_step, n)
                done(v.tensor_scalar(ei[:, 1, :], ei[:, 0, :], 7, None, ALU.arith_shift_right))
                v.wait_ge(place_step, n)
                done(v.tensor_copy(ef[:, 0, :], ei[:, 1, :]))
                v.wait_ge(place_step, n)
                done(v.tensor_tensor_scan(ef[:, 1, :], ones128[:, 0:NE], ef[:, 0, :], 0.0, ALU.mult, ALU.add))
                v.wait_ge(place_step, n)
                done(v.tensor_tensor(slots[:, :, :], slot_no.unsqueeze(2).broadcast_to([128, SLOTS, NE]),
                                     ef[:, 1, :].unsqueeze(1).broadcast_to([128, SLOTS, NE]), ALU.is_ge))
                done(v.tensor_tensor(ef[:, 2, :], ef[:, 1, :], ef[:, 0, :], ALU.subtract))
                v.wait_ge(place_step, n)
                done(v.tensor_reduce(slotf[:, :], slots[:, :, :], AX.X, ALU.add))
                done(v.scalar_tensor_tensor(rt[:, 0, :, :], ef[:, 2, :].unsqueeze(2).broadcast_to([128, NE, TILES]), 128.0,
                                            rt[:, 3, :, :], ALU.mult, ALU.add))
                v.wait_ge(place_step, n)
                done(v.tensor_scalar(slot_e[:, :], slotf[:, :], float(NE - 1), None, ALU.min))
                done(v.scalar_tensor_tensor(rt[:, 1, :, :], rt[:, 0, :, :], -1.0, oh[:, :, :], ALU.add, ALU.mult))
                v.wait_ge(place_step, n)
                done(v.tensor_reduce(gate[:, 2, :], rt[:, 1, :, :].rearrange("p e t -> p t e"), AX.X, ALU.add))
                v.wait_ge(place_step, n)
                done(v.tensor_copy(dest[:, :], gate[:, 2, :]))
                assert n == PLACE_STEPS[m + 1], n

                def shared_step(k, turn, u, live):
                    if live(0):
                        for j in range(2):
                            v.wait_ge(sh_act, 2 * k + j + 1)
                            v.wait_ge(sh_up, 2 * k + j + 1)
                            wait_reuse(v, sh_out, k - 1)
                            v.tensor_tensor(sh_h[u][j][:, :], sc2[j][:, :], psP[j][:, :], ALU.mult).then_inc(sh_hid, 1)
                    if live(1):
                        v.wait_ge(sh_out, k)
                        xc = X[:, bass.ds((k - 1) * TPC, TPC), :].rearrange("p t d -> p (t d)")
                        v.tensor_tensor(xc, psO[(u + 1) % 2][:, :], xc, ALU.add).then_inc(sh_added, 1)

                if m == 0:
                    pipeline(v, CHUNKS, 2, 1, shared_step)

                def expert_step(k, turn, u, live):
                    s = u % 2
                    if u % 4 == 3 and live(0):
                        v.wait_ge(e_turned, before + k + 1)
                        wait_reuse(v, rows_out[u // 4], 64 * (tiles // 8) * m + 64 * turn)
                        v.tensor_tensor(to_row[u // 4][:, :], by_row(xl[u // 4])[:, :, D], spare_row[:, bass.ds(k - 3, TPC)],
                                        ALU.max).then_inc(row_nos, 1)
                    if live(0):
                        v.wait_ge(e_turned, before + k + 1)
                        wait_reuse(v, e_hidden, before + k - 1)
                        v.tensor_copy(xT[s], (psT, psY)[s][:, 0:128]).then_inc(e_xT, 1)
                    if live(1):
                        r = (s + 1) % 2
                        if m == 0:
                            v.wait_ge(e_act, before + k)
                            wait_reuse(v, e_hturned, before + k - 2)
                            v.tensor_tensor(hb[r][:, 0:F], act2[r][:, 0:F], psS[r][:, F:2 * F], ALU.mult).then_inc(e_h, 1)
                    if live(2):
                        v.wait_ge(e_hturned, before + k - 1)
                        wait_reuse(v, e_out, before + k - 3)
                        v.tensor_copy(hT[s][:, 0:F], psP[s][:, 0:F]).then_inc(e_hT, 1)

                pipeline(v, tiles, 8, 2, expert_step)
                if m == 0:
                    v.wait_ge(sh_added, CHUNKS)
                    keys(3)
                for q in range(4):
                    v.wait_ge(rows_back[q], 16 * (m + 1))
                    for k in range(2 * q, 2 * q + 2):
                        xc = X[:, k * TPC:k * TPC + TPC, :].rearrange("p t d -> p (t d)")
                        v.tensor_tensor(xc, QT[:, k * CHUNK:k * CHUNK + CHUNK], xc, ALU.add).then_inc(x_updated, TPC)
                    if m == 0:
                        for t in range(8 * q, 8 * q + 8):
                            tile_stats(6, t)

            attention2()
            mixture(0)
            v.wait_ge(b_loaded, 32)
            split3(dl, dlb, b_split, 0)
            split3(b2l, b2b, b_split, 5)
            norms(6)
            prepare(3, 6, tau_s)
            attention(3)
            mixture(1)

        @block.scalar
        def _(act):
            act.dma_start(W[0][:, :, :], a["W"][0].rearrange("j d e -> d j e")).then_inc(w0_loaded, 16)
            act.dma_start(bqkv[:, :, :].rearrange("p l j -> p (l j)"), a["bqkv"]).then_inc(w0_loaded, 16)
            def rstds(ln):
                act.wait_ge(ln_step, 2 + 9 * ln + 6)
                act.activation(lnw[:, 4, :], lnw[:, 3, :], ACT.Sqrt).then_inc(rsqrt_ready, 1)
                act.wait_ge(norm_ready, 2 * ln + 2)

            def normalise(ln, k, u):
                wait_reuse(act, xt_in_psum, CHUNKS * ln + k - 1)
                tiles = TPC // 2 if ln in SHARED_LN else TPC
                for j in range(tiles):
                    t = k * TPC + j
                    act.activation(xn[u][:, j, :], X[:, bass.ds(t, 1), :].rearrange("p o d -> p (o d)"),
                                   ACT.Identity, bias=nmr[:, bass.ds(t, 1)],
                                   scale=rstd[:, bass.ds(t, 1)]).then_inc(xn_ready, TPC // tiles)

            def double(l, c, src, slot):
                wait_reuse(act, v_proj, 2 * (CHUNKS * l + c - 1))
                act.activation(xd[slot][:, :, :, :], src.rearrange("p (b s) -> p b s", b=BPC).unsqueeze(2)
                               .broadcast_to([128, BPC, 2, S]), ACT.Copy).then_inc(doubled, 1)

            def take_keys(l, c, slot):
                act.wait_ge(k_proj, CHUNKS * l + c + 1)
                act.activation(KT[:, bass.ds(c * CHUNK, CHUNK)], psP[slot][:, :], ACT.Identity,
                               bias=bqkv[:, l, 1:2]).then_inc(k_ready, 1)

            def keys(l):
                def step(k, turn, u, live):
                    if live(0):
                        if l == 0:
                            act.wait_ge(ctx_first if isinstance(k, int) and k < 2 else ctx_loaded,
                                        16 if isinstance(k, int) and k < 2 else 48)
                        double(l, k, ctxT[:, bass.ds(k * CHUNK, CHUNK)], u)
                    if live(1):
                        take_keys(l, k - 1, (u + 1) % 2)

                pipeline(act, CHUNKS, 2, 1, step)

            def prepare(l, ln, cross):
                def step(k, turn, u, live):
                    if live(0):
                        normalise(ln, k, u)
                    if live(1) and not cross:
                        r = (u + 1) % 2
                        act.wait_ge(xt_ready, CHUNKS * ln + k)
                        double(l, k - 1, xts[r][:, :], r)
                        take_keys(l, k - 1, r)

                pipeline(act, CHUNKS, 2, 1, step)

            def attention(l):
                wb = units_before[l]

                def step(k, turn, u, live):
                    s = u % 2
                    if live(0):
                        act.wait_ge(shifted, wb + k + 1)
                        act.activation(Pr[s][:, :], Pr[s][:, :], ACT.Exp).then_inc(exp_ready, 1)
                    if live(1):
                        r = (s + 1) % 2
                        act.wait_ge(p_turned, wb + k)
                        wait_reuse(act, pv_ready, wb + k - 2)
                        act.activation(Pt[r][:, :], psP[r][:, :], ACT.Copy).then_inc(p_evac, 1)
                    if u % 2 == 1 and live(5):
                        m = turn * 2 + u // 2 - 2
                        o = u // 2
                        act.wait_ge(ot_ready, TILES * l + m + 1)
                        wait_reuse(act, y_ready, TILES * l + m - 1)
                        act.activation(ots[o][:, :], psT[:, 0:128], ACT.Copy).then_inc(ot_evac, 1)

                pipeline(act, B, 4, 5, step)

            def classes():
                act.wait_ge(q_ready, 2 * CHUNKS)
                for c in range(CHUNKS):
                    wait_reuse(act, sq_summed, c - 1)
                    act.activation(sq[c % 2][:, :], QT[:, CHUNK * c:CHUNK * c + CHUNK], ACT.Square).then_inc(squared, 1)
                act.wait_ge(sim_act, 1)
                act.activation(n2[1][:, :], n2[0][:, :], ACT.Sqrt).then_inc(sim_act, 1)

            def registers():
                rows = slice(0, H * REG)

                def step(k, turn, u, live):
                    s = u
                    if live(0):
                        act.wait_ge(reg_shifted, k + 1)
                        act.activation(Pr[s][rows, 0:4 * S], Pr[s][rows, 0:4 * S], ACT.Exp).then_inc(reg_exp, 1)
                    if live(2):
                        act.wait_ge(reg_turned, k - 1)
                        wait_reuse(act, reg_pv, k - 3)
                        act.activation(Pt[s][:, 0:4 * H * REG], psP[s][:, 0:4 * H * REG], ACT.Copy).then_inc(reg_evac, 1)
                        act.activation(sc2[s][:, :].rearrange("p (g w) -> p g w", w=2 * E),
                                       VB[:, bass.ds((k - 2) * 4, 4), :].rearrange("p b (g w) -> p (b g) w", w=VW)[:, :, 0:2 * E],
                                       ACT.Copy).then_inc(reg_values, 1)

                pipeline(act, REG_STEPS, 2, 2, step)
                act.wait_ge(reg_pv, REG_STEPS)

            act.wait_ge(w0_loaded, 32)
            keys(0)
            rstds(0)
            prepare(0, 0, True)
            act.wait_ge(gcol_step, 2)
            act.activation(gcols[:, 1, :], gcols[:, 1, :], ACT.Exp, scale=-1.0 / DEV_POW).then_inc(gauss_ready, 1)
            attention(0)
            rstds(1)
            prepare(1, 1, False)
            classes()
            registers()
            attention(1)
            rstds(2)
            keys(2)
            prepare(2, 2, True)
            attention(2)

            def mixture1():
                rstds(3)

                def step(k, turn, u, live):
                    normalise(3, k, u)

                pipeline(act, CHUNKS, 2, 0, step)
                act.wait_ge(route_step, ROUTE_STEPS)
                act.activation(rt[:, 2, :, :], rt[:, 0, :, :], ACT.Exp).then_inc(route_act, 1)
                act.wait_ge(keep_step, 5)
                act.wait_ge(y_kept, 2 * CHUNKS)

                def gated(k, turn, u, live):
                    for t in range(TPC):
                        row = Yt[:, bass.ds((k * TPC + t) * D, D)]
                        act.activation(row, row, ACT.Copy, scale=gate[:, 1, bass.ds(k * TPC + t, 1)]).then_inc(y_gated, 1)

                pipeline(act, CHUNKS, 2, 0, gated)

            def attention2():
                rstds(4)

                def step(k, turn, u, live):
                    s, r = u, (u + 1) % 2
                    if live(4):
                        act.wait_ge(cx_turned, k - 3)
                        wait_reuse(act, c_in_psum, k - 5)
                        act.activation(cxT[s][:, :], psP[1][:, :], ACT.Copy).then_inc(cxT_ready, 1)
                    if live(3):
                        act.wait_ge(at_turned, k - 2)
                        wait_reuse(act, cx_in_psum, k - 4)
                        act.activation(at2[r][:, :], psO[1][:, :], ACT.Copy).then_inc(at_ready, 1)
                    if live(2):
                        act.wait_ge(nmx_ready, k - 1)
                        wait_reuse(act, at_turned, k - 3)
                        wait_reuse(act, rd2_ready, k - 3)
                        for t in range(TPC):
                            act.activation(sc2[s][:, 128 * t:128 * t + 128], psS[0][:, 128 * t:128 * t + 128], ACT.Exp,
                                           bias=nmx[s][:, t:t + 1], accum_out=den[s][:, 0, t:t + 1]).then_inc(e2_ready, 1)
                    if live(0):
                        normalise(4, k, u)
                    if live(4):
                        act.wait_ge(c_in_psum, k - 3)
                        wait_reuse(act, x_updated, TILES * 4 + TPC * (k - 5))
                        act.activation(th[s][:, :], psS[1][:, :], ACT.Tanh).then_inc(th_ready, 1)

                pipeline(act, CHUNKS, 2, 4, step)

            mixture1()
            def mixture(m):
                ln, F, tiles, before = MOE[m]
                rstds(ln)

                def step(k, turn, u, live):
                    wait_reuse(act, xn_kept, CHUNKS * m + k - 1)
                    normalise(ln, k, u)

                pipeline(act, CHUNKS, 2, 0, step)
                if m == 0:
                    act.wait_ge(route_step, ROUTE_STEPS + 1)
                    act.activation(gate[:, 2, :], gate[:, 0, :], ACT.Exp, scale=-1.0).then_inc(score_act, 1)

                    def shared_step(k, turn, u, live):
                        for j in range(2):
                            act.wait_ge(sh_gate, 2 * k + j + 1)
                            wait_reuse(act, sh_hid, 2 * k + j - 1)
                            act.activation(sc2[j][:, :], psS[j][:, :], ACT.Silu).then_inc(sh_act, 1)

                    pipeline(act, CHUNKS, 2, 0, shared_step)

                def expert_step(k, turn, u, live):
                    s = u % 2
                    if live(1):
                        r = (s + 1) % 2
                        act.wait_ge(e_hidden, before + k)
                        if m == 0:
                            wait_reuse(act, e_h, before + k - 2)
                            act.activation(act2[r][:, 0:F], psS[r][:, 0:F], ACT.Silu).then_inc(e_act, 1)
                        else:
                            wait_reuse(act, e_hturned, before + k - 2)
                            act.activation(hb[r][:, 0:F], psS[r][:, 0:F], ACT.Relu).then_inc(e_h, 1)
                    if live(3):
                        act.wait_ge(e_out, before + k - 2)
                        us = (u + 5) % 8
                        if us % 4 == 0:
                            wait_reuse(act, rows_out[us // 4], 64 * (tiles // 8) * m + 64 * (turn - (1 if u < 3 else 0)))
                        act.activation(ys[us // 4][:, 128 * (us % 4):128 * (us % 4) + 128], psO[(s + 1) % 2][:, 0:128],
                                       ACT.Copy).then_inc(e_y, 1)

                if m == 0:
                    act.wait_ge(sh_out, CHUNKS)
                pipeline(act, tiles, 8, 3, expert_step)

            attention2()
            mixture(0)
            keys(3)
            rstds(6)
            prepare(3, 6, True)
            attention(3)
            mixture(1)

        @block.tensor
        def _(pe):
            pe.wait_ge(w0_loaded, 32)

            def normalised(ln, k):
                pe.wait_ge(xn_ready, TPC * (CHUNKS * ln + k + 1))
                if ln in SHARED_LN:
                    pe.wait_ge(xn_half, TPC // 2 * (CHUNKS * SHARED_LN.index(ln) + k + 1))

            def project_kv(l, c, src, slot):
                w = W[l]
                wait_reuse(pe, k_ready, CHUNKS * l + c - 1)
                pe.matmul(psP[slot][:, :], w[:, 1, :], src, start=True, stop=True).then_inc(k_proj, 1)
                pe.wait_ge(doubled, CHUNKS * l + c + 1)
                for h in range(2):
                    wait_reuse(pe, v_ready, 2 * (CHUNKS * l + c) - 1 + h)
                    for j in range(4):
                        mm = pe.matmul(psO[h][:, 128 * j:128 * j + 128],
                                       xd[slot][:, 4 * h + j, :, :].rearrange("p j s -> p (j s)"),
                                       w[:, 2, :], start=True, stop=True)
                    mm.then_inc(v_proj, 1)

            def keys(l):
                def step(k, turn, u, live):
                    pe.wait_ge(doubled, CHUNKS * l + k + 1)
                    project_kv(l, k, ctxT[:, bass.ds(k * CHUNK, CHUNK)], u)

                pipeline(pe, CHUNKS, 2, 0, step)

            def prepare(l, ln, cross):
                w = W[l]

                def step(k, turn, u, live):
                    s = u % 2
                    if live(0):
                        normalised(ln, k)
                        wait_reuse(pe, xt_ready, CHUNKS * ln + k - 1)
                        for j in range(TPC):
                            mm = pe.transpose((psT, psY)[s][:, 128 * j:128 * j + 128], xn[u][:, j, :], ident)
                        mm.then_inc(xt_in_psum, 1)
                    if live(1):
                        c = k - 1
                        r = (s + 1) % 2
                        pe.wait_ge(xt_ready, CHUNKS * ln + k)
                        wait_reuse(pe, q_ready, CHUNKS * l + k - 2)
                        pe.matmul(psS[r][:, :], w[:, 0, :], xts[r][:, :], start=True, stop=True).then_inc(q_proj, 1)
                        if not cross:
                            project_kv(l, c, xts[r][:, :], r)

                pipeline(pe, CHUNKS, 2, 1, step)

            def attention(l, add):
                wb = units_before[l]
                masked = l == 1
                w = W[l]
                pe.wait_ge(v_ready, 2 * CHUNKS * (l + 1))

                def step(k, turn, u, live):
                    s = u % 2
                    if live(0):
                        pe.wait_ge(staged, 2 * (wb + k + 1))
                        if masked:
                            pe.wait_ge(class_staged, k + 1)
                        wait_reuse(pe, shifted, wb + k - 1)
                        pe.matmul(psS[s][:, :], qbd[s][:, :], kbd[s][:, :], start=True, stop=False)
                        rows, left = (2, addL[s]) if masked else (3, onesr)
                        row = add[0:rows, bass.ds(k * S, S)]
                        pe.matmul(psS[s][:, :].rearrange("p (g k) -> p g k", g=G), left[:, :],
                                  row.unsqueeze(1).broadcast_to([rows, G, S]),
                                  start=False, stop=True).then_inc(scores_ready, 1)
                    if live(1):
                        r = (s + 1) % 2
                        pe.wait_ge(exp_ready, wb + k)
                        wait_reuse(pe, p_evac, wb + k - 2)
                        for g in range(4):
                            mm = pe.transpose(psP[r][:, 128 * g:128 * g + 128], Pr[r][:, 128 * g:128 * g + 128], ident)
                        mm.then_inc(p_turned, 1)
                    if live(2):
                        r = s
                        pe.wait_ge(p_evac, wb + k - 1)
                        us = (u + 2) % 4
                        batch = turn * 4 + u - 2
                        vb = VB[:, bass.ds(batch, 1), :].rearrange("p o c -> p (o c)")
                        if us % 2 == 0:
                            wait_reuse(pe, on_ready, wb + k - 4)
                        o = psO[us // 2]
                        c0 = (us % 2) * G * VW
                        for g in range(4):
                            mm = pe.matmul(o[:, c0 + 2 * VW * g:c0 + 2 * VW * (g + 1)],
                                           Pt[r][:, 128 * g:128 * g + 128],
                                           vb[:, 2 * VW * g:2 * VW * (g + 1)], start=True, stop=True)
                        mm.then_inc(pv_ready, 1)
                    if u % 2 == 1 and live(5):
                        m = turn * 2 + u // 2 - 2
                        pe.wait_ge(on_ready, wb + k - 3)
                        wait_reuse(pe, ot_evac, TILES * l + m)
                        for b in range(2):
                            mm = pe.matmul(psT[:, 64 * b:64 * b + 64], on[u // 2][:, b, :], fold_self if masked else fold2,
                                           start=(b == 0 or not masked), stop=not masked)
                        if masked:
                            mm = pe.matmul(psT[:, 0:128].rearrange("p (b s) -> p b s", b=2)[:, :, 0:REG], ident,
                                           reg_out[:, bass.ds(2 * m, 2), :], start=False, stop=True)
                        mm.then_inc(ot_ready, 1)
                    if u % 2 == 0 and live(6):
                        m = turn * 2 + u // 2 - 3
                        o = (u // 2 + 1) % 2
                        pe.wait_ge(ot_evac, TILES * l + m + 1)
                        wait_reuse(pe, x_updated, TILES * UPD_OF[l] + m)
                        pe.matmul(psY[:, 0:128], ots[o][:, :], w[:, 3, :],
                                  start=True, stop=True).then_inc(y_ready, 1)

                pipeline(pe, B, 4, 5, step)

            def turn_x(ln, k, u):
                normalised(ln, k)
                wait_reuse(pe, xt_ready, CHUNKS * ln + k - 1)
                for j in range(TPC):
                    mm = pe.transpose((psT, psY)[u][:, 128 * j:128 * j + 128], xn[u][:, j, :], ident)
                mm.then_inc(xt_in_psum, 1)

            def ranks(r):
                pe.wait_ge(route_step, ROUTE_STEPS * r + 5)
                cols = oh[:, :, :].rearrange("p e t -> p (e t)")
                pe.matmul(psO[0][:, 0:256], ones128[:, :], cols, start=True, stop=True).then_inc(rank_ready, 1)
                pe.matmul(psO[1][:, 0:256], upto, cols, start=True, stop=True).then_inc(rank_ready, 1)

            def mixture1():
                pe.wait_ge(w1f_loaded, 48)

                def step(k, turn, u, live):
                    if live(0):
                        turn_x(3, k, u)
                    if live(1):
                        r = (u + 1) % 2
                        pe.wait_ge(xt_ready, CHUNKS * 3 + k)
                        wait_reuse(pe, y_kept, 2 * (k - 2))
                        for j in range(TPC):
                            mm = pe.matmul((psS[r], psO[r])[j // 2][:, (NE + D) * (j % 2):(NE + D) * (j % 2 + 1)],
                                           xts[r][:, 128 * j:128 * j + 128], w1f[:, :], start=True, stop=True)
                        mm.then_inc(route_pe, 1)

                pipeline(pe, CHUNKS, 2, 1, step)
                ranks(0)

            def attention2():
                pe.wait_ge(l2_loaded, 80)
                pe.wait_ge(win_rows, 32)
                pe.wait_ge(half_ready, 1)
                pe.wait_ge(gauss_ready, 2)

                def step(k, turn, u, live):
                    s, r = u, (u + 1) % 2
                    if live(3):
                        pe.wait_ge(cx_ready, k - 2)
                        wait_reuse(pe, cxT_ready, k - 3)
                        for j in range(TPC):
                            mm = pe.transpose(psP[1][:, 128 * j:128 * j + 128], cx[r][:, 128 * j:128 * j + 128], ident)
                        mm.then_inc(cx_turned, 1)
                    if live(2):
                        pe.wait_ge(e2_ready, TPC * (k - 1))
                        wait_reuse(pe, at_ready, k - 2)
                        for j in range(TPC):
                            mm = pe.transpose(psO[1][:, 128 * j:128 * j + 128], sc2[s][:, 128 * j:128 * j + 128], ident)
                        mm.then_inc(at_turned, 1)
                    if live(1):
                        pe.wait_ge(xt_ready, CHUNKS * 4 + k)
                        pe.wait_ge(a_ready, k)
                        wait_reuse(pe, e2_ready, TPC * (k - 1))
                        pe.matmul(psS[0][:, :], half[:, :], maskR[0:2, bass.ds((k - 1) * CHUNK, CHUNK)], start=True, stop=False)
                        for j in range(TPC):
                            mm = pe.matmul(psS[0][:, 128 * j:128 * j + 128], xts[r][:, 128 * j:128 * j + 128],
                                           KT[:, bass.ds((k - 1) * CHUNK + 128 * j, 128)], start=False, stop=(j == TPC - 1))
                        mm.then_inc(s2_ready, 1)
                    if live(0):
                        turn_x(4, k, u)
                        wait_reuse(pe, a_ready, k)
                        pe.matmul(psP[0][:, :], wa[:, 0, :], ctxT[:, bass.ds(k * CHUNK, CHUNK)], start=True, stop=True).then_inc(a_in_psum, 1)
                    if live(3):
                        pe.wait_ge(x2_copied, k - 2)
                        pe.wait_ge(cxT_ready, k - 2)
                        wait_reuse(pe, th_ready, k - 3)
                        for j in range(TPC):
                            cols = slice(128 * j, 128 * j + 128)
                            pe.matmul(psS[1][:, cols], xt2[r][:, cols], wa[:, 2, :], start=True, stop=False)
                            mm = pe.matmul(psS[1][:, cols], cxT[r][:, cols], wa[:, 1, :], start=False, stop=True)
                        mm.then_inc(c_in_psum, 1)
                    if live(2):
                        pe.wait_ge(at_ready, k - 1)
                        wait_reuse(pe, cx_ready, k - 2)
                        for j in range(TPC):
                            mm = pe.matmul(psO[0][:, 128 * j:128 * j + 128], at2[s][:, 128 * j:128 * j + 128],
                                           QT[:, bass.ds((k - 2) * CHUNK + 128 * j, 128)], start=True, stop=True)
                        mm.then_inc(cx_in_psum, 1)

                pipeline(pe, CHUNKS, 2, 3, step)

            def mixture(m):
                ln, F, tiles, before = MOE[m]
                pe.wait_ge(mw_loaded, 48)

                def step(k, turn, u, live):
                    if live(0):
                        turn_x(ln, k, u)
                    if live(1):
                        r = (u + 1) % 2
                        pe.wait_ge(xt_ready, CHUNKS * ln + k)
                        wait_reuse(pe, logit_ready, CHUNKS * m + k - 2)
                        for j in range(TPC):
                            mm = pe.matmul(psO[r][:, NE * j:NE * j + NE], xts[r][:, 128 * j:128 * j + 128], rw[:, m, :],
                                           start=True, stop=True)
                        mm.then_inc(route_pe, 1)

                pipeline(pe, CHUNKS, 2, 1, step)
                ranks(m + 1)
                pe.wait_ge(experts_loaded, 16 * (6 if m == 0 else 10))

                def shared_step(k, turn, u, live):
                    if live(0):
                        for j in range(2):
                            for half, ps, made, free, n in ((0, psS, sh_gate, sh_act, 2 * k + j - 1), (1, psP, sh_up, sh_hid, 2 * k + j - 1)):
                                wait_reuse(pe, free, n)
                                at = NE * 512 + 256 * half + 128 * j
                                pe.matmul(ps[j][:, :], wv[:, at:at + 128], KT[:, bass.ds(k * CHUNK, CHUNK)],
                                          start=True, stop=True).then_inc(made, 1)
                    if live(1):
                        r = (u + 1) % 2
                        pe.wait_ge(sh_hid, 2 * k)
                        wait_reuse(pe, sh_added, k - 2)
                        for t in range(TPC):
                            for j in range(2):
                                at = (NE + 1) * 512 + NE * 256 + 128 * j
                                mm = pe.matmul(psO[r][:, 128 * t:128 * t + 128], sh_h[r][j][:, 128 * t:128 * t + 128],
                                               wv[:, at:at + 128], start=(j == 0), stop=(j == 1))
                        mm.then_inc(sh_out, 1)

                if m == 0:
                    pe.wait_ge(xT_kept, CHUNKS)
                    pe.wait_ge(route_step, ROUTE_STEPS * 2)
                    pipeline(pe, CHUNKS, 2, 1, shared_step)
                    pe.wait_ge(sh_added, CHUNKS)
                pe.wait_ge(place_step, PLACE_STEPS[m + 1])
                if m == 1:
                    pe.wait_ge(b_rows, 96)
                w_out_at = (NE + 1) * 512 if m == 0 else NE * 512

                experts = [pe.alloc_register(f"expert{m}{i}") for i in range(4)]
                expert_in = lambda i: pe.snap(experts[i], min_val=0, max_val=NE - 1)

                def expert_step(k, turn, u, live):
                    s = u % 2
                    if live(0):
                        if u % 4 == 0:
                            pe.wait_ge(tiles_loaded[u // 4], 16 * (tiles // 8) * m + 16 * (turn + 1))
                        wait_reuse(pe, e_xT, before + k - 1)
                        pe.transpose((psT, psY)[s][:, 0:128], by_row(xl[u // 4])[:, u % 4, 0:D], ident).then_inc(e_turned, 1)
                    if live(1):
                        r = (s + 1) % 2
                        pe.reg_load(experts[(u + 3) % 4], slot_e[0:1, bass.ds(k - 1, 1)])
                        e_in = expert_in((u + 3) % 4)
                        pe.wait_ge(e_xT, before + k)
                        wait_reuse(pe, e_h, before + k - 2)
                        mm = pe.matmul(psS[r][:, :], xT[r], wv[:, bass.ds(e_in * 512, 512)], start=True, stop=(m == 0))
                        if m == 1:
                            mm = pe.matmul(psS[r][:, :], onesr[:, :], b1r[:, bass.ds(e_in * 512, 512)], start=False, stop=True)
                        mm.then_inc(e_hidden, 1)
                    if live(3):
                        e_back = expert_in((u + 1) % 4)
                    if live(2):
                        pe.wait_ge(e_h, before + k - 1)
                        wait_reuse(pe, e_hT, before + k - 3)
                        for j in range(F // 128):
                            mm = pe.transpose(psP[s][:, 128 * j:128 * j + 128], hb[s][:, 128 * j:128 * j + 128], ident)
                        mm.then_inc(e_hturned, 1)
                    if live(3):
                        r = (s + 1) % 2
                        pe.wait_ge(e_hT, before + k - 2)
                        wait_reuse(pe, e_y, before + k - 4)
                        for j in range(F // 128):
                            mm = pe.matmul(psO[r][:, 0:128], hT[r][:, 128 * j:128 * j + 128],
                                           wv[:, bass.ds(e_back * F + (w_out_at + 128 * j), 128)], start=(j == 0),
                                           stop=(m == 0 and j == F // 128 - 1))
                        if m == 1:
                            mm = pe.matmul(psO[r][:, 0:128], onesr[:, :], b2r[:, bass.ds(e_back * D, D)], start=False, stop=True)
                        mm.then_inc(e_out, 1)

                pipeline(pe, tiles, 8, 3, expert_step)

            def classes():
                pe.wait_ge(sim_step, 2)
                pe.wait_ge(k_ready, 2 * CHUNKS)
                pe.matmul(psY[:, 0:1], heads_rep, gcol[:, 1:2], start=True, stop=True).then_inc(sim_pe, 1)
                pe.wait_ge(q_ready, 2 * CHUNKS)
                for c in range(CHUNKS):
                    mm = pe.matmul(psS[1][:, :], guide_pad[:, 112 - H * c:240 - H * c], QT[:, CHUNK * c:CHUNK * c + CHUNK],
                                   start=(c == 0), stop=(c == CHUNKS - 1))
                mm.then_inc(sim_pe, 1)
                for c in range(CHUNKS):
                    pe.wait_ge(squared, c + 1)
                    mm = pe.matmul(psS[0][:, :], heads_pad[:, 112 - H * c:240 - H * c], sq[c % 2][:, :],
                                   start=(c == 0), stop=(c == CHUNKS - 1)).then_inc(sq_summed, 1)
                pe.wait_ge(sq_summed, CHUNKS)
                pe.sem_inc(sim_pe, 1)
                pe.wait_ge(sim_step, 4)
                pe.matmul(psP[0][0:CHUNKS, :], mean_h, n2[4][:, :], start=True, stop=True).then_inc(sim_pe, 1)
                pe.wait_ge(cls_rows, 48)
                pe.wait_ge(sim_step, 8)

            def registers():
                rows, cols = slice(0, H * REG), H * REG
                pe.wait_ge(v_ready, 2 * CHUNKS * 2)

                def step(k, turn, u, live):
                    s, r = u, (u + 1) % 2
                    if live(0):
                        pe.wait_ge(reg_staged, k + 1)
                        wait_reuse(pe, reg_shifted, k - 1)
                        pe.matmul(psS[s][rows, 0:4 * S], neg_class[:, :], maskR[0:2, bass.ds(k * 4 * S, 4 * S)],
                                  start=True, stop=False)
                        for b in range(4):
                            mm = pe.matmul(psS[s][rows, S * b:S * b + S], kbd[s][:, cols * b:cols * b + cols],
                                           KT[:, bass.ds(k * 4 * S + S * b, S)], start=False, stop=(b == 3))
                        mm.then_inc(reg_scores, 1)
                    if live(2):
                        pe.wait_ge(reg_probs, k - 1)
                        wait_reuse(pe, reg_evac, k - 3)
                        for b in range(4):
                            mm = pe.transpose(psP[s][:, cols * b:cols * b + cols], th[s][rows, 128 * b:128 * b + 128],
                                              ident[rows, 0:cols])
                        mm.then_inc(reg_turned, 1)
                    if live(3):
                        pe.wait_ge(reg_evac, k - 2)
                        pe.wait_ge(reg_values, k - 2)
                        wait_reuse(pe, reg_masked, k - 4)
                        for b in range(4):
                            mm = pe.matmul(psO[r][:, cols * b:cols * b + cols], sc2[r][:, 128 * b:128 * b + 128],
                                           Pt[r][:, cols * b:cols * b + cols], start=True, stop=True)
                        mm.then_inc(reg_pv, 1)

                pipeline(pe, REG_STEPS, 2, 3, step)
                pe.wait_ge(reg_kept, REG_STEPS)

            keys(0)
            pe.wait_ge(w_loaded, W_DMAS * 16)
            for l in range(4):
                mm = pe.matmul(psY[:, D * l:D * l + D], bqkv[:, l, 2:3].broadcast_to([128, 128]), W[l][:, 3, :],
                               start=True, stop=True)
            mm.then_inc(bias_through, 1)
            pe.wait_ge(cst_loaded, CST_DMAS * 16)
            pe.wait_ge(consts_ready, CONSTS)
            pe.wait_ge(bo_ready, 1)
            prepare(0, 0, True)
            pe.wait_ge(rows_moved, 48)
            attention(0, addR)
            prepare(1, 1, False)
            classes()
            registers()
            attention(1, maskR)
            keys(2)
            prepare(2, 2, True)
            attention(2, addR)
            mixture1()
            attention2()
            mixture(0)
            pe.wait_ge(e_y, SLOTS)
            pe.wait_ge(e_hT, SLOTS)
            keys(3)
            prepare(3, 6, True)
            pe.wait_ge(ones_again, 1)
            attention(3, addR)
            mixture(1)


LAYERS = ("L0_xcond", "L1_xcond", "L3_xcond")


def kernel(**inputs):
    import concourse.bacc as bacc
    from concourse.bass_utils import run_bass_kernel_spmd

    i = {k: np.asarray(v) for k, v in inputs.items()}
    arrays = {"x": i["x"], "ctxT": np.ascontiguousarray(i["ctx_1024"].reshape(TOK, D).T),
              "condB_tau": i["condB_tau"], "fside_BxS2_0": i["fside_BxS2_0"]}
    weights = [np.stack([i[f"{n}_W{c}"].T for c in "qkvo"]) for n in LAYERS]
    biases = [np.stack([i[f"{n}_b{c}"] for c in "qkvo"]) for n in LAYERS]
    qkv = i["L0_ffn_W_qkv"]
    weights.insert(1, np.stack([qkv[:, 0:D], qkv[:, D:2 * D], qkv[:, 2 * D:3 * D], i["L0_ffn_W_proj"]]))
    zero = np.zeros(D, np.float32)
    biases.insert(1, np.stack([zero, zero, zero, i["L0_ffn_b_proj"]]))
    arrays["W"] = np.stack(weights)
    arrays["bqkv"] = np.ascontiguousarray(np.stack(biases).reshape(16, D).T)
    arrays["bo"] = np.stack(biases)[:, 3].reshape(1, 4 * D)
    arrays["g_first"] = np.ascontiguousarray(i["L0_ffn_g_info"][0, 0].reshape(D, 1))
    arrays["cst"] = constants()

    arrays["ctx_1024"] = i["ctx_1024"]
    arrays["L1_ffn_Wg"], arrays["L1_ffn_We"], arrays["L1_ffn_be"] = i["L1_ffn_Wg"], i["L1_ffn_We"], i["L1_ffn_be"].reshape(1, D)
    wc = i["L2_xcond_W_c"].T
    arrays["L2_W"] = np.stack([np.ascontiguousarray(i["L2_xcond_W_a"].T), wc[0:D], wc[D:2 * D]])
    arrays["pt2"] = np.ascontiguousarray(i["condB_pt"].reshape(TILES, 2).T)
    arrays["condB_pt"] = np.ascontiguousarray(i["condB_pt"].reshape(TILES, 2).T).reshape(B, 1)
    arrays["lenS2"] = np.ascontiguousarray(i["_lenS2"].reshape(TILES, 2).T).reshape(B, 1)
    for n in ("gate_w", "sh_gate", "sh_up", "sh_down", "rt_gate", "rt_up", "rt_down"):
        arrays["L2_ffn_" + n] = i["L2_ffn_" + n]
    arrays["L3_ffn_WrT"] = np.ascontiguousarray(i["L3_ffn_Wr"].T)
    arrays["L3_ffn_br"] = i["L3_ffn_br"].reshape(1, NE)
    arrays["L3_ffn_W1T"] = np.ascontiguousarray(i["L3_ffn_W1"].transpose(0, 2, 1))
    arrays["L3_ffn_W2T"] = np.ascontiguousarray(i["L3_ffn_W2"].transpose(0, 2, 1))
    arrays["L3_ffn_b1"] = i["L3_ffn_b1"].reshape(64, 64)
    arrays["L3_ffn_b2"] = i["L3_ffn_b2"].reshape(64, 16)

    nc = bacc.Bacc("TRN2", target_bir_lowering=False, num_devices=1)
    handles = {k: nc.dram_tensor(k + "_in", v.shape, mybir.dt.from_np(v.dtype), kind="ExternalInput").ap()
               for k, v in arrays.items()}
    out = nc.dram_tensor("out", (B, S, D), F32, kind="ExternalOutput").ap()
    build(nc, handles, out)
    r = run_bass_kernel_spmd(nc, [{k + "_in": np.ascontiguousarray(v) for k, v in arrays.items()}], core_ids=[0])
    return r.results[0]["out"]
```
